# Optimizing a Trainium2 kernel written in Bass

```python
import numpy as np
import jax
import jax.numpy as jnp

def _softmax(x, axis=-1):
    return jax.nn.softmax(x, axis=axis)

def _gelu(x):
    return jax.nn.gelu(x, approximate=True)

def _silu(x):
    return jax.nn.silu(x)

def _sigmoid(x):
    return jax.nn.sigmoid(x)

def _layernorm(x, axis=-1, eps=1e-05):
    m = jnp.mean(x, axis=axis, keepdims=True)
    v = jnp.var(x, axis=axis, keepdims=True)
    return (x - m) / jnp.sqrt(v + eps)

def _scatter_add(tgt, idx, src, axis=0):
    return tgt.at[idx].add(src)

def _segment_sum(src, seg, n):
    return jax.ops.segment_sum(src, seg, n)
kernel_name = 'mk_decoder_preln_d1_seqx_r4_419adb'

def setup_inputs(seed: int=0):
    np.random.seed(seed)
    _w = jnp.asarray

    def _rec_inputs():
        import jax
        import jax.numpy as jnp
        _rk = jax.random.key(seed)
        x = -0.0002928 + 1 * jax.random.normal(jax.random.fold_in(_rk, 1), (1, 2048, 256), jnp.float32)
        _lenS = 2048 - jax.random.randint(jax.random.fold_in(_rk, 7), (1,), 0, max(1, 2048 // 4) + 1, jnp.int32)
        _lenS2 = 1601 - jax.random.randint(jax.random.fold_in(_rk, 8), (1,), 0, max(1, 1601 // 4) + 1, jnp.int32)
        _ctx_1024P = jax.random.normal(jax.random.fold_in(_rk, 11), (1, 16, 256), jnp.float32)
        _ctx_1024c = jax.random.dirichlet(jax.random.fold_in(_rk, 511), 0.3 * jnp.ones((16,), jnp.float32), (1, 1601))
        _ctx_1024t = jnp.einsum('bsk,bkd->bsd', _ctx_1024c, _ctx_1024P)
        _ctx_1024t = _ctx_1024t * jax.lax.rsqrt(jnp.mean(jnp.square(_ctx_1024t)) + 1e-12) * 0.953939
        ctx_1024 = -1.39393e-06 + 0.999914 * (_ctx_1024t + 0.3 * jax.random.normal(jax.random.fold_in(_rk, 611), (1, 1601, 256), jnp.float32))
        return (x, ctx_1024)
    x, ctx_1024 = _rec_inputs()

    def _L0_attn_setup():
        import jax, jax.numpy as jnp
        import numpy as np
        import math
        D = 256
        key = jax.random.key(seed)
        ks = jax.random.split(key, 5)
        B, S = (4, 512)
        scale = 1.0 / math.sqrt(D)
        x = jax.random.normal(ks[0], (B, S, D), dtype=jnp.float32)
        W_qkv = jax.random.normal(ks[1], (D, 3 * D), dtype=jnp.float32) * scale
        b_qkv = jax.random.normal(ks[2], (3 * D,), dtype=jnp.float32) * 0.01
        W_out = jax.random.normal(ks[3], (D, D), dtype=jnp.float32) * scale
        b_out = jax.random.normal(ks[4], (D,), dtype=jnp.float32) * 0.01
        return {'x': x, 'W_qkv': W_qkv, 'b_qkv': b_qkv, 'W_out': W_out, 'b_out': b_out}
    _L0_attn_all = _L0_attn_setup()
    _L0_attn_in = {k: v for k, v in _L0_attn_all.items() if k in ('W_qkv', 'b_qkv', 'W_out', 'b_out')}
    del _L0_attn_all

    def _L0_xattn_setup():
        import jax, jax.numpy as jnp
        import numpy as np
        import math
        NUM_HEADS = 16
        key = jax.random.key(seed)
        ks = jax.random.split(key, 7)
        B, S, D = (2, 512, 256)
        scale = 1.0 / math.sqrt(D)
        return {'query': jax.random.normal(ks[0], (B, S, D), jnp.float32), 'key': jax.random.normal(ks[1], (B, S, D), jnp.float32), 'value': jax.random.normal(ks[2], (B, S, D), jnp.float32), 'Wq': jax.random.normal(ks[3], (D, D), jnp.float32) * scale, 'Wk': jax.random.normal(ks[4], (D, D), jnp.float32) * scale, 'Wv': jax.random.normal(ks[5], (D, D), jnp.float32) * scale, 'Wo': jax.random.normal(ks[6], (D, D), jnp.float32) * scale}
    _L0_xattn_all = _L0_xattn_setup()
    _L0_xattn_in = {k: v for k, v in _L0_xattn_all.items() if k in ('Wq', 'Wk', 'Wv', 'Wo')}
    del _L0_xattn_all

    def _L0_ffn_setup():
        import jax, jax.numpy as jnp
        import numpy as np
        H, F, E_SHARED, E_ROUTED, K = (256, 1024, 1, 8, 2)

        def _expert(x, w_up, w_down):
            h = jax.nn.gelu(jnp.einsum('bsh,hf->bsf', x, w_up), approximate=False)
            return jnp.einsum('bsf,fh->bsh', h, w_down)
        key = jax.random.key(seed)
        ks = jax.random.split(key, 6)
        x = jax.random.normal(ks[0], (4, 512, H), dtype=jnp.float32)
        s = 0.02
        shared_up = jax.random.normal(ks[1], (E_SHARED, H, F), dtype=jnp.float32) * s
        shared_down = jax.random.normal(ks[2], (E_SHARED, F, H), dtype=jnp.float32) * s
        routed_up = jax.random.normal(ks[3], (E_ROUTED, H, F), dtype=jnp.float32) * s
        routed_down = jax.random.normal(ks[4], (E_ROUTED, F, H), dtype=jnp.float32) * s
        router_w = jax.random.normal(ks[5], (H, E_ROUTED), dtype=jnp.float32) * s
        return {'x': x, 'shared_up': shared_up, 'shared_down': shared_down, 'routed_up': routed_up, 'routed_down': routed_down, 'router_w': router_w}
    _L0_ffn_all = _L0_ffn_setup()
    _L0_ffn_in = {k: v for k, v in _L0_ffn_all.items() if k in ('shared_up', 'shared_down', 'routed_up', 'routed_down', 'router_w')}
    del _L0_ffn_all
    return {'x': x, 'ctx_1024': ctx_1024, 'L0_attn_W_qkv': _L0_attn_in['W_qkv'], 'L0_attn_b_qkv': _L0_attn_in['b_qkv'], 'L0_attn_W_out': _L0_attn_in['W_out'], 'L0_attn_b_out': _L0_attn_in['b_out'], 'L0_xattn_Wq': _L0_xattn_in['Wq'], 'L0_xattn_Wk': _L0_xattn_in['Wk'], 'L0_xattn_Wv': _L0_xattn_in['Wv'], 'L0_xattn_Wo': _L0_xattn_in['Wo'], 'L0_ffn_shared_up': _L0_ffn_in['shared_up'], 'L0_ffn_shared_down': _L0_ffn_in['shared_down'], 'L0_ffn_routed_up': _L0_ffn_in['routed_up'], 'L0_ffn_routed_down': _L0_ffn_in['routed_down'], 'L0_ffn_router_w': _L0_ffn_in['router_w']}

def reference(x, ctx_1024, L0_attn_W_qkv, L0_attn_b_qkv, L0_attn_W_out, L0_attn_b_out, L0_xattn_Wq, L0_xattn_Wk, L0_xattn_Wv, L0_xattn_Wo, L0_ffn_shared_up, L0_ffn_shared_down, L0_ffn_routed_up, L0_ffn_routed_down, L0_ffn_router_w):
    import jax
    import jax.numpy as jnp

    def _L0_attn_ref(x, W_qkv, b_qkv, W_out, b_out):
        import jax, jax.numpy as jnp
        import numpy as np
        import math
        D = 256
        qkv = x @ W_qkv + b_qkv
        q, k, v = jnp.split(qkv, 3, axis=-1)
        inv_sqrt_d = 1.0 / math.sqrt(D)
        scores = jnp.einsum('bqd,bkd->bqk', q, k) * inv_sqrt_d
        attn = jax.nn.softmax(scores, axis=-1)
        ctx = jnp.einsum('bqk,bkd->bqd', attn, v)
        return ctx @ W_out + b_out

    def _L0_xattn_ref(query, key, value, Wq, Wk, Wv, Wo):
        import jax, jax.numpy as jnp
        import numpy as np
        import math
        NUM_HEADS = 16
        B, Sq, D = query.shape
        Sk = key.shape[1]
        H = NUM_HEADS
        dk = D // H
        q = (query @ Wq.T).reshape(B, Sq, H, dk).transpose(0, 2, 1, 3)
        k = (key @ Wk.T).reshape(B, Sk, H, dk).transpose(0, 2, 1, 3)
        v = (value @ Wv.T).reshape(B, Sk, H, dk).transpose(0, 2, 1, 3)
        scores = jnp.einsum('bhqd,bhkd->bhqk', q, k) / jnp.sqrt(jnp.float32(dk))
        causal = jnp.tril(jnp.ones((Sq, Sk), dtype=bool))
        scores = jnp.where(causal[None, None], scores, jnp.float32(-1000000000.0))
        p = jax.nn.softmax(scores, axis=-1)
        x = jnp.einsum('bhqk,bhkd->bhqd', p, v)
        x = x.transpose(0, 2, 1, 3).reshape(B, Sq, D)
        return x @ Wo.T

    def _L0_ffn_ref(x, shared_up, shared_down, routed_up, routed_down, router_w):
        import jax, jax.numpy as jnp
        import numpy as np
        H, F, E_SHARED, E_ROUTED, K = (256, 1024, 1, 8, 2)

        def _expert(x, w_up, w_down):
            h = jax.nn.gelu(jnp.einsum('bsh,hf->bsf', x, w_up), approximate=False)
            return jnp.einsum('bsf,fh->bsh', h, w_down)
        shared_out = jnp.zeros_like(x)
        for i in range(E_SHARED):
            shared_out = shared_out + _expert(x, shared_up[i], shared_down[i])
        probs = jax.nn.softmax(jnp.einsum('bsh,he->bse', x, router_w), axis=-1)
        top_k_prob, top_k_idx = jax.lax.top_k(probs, K)
        onehot = jax.nn.one_hot(top_k_idx, E_ROUTED, dtype=x.dtype)
        gates = jnp.einsum('bsk,bske->bse', top_k_prob, onehot)
        routed_out = jnp.zeros_like(x)
        for e in range(E_ROUTED):
            y = _expert(x, routed_up[e], routed_down[e])
            routed_out = routed_out + gates[..., e:e + 1] * y
        return shared_out + routed_out + x
    x = x + _L0_attn_ref(_layernorm(x, axis=-1), L0_attn_W_qkv, L0_attn_b_qkv, L0_attn_W_out, L0_attn_b_out)
    x = x + _L0_xattn_ref(_layernorm(x, axis=-1), ctx_1024, ctx_1024, L0_xattn_Wq, L0_xattn_Wk, L0_xattn_Wv, L0_xattn_Wo)
    x = x + _L0_ffn_ref(_layernorm(x, axis=-1), L0_ffn_shared_up, L0_ffn_shared_down, L0_ffn_routed_up, L0_ffn_routed_down, L0_ffn_router_w)
    return x

_drawn_inputs = setup_inputs


def setup_inputs(seed=0):
    import zlib

    import numpy as np

    out = dict(_drawn_inputs(seed))
    spreads = {}
    factors = {'L0_attn_b_qkv': 5.332,
     'L0_attn_b_out': 6.549,
     'L0_ffn_routed_up': 4.559,
     'L0_ffn_routed_down': 4.404,
     'L0_ffn_router_w': 4.992}
    for name, (base, spread) in spreads.items():
        noise = np.random.default_rng([zlib.crc32(name.encode()), seed]).standard_normal(out[name].shape)
        drawn = base * np.exp(spread * noise) if base else spread * noise
        out[name] = jnp.asarray(drawn.astype(out[name].dtype))
    for name, factor in factors.items():
        out[name] = (out[name] * factor).astype(out[name].dtype)
    return out
```

```python
from contextlib import ExitStack

import numpy as np

import concourse.bass as bass
from concourse import mybir

F32 = mybir.dt.float32
BF16 = mybir.dt.bfloat16
U32 = mybir.dt.uint32
ALU = mybir.AluOpType
ACT = mybir.ActivationFunctionType
AX_X = mybir.AxisListType.X
ds = bass.ds

P = 128
D = 256
KC = D // P
T = 2048
NT = T // P
CH = 512
NC = T // CH
TPC = CH // P
S_CTX = 1601
NTC = (S_CTX + P - 1) // P
CTX_LAST = S_CTX - (NTC - 1) * P
HEADS = 16
DK = D // HEADS
GH = 4
NG = HEADS // GH
F = 1024
NF = F // P
E = 8
TOPK = 2
ROUTED = T * TOPK // P + E
NBLK = NT + ROUTED
SLOTS = NBLK * P
WEIGHT_ORDER = [E, *range(E)]
WCOLS = 2 * KC * F + 2 * NF * D
EPS = 1e-5
NEG = -1.0e30
LOWEST = -3.0e38
PASSES = ((0, 0), (0, 1), (1, 0))
Q_PARTS = (0, 0, 0, 1, 1, 2)
K_PARTS = (0, 1, 2, 0, 1, 0)
STACK = len(Q_PARTS) * DK
STEPS = [(c, j, max(0, j - TPC * c) * P) for c in range(NC) for j in range(min(TPC * (c + 1), NTC))]
NSTEP = len(STEPS)
DIAG = [s for s, (c, j, _) in enumerate(STEPS) if j >= TPC * c]
LAST_OF = {c: max(s for s, x in enumerate(STEPS) if x[0] == c) for c in range(NC)}
UNITS = []
for _i in range(NT):
    _w = min(P * (_i + 1), S_CTX)
    for _h in range(GH):
        UNITS += [(_i, _h, k, min(CH, _w - k)) for k in range(0, _w, CH)]
NU = len(UNITS)


class Shared:
    pass

def layernorm_dve(v, m, s_dve, n0, s_pow, s_xn, xn):
    for t in range(NT):
        v.bn_stats(m.stats[:, t, :], m.x_res[:, t * D:(t + 1) * D]).then_inc(s_dve, 1)
    for t in range(NT):
        v.wait_ge(s_dve, n0 + t + 1)
        v.bn_aggr(m.mv[:, t, :], m.stats[:, t, :]).then_inc(s_dve, 1)
    v.wait_ge(s_dve, n0 + 2 * NT)
    v.tensor_scalar(m.var_eps[:], m.mv[:, :, 1], EPS, None, ALU.add).then_inc(s_dve, 1)
    v.wait_ge(s_pow, 1)
    for t in range(NT):
        v.tensor_scalar(xn[:, t * D:(t + 1) * D], m.x_res[:, t * D:(t + 1) * D],
                        m.mv[:, t, 0:1], m.rstd[:, t:t + 1], ALU.subtract, ALU.mult).then_inc(s_xn, 1)
    return n0 + 2 * NT + 1


def layernorm_pool(g, m, s_dve, n, s_pow):
    g.wait_ge(s_dve, n)
    g.tensor_tensor(m.rstd[:], m.var_eps[:], m.neg_half[:], ALU.pow).then_inc(s_pow, 1)


def qkv_phase(nc, m, qk, vv):
    with ExitStack() as st:
        xn = m.sb("xn", [P, NT * D], F32, st)
        rows = m.sb("rows", [P, TPC * D], F32, st)
        xnT = m.sb("xnT", [P, KC, CH], F32, st)
        p_t = m.pb("p_t", [P, KC, CH], F32, st)
        p_qk = m.pb("p_qk", [P, 2 * KC, CH], F32, st)
        p_v = m.pb("p_v", [P, TPC, D], F32, st)
        s_dve, s_pow, s_xn = m.sem("ln_dve", st), m.sem("ln_pow", st), m.sem("xn_ready", st)
        s_rows = m.sem("rows_ready", st)
        s_tr, s_xnT = m.sem("transposed", st), m.sem("xnT_ready", st)
        s_mm, s_hi, s_lo = m.sem("projected", st), m.sem("high_ready", st), m.sem("low_ready", st)
        NOUT = 2 * KC + 1
        with nc.Block() as block:
            @block.vector
            def _(v):
                v.sem_inc(s_lo, NOUT)
                layernorm_dve(v, m, s_dve, 0, s_pow, s_xn, xn)
                with v.Fori(0, NC) as c:
                    for k in range(2 * KC):
                        v.wait_ge(s_hi, c * NOUT + k + 1)
                        v.scalar_tensor_tensor(out=qk[1][:, k, ds(c * CH, CH)], in0=p_qk[:, k, :],
                                               scalar=m.b_qk[:, k:k + 1], in1=qk[0][:, k, ds(c * CH, CH)],
                                               op0=ALU.add, op1=ALU.subtract).then_inc(s_lo, 1)
                    v.wait_ge(s_hi, c * NOUT + NOUT)
                    v.tensor_tensor(vv[1][:, ds(c * TPC * D, TPC * D)], p_v[:].rearrange("p a d -> p (a d)"),
                                    vv[0][:, ds(c * TPC * D, TPC * D)], ALU.subtract).then_inc(s_lo, 1)

            @block.gpsimd
            def _(g):
                layernorm_pool(g, m, s_dve, 2 * NT + 1, s_pow)

            @block.scalar
            def _(a):
                with a.Fori(0, NC) as c:
                    a.wait_ge(s_xn, c * TPC + TPC)
                    a.copy(rows[:], xn[:, ds(c * TPC * D, TPC * D)]).then_inc(s_rows, 1)
                    a.wait_ge(s_tr, c + 1)
                    a.copy(xnT[:], p_t[:]).then_inc(s_xnT, 1)
                    for k in range(2 * KC):
                        a.wait_ge(s_mm, c * NOUT + k + 1)
                        a.activation(qk[0][:, k, ds(c * CH, CH)], p_qk[:, k, :], ACT.Identity,
                                     bias=m.b_qk[:, k:k + 1]).then_inc(s_hi, 1)
                    a.wait_ge(s_mm, c * NOUT + NOUT)
                    a.copy(vv[0][:, ds(c * TPC * D, TPC * D)],
                           p_v[:].rearrange("p a d -> p (a d)")).then_inc(s_hi, 1)

            @block.tensor
            def _(pe):
                with pe.Fori(0, NC) as c:
                    pe.wait_ge(s_rows, c + 1)
                    for k in range(KC):
                        for j in range(TPC):
                            last = pe.transpose(p_t[:, k, j * P:(j + 1) * P],
                                                rows[:, j * D + k * P:j * D + (k + 1) * P], m.ident[:])
                    last.then_inc(s_tr, 1)
                    pe.wait_ge(s_xnT, c + 1)
                    for n in range(2 * KC):
                        pe.wait_ge(s_lo, c * NOUT + n + 1)
                        for k in range(KC):
                            last = pe.matmul(p_qk[:, n, :], m.w_qkv[:, k, n * P:(n + 1) * P], xnT[:, k, :],
                                             start=(k == 0), stop=(k == KC - 1))
                        last.then_inc(s_mm, 1)
                    pe.wait_ge(s_lo, c * NOUT + NOUT)
                    for j in range(TPC):
                        pe.matmul(p_v[:, j, :], m.ones_row[:], m.b_rows[:, 0:D], start=True, stop=False)
                        for k in range(KC):
                            last = pe.matmul(p_v[:, j, :], xnT[:, k, j * P:(j + 1) * P], m.w_qkv[:, k, 2 * D:],
                                             start=False, stop=(k == KC - 1))
                    last.then_inc(s_mm, 1)


def self_attention_phase(nc, m, qk, vv):
    with ExitStack() as st:
        p32 = m.sb("p32", [P, T], F32, st)
        pp = [m.sb(f"pp{r}", [P, T], BF16, st) for r in range(2)]
        ppT = m.sb("ppT", [P, NC, 2, TPC * P], BF16, st)
        ctx_n = m.sb("ctx_n", [P, D], F32, st)
        ctxT = m.sb("ctxT", [P, KC, P], F32, st)
        mx4 = m.sb("mx4", [P, NC], F32, st)
        mx1 = m.sb("mx1", [P, 1], F32, st)
        neg_max = m.sb("neg_max", [P, 1], F32, st)
        sums = m.sb("sums", [P, NC], F32, st)
        sum1 = m.sb("sum1", [P, 1], F32, st)
        rsum = m.sb("rsum", [P, 1], F32, st)
        w32 = m.sb("w32", [P, 2, 2 * KC * F // 2], F32, st)
        zeros = m.sb("zeros", [P, KC * F], F32, st)
        whl = m.sb("whl", [P, 2, 2, KC * F], BF16, st)
        p_s = m.pb("p_s", [P, NC, CH], F32, st)
        p_t = m.pb("p_pt", [P, 2, 2 * TPC * P], BF16, st)
        p_o = m.pb("p_o", [P, D], F32, st)
        p_y = m.pb("p_y", [P, 2, D], F32, st)
        s_s, s_max, s_exp = m.sem("scores", st), m.sem("max_ready", st), m.sem("exp_done", st)
        s_split, s_tr, s_pt = m.sem("split", st), m.sem("p_transposed", st), m.sem("pT_ready", st)
        s_pv, s_ctx, s_ct = m.sem("pv_done", st), m.sem("ctx_ready", st), m.sem("ctx_transposed", st)
        s_ctT, s_y, s_add = m.sem("ctxT_ready", st), m.sem("y_ready", st), m.sem("added", st)
        s_v = m.sem("dve_chain", st)
        NV = 10
        s_wl = [m.sem(f"weights_in{r}", st) for r in range(2)]
        s_wh, s_wlo = m.sem("weights_high", st), m.sem("weights_low", st)
        s_ws = [m.sem(f"weights_stored{r}", st) for r in range(2)]
        s_zero, s_zs = m.sem("zeroed", st), m.sem("slots_zeroed", st)
        NW = KC * F
        SCALE = 1.0 / 16.0
        assert SCALE * SCALE * D == 1.0

        with nc.Block() as block:
            @block.tensor
            def _(pe):
                def scores(i):
                    for c in range(NC):
                        pe.wait_ge(s_exp, i * NC + c + 1)
                        n = 0
                        for a, b in PASSES:
                            for k in range(KC):
                                last = pe.matmul(p_s[:, c, :], qk[a][:, k, ds(i * P, P)],
                                                 qk[b][:, KC + k, c * CH:(c + 1) * CH],
                                                 start=(n == 0), stop=(n == 3 * KC - 1))
                                n += 1
                        last.then_inc(s_s, 1)

                def transposes(i, g):
                    pe.wait_ge(s_split, NC + i * NC + g + 1)
                    pe.wait_ge(s_pt, i * NC + g + 1)
                    for r in range(2):
                        for b in range(TPC):
                            last = pe.transpose(p_t[:, g % 2, (r * TPC + b) * P:(r * TPC + b + 1) * P],
                                                pp[r][:, g * CH + b * P:g * CH + (b + 1) * P], m.identb[:])
                    last.then_inc(s_tr, 1)

                def values(i, g):
                    pe.wait_ge(s_pt, 2 + i * NC + g + 1)
                    if g == 0:
                        pe.wait_ge(s_ctx, i + 1)
                    for b in range(TPC):
                        kt = g * TPC + b
                        for n, (a, w) in enumerate(PASSES):
                            last = pe.matmul(p_o[:], ppT[:, g, a, b * P:(b + 1) * P],
                                             vv[w][:, kt * D:(kt + 1) * D],
                                             start=(kt == 0 and n == 0), stop=(kt == NT - 1 and n == 2))
                    last.then_inc(s_pv, 1)

                def weigh(i):
                    transposes(i, 0)
                    for g in range(NC):
                        if g + 1 < NC:
                            transposes(i, g + 1)
                        values(i, g)

                def context_T(i):
                    pe.wait_ge(s_ctx, 1 + i + 1)
                    pe.wait_ge(s_add, i + 1)
                    for k in range(KC):
                        last = pe.transpose(p_y[:, 0, k * P:(k + 1) * P], ctx_n[:, k * P:(k + 1) * P], m.ident[:])
                    last.then_inc(s_ct, 1)

                def project(i):
                    pe.wait_ge(s_ctT, i + 1)
                    pe.matmul(p_y[:, 1, :], m.ones_row[:], m.b_rows[:, D:2 * D], start=True, stop=False)
                    for k in range(KC):
                        last = pe.matmul(p_y[:, 1, :], ctxT[:, k, :], m.w_out[:, k, :],
                                         start=False, stop=(k == KC - 1))
                    last.then_inc(s_y, 1)

                scores(0)
                scores(1)
                weigh(0)
                with pe.Fori(2, NT) as i:
                    scores(i)
                    context_T(i - 2)
                    weigh(i - 1)
                    project(i - 2)
                context_T(NT - 2)
                weigh(NT - 1)
                project(NT - 2)
                context_T(NT - 1)
                project(NT - 1)

            @block.vector
            def _(v):
                v.sem_inc(s_split, NC)
                v.sem_inc(s_ctx, 1)
                v.sem_inc(s_add, 1)

                def maxima(i):
                    for c in range(NC):
                        v.wait_ge(s_s, i * NC + c + 1)
                        v.reduce_max(mx4[:, c:c + 1], p_s[:, c, :], AX_X).then_inc(s_v, 1)
                    v.wait_ge(s_v, i * NV + NC)
                    v.reduce_max(mx1[:], mx4[:], AX_X).then_inc(s_v, 1)
                    v.wait_ge(s_v, i * NV + NC + 1)
                    v.tensor_scalar(neg_max[:], mx1[:], -SCALE, None, ALU.mult).then_inc(s_max, 1)

                def split(i):
                    for g in range(NC):
                        cols = slice(g * CH, (g + 1) * CH)
                        v.wait_ge(s_exp, NC + i * NC + g + 1)
                        v.wait_ge(s_tr, i * NC + g + 1)
                        v.tensor_copy(pp[0][:, cols], p32[:, cols]).then_inc(s_v, 1)
                        v.wait_ge(s_v, i * NV + NC + 2 + g)
                        v.tensor_tensor(pp[1][:, cols], p32[:, cols], pp[0][:, cols], ALU.subtract).then_inc(s_split, 1)

                def normalise(i):
                    v.wait_ge(s_pv, NC + i * NC + NC)
                    v.wait_ge(s_ct, i + 1)
                    v.tensor_scalar(ctx_n[:], p_o[:], rsum[:], None, ALU.mult).then_inc(s_ctx, 1)

                def row_sums(i):
                    v.reduce_sum(sum1[:], sums[:], AX_X).then_inc(s_v, 1)
                    v.wait_ge(s_v, i * NV + NV)
                    v.reciprocal(rsum[:], sum1[:]).then_inc(s_rs, 1)

                def add(i):
                    v.wait_ge(s_y, 1 + i + 1)
                    xs = m.x_res[:, ds(i * D, D)]
                    v.tensor_tensor(xs, p_y[:, 1, :], xs, ALU.add).then_inc(s_add, 1)

                s_rs = m.sem("row_sums", st)
                maxima(0)
                split(0)
                row_sums(0)
                maxima(1)
                split(1)
                v.wait_ge(s_rs, 1)
                normalise(0)
                v.wait_ge(s_ctx, 2)
                row_sums(1)
                with v.Fori(2, NT) as i:
                    maxima(i)
                    split(i)
                    v.wait_ge(s_rs, i)
                    normalise(i - 1)
                    v.wait_ge(s_ctx, i + 1)
                    row_sums(i)
                    add(i - 2)
                v.wait_ge(s_rs, NT)
                normalise(NT - 1)
                add(NT - 2)
                add(NT - 1)

            @block.scalar
            def _(a):
                a.sem_inc(s_exp, NC)
                a.sem_inc(s_pt, 2)

                def exps(i, c):
                    if c == 0:
                        a.wait_ge(s_max, i + 1)
                    a.wait_ge(s_split, i * NC + c + 1)
                    a.activation(p32[:, c * CH:(c + 1) * CH], p_s[:, c, :], ACT.Exp, bias=neg_max[:],
                                 scale=SCALE, accum_out=sums[:, c:c + 1]).then_inc(s_exp, 1)

                def copy_pT(i, g):
                    a.wait_ge(s_tr, NC + i * NC + g + 1)
                    a.wait_ge(s_pv, i * NC + g + 1)
                    a.copy(ppT[:, g].rearrange("p r n -> p (r n)"), p_t[:, g % 2, :]).then_inc(s_pt, 1)

                def copy_ctxT(i):
                    a.wait_ge(s_ct, 1 + i + 1)
                    a.wait_ge(s_y, i + 1)
                    a.copy(ctxT[:].rearrange("p k n -> p (k n)"), p_y[:, 0, :]).then_inc(s_ctT, 1)

                def mixed(i):
                    copy_pT(i - 1, 0)
                    copy_pT(i - 1, 1)
                    exps(i, 0)
                    copy_pT(i - 1, 2)
                    exps(i, 1)
                    copy_pT(i - 1, 3)
                    exps(i, 2)
                    exps(i, 3)

                for c in range(NC):
                    exps(0, c)
                mixed(1)
                with a.Fori(2, NT) as i:
                    copy_ctxT(i - 2)
                    mixed(i)
                copy_ctxT(NT - 2)
                for g in range(NC):
                    copy_pT(NT - 1, g)
                copy_ctxT(NT - 1)

            @block.gpsimd
            def _(g):
                for s, n in ((s_tr, NC), (s_pv, NC), (s_ct, 1), (s_y, 1)):
                    g.sem_inc(s, n)

                g.memset(zeros[:], 0.0).then_inc(s_zero, 1)
                g.wait_ge(s_zero, 1)

                def split_weights(e, r):
                    g.wait_ge(s_wl[r], (e + 1) * 16)
                    g.wait_ge(s_ws[r], (e + 1) * 16)
                    g.tensor_tensor(whl[:, r, 0, :], w32[:, r, :], zeros[:], ALU.add).then_inc(s_wh, 1)
                    g.wait_ge(s_wh, 2 * e + r + 1)
                    g.tensor_tensor(whl[:, r, 1, :], w32[:, r, :], whl[:, r, 0, :], ALU.subtract).then_inc(s_wlo, 1)

                with g.Fori(0, E + 1) as e:
                    split_weights(e, 0)
                    split_weights(e, 1)

            @block.sync
            def _(sp):
                def load(r, src):
                    sp.dma_start(w32[:, r, :].rearrange("p (k n) -> p k n", k=src.shape[0] // P),
                                 src.rearrange("(k p) n -> p k n", p=P)).then_inc(s_wl[r], 16)

                def store(e, r):
                    sp.wait_ge(s_wlo, 2 * e + r + 1)
                    sp.dma_start(m.w_img[ds(e, 1), :, r * 2 * NW:(r + 1) * 2 * NW].rearrange("e p n -> (e p) n"),
                                 whl[:, r].rearrange("p h n -> p (h n)")).then_inc(s_ws[r], 16)

                sp.wait_ge(s_zero, 1)
                ZR = zeros.shape[1] * 2 // (2 * D)
                zv = zeros[:].bitcast(BF16).rearrange("p (a n) -> p a n", n=2 * D)
                for b in range(NT, NBLK, ZR):
                    sp.dma_start(m.x_slots[b * P:(b + ZR) * P, :].rearrange("(a p) n -> p a n", p=P), zv).then_inc(s_zs, 16)
                sp.sem_inc(s_ws[0], 16)
                sp.sem_inc(s_ws[1], 16)
                load(0, m.routed_up[0])
                load(1, m.routed_down[0])
                with sp.Fori(0, E - 1) as e:
                    store(e, 0)
                    load(0, m.routed_up[ds(e + 1, 1)].rearrange("e k n -> (e k) n"))
                    store(e, 1)
                    load(1, m.routed_down[ds(e + 1, 1)].rearrange("e k n -> (e k) n"))
                store(E - 1, 0)
                load(0, m.shared_up[0])
                store(E - 1, 1)
                load(1, m.shared_down[0])
                store(E, 0)
                store(E, 1)
                sp.wait_ge(s_zs, 16 * ((NBLK - NT) // ZR))
                sp.wait_ge(s_ws[0], 16 * (E + 2))
                sp.wait_ge(s_ws[1], 16 * (E + 2))

def cross_projection_phase(nc, m, v2):
    with ExitStack() as st:
        xn = m.sb("xn2", [P, NT * D], F32, st)
        ctx_sb = m.sb("ctx_sb", [P, NT * D], F32, st)
        rows = m.sb("rows2", [P, TPC * D], F32, st)
        rT = m.sb("rT2", [P, KC, CH], F32, st)
        parts = m.sb("parts", [P, 3, KC, CH], BF16, st)
        rest = m.sb("rest", [P, KC, CH], F32, st)
        p_t = m.pb("p_t2", [P, KC, CH], F32, st)
        p_m = m.pb("p_m2", [P, KC, CH], F32, st)
        p_v = m.pb("p_v2", [P, TPC, D], F32, st)
        s_dve, s_pow, s_xn = m.sem("ln2_dve", st), m.sem("ln2_pow", st), m.sem("xn2_ready", st)
        s_z, s_cx, s_one = m.sem("ctx_zeroed", st), m.sem("ctx_in", st), m.sem("ones_set", st)
        s_rows, s_tr, s_rT = m.sem("rows2_ready", st), m.sem("transposed2", st), m.sem("rT2_ready", st)
        s_mm, s_p0, s_r1 = m.sem("projected2", st), m.sem("part0", st), m.sem("rest1", st)
        s_p1, s_p2, s_st = m.sem("part1", st), m.sem("part2", st), m.sem("parts_stored", st)
        s_vm, s_vd = m.sem("values_done", st), m.sem("values_copied", st)
        q_dst = m.q2_parts.rearrange("r (m h) k t -> (h k) (r m) t", m=KC)
        k_dst = m.k2_parts.rearrange("r (m h) k t -> (h k) (r m) t", m=KC)
        WHOLE = S_CTX - CTX_LAST
        with nc.Block() as block:
            @block.sync
            def _(sp):
                sp.sem_inc(s_st, 16)
                cv = ctx_sb[:].rearrange("p (t d) -> p t d", d=D)
                for c in range(NC - 1):
                    sp.dma_start(cv[:, TPC * c:TPC * (c + 1), :],
                                 m.ctx_in[0, c * CH:(c + 1) * CH].rearrange("(t p) d -> p t d", p=P)).then_inc(s_cx, 16)
                sp.wait_ge(s_z, 1)
                sp.dma_start(cv[0:CTX_LAST, NTC - 1, :], m.ctx_in[0, WHOLE:S_CTX, :]).then_inc(s_cx, 16)

                def store(c, dst, col):
                    sp.wait_ge(s_p2, c * KC + KC)
                    sp.dma_start(dst[:, :, ds(col, CH)], parts[:].rearrange("p r m t -> p (r m) t")).then_inc(s_st, 16)

                with sp.Fori(0, NC) as c:
                    store(c, k_dst, c * CH)
                with sp.Fori(0, NC) as c:
                    store(c + NC, q_dst, c * CH)
                sp.wait_ge(s_st, 16 * (2 * NC + 1))

            @block.gpsimd
            def _(g):
                assert (NC - 1) * TPC == NTC - 1
                g.memset(ctx_sb[:, (NTC - 1) * D:], 0.0).then_inc(s_z, 1)
                layernorm_pool(g, m, s_dve, 2 * NT + 1, s_pow)

            @block.scalar
            def _(a):
                def chunk(c, src, col, values):
                    a.copy(rows[:], src[:, ds(col * TPC * D, TPC * D)]).then_inc(s_rows, 1)
                    a.wait_ge(s_tr, c + 1)
                    a.copy(rT[:], p_t[:]).then_inc(s_rT, 1)
                    for k in range(KC):
                        a.wait_ge(s_st, (c + 1) * 16)
                        a.wait_ge(s_mm, c * KC + k + 1)
                        a.copy(parts[:, 0, k, :], p_m[:, k, :]).then_inc(s_p0, 1)
                    if values:
                        a.wait_ge(s_vm, c + 1)
                        a.copy(v2[:, ds(col * TPC, TPC), :, 0:DK],
                               p_v[:].rearrange("p a (h k) -> p a h k", k=DK)).then_inc(s_vd, 1)

                a.wait_ge(s_cx, 16 * NC)
                with a.Fori(0, NC) as c:
                    chunk(c, ctx_sb, c, True)
                a.wait_ge(s_xn, NT)
                with a.Fori(0, NC) as c:
                    chunk(c + NC, xn, c, False)

            @block.vector
            def _(v):
                v.sem_inc(s_r1, KC)
                v.memset(v2[:, :, :, DK:DK + 1], 1.0).then_inc(s_one, 1)
                layernorm_dve(v, m, s_dve, 0, s_pow, s_xn, xn)

                with v.Fori(0, 2 * NC) as c:
                    for k in range(KC):
                        v.wait_ge(s_p0, c * KC + k + 1)
                        v.tensor_tensor(rest[:, k, :], p_m[:, k, :], parts[:, 0, k, :], ALU.subtract).then_inc(s_r1, 1)
                        v.wait_ge(s_r1, KC + c * KC + k + 1)
                        v.tensor_copy(parts[:, 1, k, :], rest[:, k, :]).then_inc(s_p1, 1)
                        v.wait_ge(s_p1, c * KC + k + 1)
                        v.tensor_tensor(parts[:, 2, k, :], rest[:, k, :], parts[:, 1, k, :], ALU.subtract).then_inc(s_p2, 1)

            @block.tensor
            def _(pe):
                pe.sem_inc(s_vd, 1)

                def chunk(c, w, values):
                    pe.wait_ge(s_rows, c + 1)
                    for k in range(KC):
                        for j in range(TPC):
                            last = pe.transpose(p_t[:, k, j * P:(j + 1) * P],
                                                rows[:, j * D + k * P:j * D + (k + 1) * P], m.ident[:])
                    last.then_inc(s_tr, 1)
                    pe.wait_ge(s_rT, c + 1)
                    for n in range(KC):
                        pe.wait_ge(s_r1, c * KC + n + 1)
                        for k in range(KC):
                            last = pe.matmul(p_m[:, n, :], m.w_x[:, w, k, n * P:(n + 1) * P], rT[:, k, :],
                                             start=(k == 0), stop=(k == KC - 1))
                        last.then_inc(s_mm, 1)
                    if values:
                        pe.wait_ge(s_vd, c + 1)
                        for j in range(TPC):
                            for k in range(KC):
                                last = pe.matmul(p_v[:, j, :], rT[:, k, j * P:(j + 1) * P], m.w_x[:, 2, k, :],
                                                 start=(k == 0), stop=(k == KC - 1))
                        last.then_inc(s_vm, 1)

                with pe.Fori(0, NC) as c:
                    chunk(c, 1, True)
                with pe.Fori(0, NC) as c:
                    chunk(c + NC, 0, False)

def cross_attention_phase(nc, m, v2, ctx2):
    KT = NTC * P
    PRING, NPAIR, NDIAG = 4, 2 * NSTEP, len(DIAG)
    FIRST_SLOT, UNIT_SLOTS = 5, 26
    ROW_SLOT = FIRST_SLOT + UNIT_SLOTS + 1
    assert ROW_SLOT < NSTEP
    slot_units = {}
    for u in range(NU):
        slot_units.setdefault(FIRST_SLOT + u * UNIT_SLOTS // NU, []).append(u)

    with ExitStack() as st:
        qs = m.sb("qs", [STACK + 2, 2 * GH * T], BF16, st)
        ks = m.sb("ks", [STACK + 2, 2 * GH * KT], BF16, st)
        pw = m.sb("pw", [P, PRING, GH, CH], F32, st)
        vg = m.sb("vg", [P, NTC, GH, 32], F32, st)
        oT = m.sb("oT", [P, CH], F32, st)
        mask = m.sb("mask", [P, P], BF16, st)
        mx_part = m.sb("mx_part", [P, GH * NT, NC], F32, st)
        mx = m.sb("mx", [P, GH * NT], F32, st)
        neg = m.sb("neg", [GH * NT, 2, P], BF16, st)
        rden = m.sb("rden", [P, TPC, GH, 1], F32, st)
        p_st = m.pb("p_st", [P, 2, 2, CH], F32, st)
        p_mu = m.pb("p_mu", [P, 2, CH], F32, st)
        p_acc = m.pb("p_acc", [P, CH], F32, st)
        p_ot = m.pb("p_ot", [P, TPC, P], F32, st)
        s_set = m.sem("masks_set", st)
        s_stack = [m.sem(f"stacks_in{r}", st) for r in range(2)]
        s_rows = [m.sem(f"neg_rows_in{r}", st) for r in range(2)]
        s_st, s_exp, s_mask = m.sem("st_scores", st), m.sem("weights_ready", st), m.sem("masked", st)
        s_pv, s_acc, s_ott = m.sem("xpv_done", st), m.sem("acc_copied", st), m.sem("oT_transposed", st)
        s_rd, s_on, s_vg = m.sem("rden_ready", st), m.sem("heads_ready", st), m.sem("values_staged", st)
        s_mu, s_mr, s_mx = m.sem("unit_scores", st), m.sem("unit_max", st), m.sem("group_max", st)
        s_mt, s_nh, s_nm = m.sem("max_transposed", st), m.sem("neg_high", st), m.sem("neg_ready", st)
        s_ns, s_zero, s_low = m.sem("neg_stored", st), m.sem("mask_zeroed", st), m.sem("lowest_set", st)

        def slots(body_main, body_max, g, mg):
            for s in range(NSTEP + 2):
                body_main(s, g, 0)
                body_max(s, mg)
                body_main(s, g, 1)

        with nc.Block() as block:
            @block.tensor
            def _(pe):
                for s, n in ((s_pv, PRING), (s_ott, 1)):
                    pe.sem_inc(s, n)

                def transposed_scores(s, g, par):
                    c, j, off = STEPS[s]
                    rows = min(P, S_CTX - j * P)
                    if s == 0:
                        pe.wait_ge(s_rows[g % 2], 16 * (g // 2 + 1))
                    for pair in range(2):
                        pe.wait_ge(s_exp, g * NPAIR + 2 * s + pair + 1)
                        for h in (0, 1):
                            hh = 2 * pair + h
                            last = pe.matmul(p_st[0:rows, pair, h, off:CH],
                                             ks[:, ds(par * (GH * KT) + (hh * KT + j * P), rows)],
                                             qs[:, ds(par * (GH * T) + (hh * T + c * CH + off), CH - off)],
                                             start=True, stop=True)
                        last.then_inc(s_st, 1)

                def values(s, g):
                    c, j, off = STEPS[s]
                    rows = min(P, S_CTX - j * P)
                    last_j = s == LAST_OF[c]
                    if s == 0:
                        pe.wait_ge(s_vg, g + 1)
                    if j == 0:
                        pe.wait_ge(s_acc, g * NC + c + 1)
                    if s in DIAG:
                        pe.wait_ge(s_mask, g * NDIAG + DIAG.index(s) + 1)
                    else:
                        pe.wait_ge(s_exp, 2 + g * NPAIR + 2 * s + 2)
                    for hh in range(GH):
                        last = pe.matmul(p_acc[32 * hh:32 * hh + 32, off:CH], vg[0:rows, j, hh, :],
                                         pw[0:rows, s % PRING, hh, off:CH], start=(j == 0), stop=last_j)
                    last.then_inc(s_pv, 1)

                def out_transposes(c, g):
                    pe.wait_ge(s_acc, 1 + g * NC + c + 1)
                    pe.wait_ge(s_on, g * NC + c + 1)
                    for a in range(TPC):
                        last = pe.transpose(p_ot[:, a, :], oT[:, a * P:(a + 1) * P], m.ident[:])
                    last.then_inc(s_ott, 1)

                def unit(u, g, par):
                    i, h, k0, w = UNITS[u]
                    if u == 0:
                        pe.wait_ge(s_stack[g % 2], 16 * 2 * len(Q_PARTS) * (g // 2 + 1))
                        pe.wait_ge(s_nm, g + 1)
                    pe.wait_ge(s_mr, g * NU + u + 1)
                    diag = k0 <= i * P < k0 + w
                    last = pe.matmul(p_mu[:, u % 2, 0:w], qs[0:STACK, ds(par * (GH * T) + (h * T + i * P), P)],
                                     ks[0:STACK, ds(par * (GH * KT) + (h * KT + k0), w)],
                                     start=True, stop=not diag)
                    if diag:
                        last = pe.matmul(p_mu[:, u % 2, i * P - k0:w], m.identb[:], mask[:, 0:w - (i * P - k0)],
                                         start=False, stop=True)
                    last.then_inc(s_mu, 1)

                def max_rows(g):
                    pe.wait_ge(s_mx, g + 1)
                    pe.transpose(p_mu[0:GH * NT, 0, 0:P], mx[:], m.ident[:]).then_inc(s_mt, 1)

                def main_part(s, g, half):
                    if g is None:
                        return
                    if half == 0:
                        if s < NSTEP:
                            transposed_scores(s, g, g % 2)
                    else:
                        if 1 <= s <= NSTEP:
                            values(s - 1, g)
                        if s >= 2 and s - 2 in LAST_OF.values():
                            out_transposes(STEPS[s - 2][0], g)

                def max_part(s, g):
                    if g is None:
                        return
                    for u in slot_units.get(s, ()):
                        unit(u, g, g % 2)
                    if s == ROW_SLOT:
                        max_rows(g)

                pe.wait_ge(s_set, 3)
                slots(main_part, max_part, None, 0)
                for g in range(NG - 1):
                    slots(main_part, max_part, g, g + 1)
                slots(main_part, max_part, NG - 1, None)

            @block.scalar
            def _(a):
                for s, n in ((s_exp, 2), (s_acc, 1)):
                    a.sem_inc(s, n)

                def exps(s, g):
                    c, j, off = STEPS[s]
                    rows = min(P, S_CTX - j * P)
                    a.wait_ge(s_pv, g * NSTEP + s + 1)
                    for pair in range(2):
                        a.wait_ge(s_st, g * NPAIR + 2 * s + pair + 1)
                        a.activation(pw[0:rows, s % PRING, 2 * pair:2 * pair + 2, off:CH],
                                     p_st[0:rows, pair, :, off:CH], ACT.Exp, scale=1.0 / 4.0).then_inc(s_exp, 1)

                def group(g):
                    a.wait_ge(s_set, 3)
                    a.copy(vg[:, :, :, 0:DK + 1], v2[:, 0:NTC, ds(g * GH, GH), :]).then_inc(s_vg, 1)
                    for s in range(NSTEP + 1):
                        if s < NSTEP:
                            exps(s, g)
                        if s >= 1 and s - 1 in LAST_OF.values():
                            c = STEPS[s - 1][0]
                            a.wait_ge(s_pv, PRING + g * NSTEP + s)
                            a.wait_ge(s_ott, g * NC + c + 1)
                            a.copy(oT[:], p_acc[:]).then_inc(s_acc, 1)

                with a.Fori(0, NG) as g:
                    group(g)

            @block.gpsimd
            def _(g):
                g.memset(mask[:], 0.0).then_inc(s_zero, 1)
                g.wait_ge(s_zero, 1)
                g.affine_select(out=mask[:], in_=mask[:], compare_op=ALU.is_ge, fill=NEG, base=0,
                                pattern=[[-1, P]], channel_multiplier=1).then_inc(s_set, 1)
                g.memset(vg[:], 0.0).then_inc(s_set, 1)
                for gr in range(NG):
                    for s in DIAG:
                        c, j, off = STEPS[s]
                        rows = min(P, S_CTX - j * P)
                        blk = pw[0:rows, s % PRING, :, off:off + P]
                        g.wait_ge(s_exp, 2 + gr * NPAIR + 2 * s + 2)
                        g.affine_select(out=blk, in_=blk, compare_op=ALU.is_ge, fill=0.0, base=0,
                                        pattern=[[0, GH], [1, P]], channel_multiplier=-1).then_inc(s_mask, 1)

            @block.vector
            def _(v):
                for s, n in ((s_mr, 2), (s_on, 1), (s_nm, 1)):
                    v.sem_inc(s, n)
                v.memset(ks[STACK:STACK + 2, :], 1.0).then_inc(s_set, 1)
                v.memset(mx_part[:], LOWEST).then_inc(s_low, 1)
                v.wait_ge(s_low, 1)

                def main_part(s, g, half):
                    if g is None or half == 0 or s < 2 or s - 2 not in LAST_OF.values():
                        return
                    c = STEPS[s - 2][0]
                    po = p_ot[:].rearrange("p a (h w) -> p a h w", w=32)
                    v.wait_ge(s_ott, 1 + g * NC + c + 1)
                    v.reciprocal(rden[:], po[:, :, :, DK:DK + 1]).then_inc(s_rd, 1)
                    v.wait_ge(s_rd, g * NC + c + 1)
                    v.tensor_tensor(ctx2[:, c * TPC:(c + 1) * TPC, ds(g * (GH * DK), GH * DK)]
                                    .rearrange("p a (h k) -> p a h k", k=DK),
                                    po[:, :, :, 0:DK], rden[:].to_broadcast([P, TPC, GH, DK]),
                                    ALU.mult).then_inc(s_on, 1)

                def max_part(s, g):
                    if g is None:
                        return
                    for u in slot_units.get(s, ()):
                        i, h, k0, w = UNITS[u]
                        v.wait_ge(s_mu, g * NU + u + 1)
                        v.reduce_max(mx_part[:, h * NT + i, k0 // CH:k0 // CH + 1], p_mu[:, u % 2, 0:w],
                                     AX_X).then_inc(s_mr, 1)
                    if s == ROW_SLOT - 1:
                        v.wait_ge(s_mr, 2 + (g + 1) * NU)
                        v.reduce_max(mx[:], mx_part[:], AX_X).then_inc(s_mx, 1)
                    if s == ROW_SLOT:
                        v.wait_ge(s_ns, 16 * (g + 1))
                        v.wait_ge(s_mt, g + 1)
                        v.tensor_scalar(neg[:, 0, :], p_mu[0:GH * NT, 0, 0:P], -1.0, None,
                                        ALU.mult).then_inc(s_nh, 1)
                        v.wait_ge(s_nh, g + 1)
                        v.scalar_tensor_tensor(out=neg[:, 1, :], in0=p_mu[0:GH * NT, 0, 0:P], scalar=-1.0,
                                               in1=neg[:, 0, :], op0=ALU.mult, op1=ALU.subtract).then_inc(s_nm, 1)

                slots(main_part, max_part, None, 0)
                with v.Fori(0, NG - 1) as g:
                    slots(main_part, max_part, g, g + 1)
                slots(main_part, max_part, NG - 1, None)

            @block.sync
            def _(sp):
                sp.sem_inc(s_ns, 16)

                def stacks(g, par):
                    for dst, src, parts, w, n in ((qs, m.q2_parts, Q_PARTS, T, T), (ks, m.k2_parts, K_PARTS, KT, KT)):
                        for r, part in enumerate(parts):
                            sp.dma_start(dst[r * DK:(r + 1) * DK, ds(par * (GH * w), GH * w)]
                                         .rearrange("k (h t) -> k h t", h=GH),
                                         src[part, ds(g * GH, GH), :, 0:n].rearrange("h k t -> k h t")
                                         ).then_inc(s_stack[par], 16)

                def rows(g, par):
                    sp.wait_ge(s_nm, 1 + g + 1)
                    sp.dma_start(m.neg_rows[ds(g, 1)].rearrange("g r a q -> (g a) r q"), neg[:]).then_inc(s_ns, 16)
                    sp.wait_ge(s_ns, 16 * (g + 2))
                    sp.dma_start(qs[STACK:STACK + 2, ds(par * (GH * T), GH * T)],
                                 m.neg_rows[ds(g, 1)].rearrange("g r a q -> (g r) (a q)")).then_inc(s_rows[par], 16)

                stacks(0, 0)
                stacks(1, 1)
                rows(0, 0)
                rows(1, 1)
                for g in range(1, NG - 1):
                    sp.wait_ge(s_st, g * NPAIR)
                    stacks(g + 1, (g + 1) % 2)
                    rows(g + 1, (g + 1) % 2)

def cross_output_phase(nc, m, ctx2):
    with ExitStack() as st:
        rows = m.sb("rows5", [P, TPC * D], F32, st)
        rT = m.sb("rT5", [P, KC, CH], F32, st)
        p_t = m.pb("p_t5", [P, 2, KC, CH], F32, st)
        p_y = m.pb("p_y5", [P, TPC, D], F32, st)
        s_rows, s_tr, s_rT = m.sem("rows5_ready", st), m.sem("transposed5", st), m.sem("rT5_ready", st)
        s_y, s_add = m.sem("y5_ready", st), m.sem("added5", st)
        flat = ctx2[:].rearrange("p a d -> p (a d)")
        with nc.Block() as block:
            @block.scalar
            def _(a):
                with a.Fori(0, NC) as c:
                    a.copy(rows[:], flat[:, ds(c * TPC * D, TPC * D)]).then_inc(s_rows, 1)
                    a.wait_ge(s_tr, c + 1)
                    a.wait_ge(s_y, c + 1)
                    a.copy(rT[:], p_t[:, 0]).then_inc(s_rT, 1)

            @block.tensor
            def _(pe):
                pe.sem_inc(s_y, 1)
                with pe.Fori(0, NC) as c:
                    pe.wait_ge(s_rows, c + 1)
                    for k in range(KC):
                        for j in range(TPC):
                            last = pe.transpose(p_t[:, 0, k, j * P:(j + 1) * P],
                                                rows[:, j * D + k * P:j * D + (k + 1) * P], m.ident[:])
                    last.then_inc(s_tr, 1)
                    pe.wait_ge(s_rT, c + 1)
                    pe.wait_ge(s_add, c + 1)
                    for j in range(TPC):
                        for k in range(KC):
                            last = pe.matmul(p_y[:, j, :], rT[:, k, j * P:(j + 1) * P], m.w_x[:, 3, k, :],
                                             start=(k == 0), stop=(k == KC - 1))
                    last.then_inc(s_y, 1)

            @block.vector
            def _(v):
                v.sem_inc(s_add, 1)
                with v.Fori(0, NC) as c:
                    xs = m.x_res[:, ds(c * TPC * D, TPC * D)]
                    v.wait_ge(s_y, 1 + c + 1)
                    v.tensor_tensor(xs, p_y[:].rearrange("p a d -> p (a d)"), xs, ALU.add).then_inc(s_add, 1)

def routing_phase(nc, m, w_sb, s_w, slot_idx, gates, block_expert):
    NR = NT * E
    with ExitStack() as st:
        rows = m.sb("rows6", [P, 2, TPC * D], F32, st)
        rT = m.sb("rT6", [P, KC, CH], F32, st)
        xhl = m.sb("xhl", [P, NT, 2, D], BF16, st)
        logit = m.sb("logit", [P, NT, E], F32, st)
        prob = m.sb("prob", [P, NT, E], F32, st)
        top1 = m.sb("top1", [P, NT, 1], F32, st)
        psum_ = m.sb("prob_sum", [P, NT, 1], F32, st)
        best_i = m.sb("best_i", [P, NT, E], U32, st)
        idx_f = m.sb("idx_f", [P, NT, TOPK], F32, st)
        pick = m.sb("pick", [P, TOPK, NT, E], F32, st)
        picked = m.sb("picked", [P, NT + 1, E], BF16, st)
        before = m.sb("before", [P, P], BF16, st)
        onesb = m.sb("onesb", [P, P], BF16, st)
        iota_i = m.sb("iota_i", [P, NBLK], mybir.dt.int32, st)
        iota = m.sb("iota", [P, NBLK], F32, st)
        ones8 = m.sb("ones8", [P, E], F32, st)
        cnt = m.sb("cnt", [P, E, 1], F32, st)
        over = m.sb("over", [P, E, NT], F32, st)
        nblk = m.sb("nblk", [P, E], F32, st)
        end = m.sb("end", [P, E], F32, st)
        base = m.sb("base", [P, 1, E], F32, st)
        pos = m.sb("pos", [P, NT, E], F32, st)
        posk = m.sb("posk", [P, NT, E], F32, st)
        slot_f = m.sb("slot_f", [P, TOPK, NT], F32, st)
        past = m.sb("past", [P, NBLK, E], F32, st)
        blk_f = m.sb("blk_f", [P, NBLK], F32, st)
        p_t = m.pb("p_t6", [P, KC, CH], F32, st)
        p_lg = m.pb("p_lg", [P, NT, E], F32, st)
        p_rank = m.pb("p_rank", [P, NT + 1, E], F32, st)
        s_dve, s_pow, s_xn = m.sem("ln3_dve", st), m.sem("ln3_pow", st), m.sem("xn3_ready", st)
        s_tr, s_rT, s_lg = m.sem("transposed6", st), m.sem("rT6_ready", st), m.sem("logits", st)
        s_xh, s_xl, s_c = m.sem("x_high", st), m.sem("x_low", st), m.sem("constants", st)
        s_v, s_sub, s_ex = m.sem("routing_chain", st), m.sem("logits_shifted", st), m.sem("prob_exp", st)
        s_pick, s_rank, s_slot = m.sem("picked_ready", st), m.sem("ranked", st), m.sem("slots_ready", st)
        s_res = m.sem("residual_added", st)
        s_xs, s_sc = m.sem("shared_rows_out", st), m.sem("rows_scattered", st)
        with nc.Block() as block:
            @block.sync
            def _(sp):
                for e in WEIGHT_ORDER:
                    sp.dma_start(w_sb[:, e, :], m.w_img[e]).then_inc(s_w[e], 16)
                sp.wait_ge(s_xl, NT)
                sp.dma_start(m.x_slots[0:T, :].rearrange("(t p) n -> p t n", p=P),
                             xhl[:].rearrange("p t r d -> p t (r d)")).then_inc(s_xs, 16)
                sp.wait_ge(s_xs, 16)

            @block.gpsimd
            def _(g):
                g.memset(onesb[:], 1.0).then_inc(s_c, 1)
                g.memset(before[:], 1.0).then_inc(s_c, 1)
                g.memset(ones8[:], 1.0).then_inc(s_c, 1)
                g.iota(iota_i[:], pattern=[[1, NBLK]], base=0, channel_multiplier=0).then_inc(s_c, 1)
                g.wait_ge(s_c, 2)
                g.affine_select(out=before[:], in_=before[:], compare_op=ALU.is_gt, fill=0.0, base=0,
                                pattern=[[1, P]], channel_multiplier=-1).then_inc(s_c, 1)
                layernorm_pool(g, m, s_dve, 2 * NT + 1, s_pow)
                g.wait_ge(s_xl, NT)
                g.wait_ge(s_slot, 1)
                for t in range(NT):
                    for k in range(TOPK):
                        g.indirect_dma_start(m.x_slots,
                                             bass.IndirectOffsetOnAxis(ap=slot_idx[:, k * NT + t:k * NT + t + 1], axis=0),
                                             xhl[:, t].rearrange("p r d -> p (r d)"), None).then_inc(s_sc, 16)
                g.wait_ge(s_sc, 16 * NT * TOPK)

            @block.tensor
            def _(pe):
                for c in range(NC):
                    pe.wait_ge(s_xn, (c + 1) * TPC)
                    if c:
                        pe.wait_ge(s_rT, c)
                    for k in range(KC):
                        for j in range(TPC):
                            last = pe.transpose(p_t[:, k, j * P:(j + 1) * P],
                                                rows[:, c % 2, j * D + k * P:j * D + (k + 1) * P], m.ident[:])
                    last.then_inc(s_tr, 1)
                    pe.wait_ge(s_rT, c + 1)
                    for j in range(TPC):
                        for k in range(KC):
                            last = pe.matmul(p_lg[:, c * TPC + j, :], rT[:, k, j * P:(j + 1) * P], m.w_rt[:, k, :],
                                             start=(k == 0), stop=(k == KC - 1))
                    last.then_inc(s_lg, 1)
                pe.wait_ge(s_c, 5)
                pe.wait_ge(s_pick, 1)
                pe.matmul(p_rank[:], before[:], picked[:], start=True, stop=False)
                for t in range(NT):
                    last = pe.matmul(p_rank[:, t + 1:, :], onesb[:],
                                     picked[:, t:t + 1, :].to_broadcast([P, NT - t, E]),
                                     start=False, stop=(t == NT - 1))
                last.then_inc(s_rank, 1)

            @block.scalar
            def _(a):
                for c in range(NC):
                    a.wait_ge(s_tr, c + 1)
                    if c:
                        a.wait_ge(s_lg, c)
                    a.copy(rT[:], p_t[:]).then_inc(s_rT, 1)
                    a.wait_ge(s_xn, (c + 1) * TPC)
                    a.copy(xhl[:, c * TPC:(c + 1) * TPC, 0, :],
                           rows[:, c % 2, :].rearrange("p (t d) -> p t d", d=D)).then_inc(s_xh, 1)
                a.wait_ge(s_sub, 1)
                a.activation(prob[:], logit[:], ACT.Exp).then_inc(s_ex, 1)

            @block.vector
            def _(v):
                for t in range(NT):
                    v.bn_stats(m.stats[:, t, :], m.x_res[:, t * D:(t + 1) * D]).then_inc(s_dve, 1)
                for t in range(NT):
                    v.wait_ge(s_dve, t + 1)
                    v.bn_aggr(m.mv[:, t, :], m.stats[:, t, :]).then_inc(s_dve, 1)
                v.wait_ge(s_dve, 2 * NT)
                v.tensor_scalar(m.var_eps[:], m.mv[:, :, 1], EPS, None, ALU.add).then_inc(s_dve, 1)
                v.wait_ge(s_pow, 1)
                for c in range(NC):
                    if c >= 2:
                        v.wait_ge(s_tr, c - 1)
                    for j in range(TPC):
                        t = c * TPC + j
                        v.tensor_scalar(rows[:, c % 2, j * D:(j + 1) * D], m.x_res[:, t * D:(t + 1) * D],
                                        m.mv[:, t, 0:1], m.rstd[:, t:t + 1], ALU.subtract, ALU.mult).then_inc(s_xn, 1)
                    for j in range(TPC):
                        t = c * TPC + j
                        v.wait_ge(s_xh, c + 1)
                        v.tensor_tensor(xhl[:, t, 1, :], rows[:, c % 2, j * D:(j + 1) * D], xhl[:, t, 0, :],
                                        ALU.subtract).then_inc(s_xl, 1)
                    xs = m.x_res[:, c * TPC * D:(c + 1) * TPC * D]
                    v.wait_ge(s_xn, (c + 1) * TPC)
                    v.tensor_tensor(xs, xs, rows[:, c % 2, :], ALU.add).then_inc(s_res, 1)
                n = [0]

                def link(ins):
                    n[0] += 1
                    ins.then_inc(s_v, 1)
                    v.wait_ge(s_v, n[0])

                v.wait_ge(s_c, 5)
                v.wait_ge(s_lg, NC)
                link(v.tensor_copy(iota[:], iota_i[:]))
                link(v.memset(picked[:, NT, :], 0.0))
                link(v.reduce_max(top1[:], p_lg[:], AX_X))
                v.tensor_tensor(logit[:], p_lg[:], top1[:].to_broadcast([P, NT, E]), ALU.subtract).then_inc(s_sub, 1)
                v.wait_ge(s_ex, 1)
                link(v.reduce_sum(psum_[:], prob[:], AX_X))
                link(v.reciprocal(top1[:], psum_[:]))
                link(v.tensor_tensor(prob[:], prob[:], top1[:].to_broadcast([P, NT, E]), ALU.mult))
                for t in range(NT):
                    v.max(gates[:, t, :], prob[:, t, :]).then_inc(s_v, 1)
                n[0] += NT
                for t in range(NT):
                    v.wait_ge(s_v, n[0] - NT + t + 1)
                    v.max_index(best_i[:, t, :], gates[:, t, :], prob[:, t, :]).then_inc(s_v, 1)
                n[0] += NT
                v.wait_ge(s_v, n[0])
                link(v.tensor_copy(idx_f[:], best_i[:, :, 0:TOPK]))
                for k in range(TOPK):
                    link(v.tensor_tensor(pick[:, k], iota[:, None, 0:E].to_broadcast([P, NT, E]),
                                         idx_f[:, :, k:k + 1].to_broadcast([P, NT, E]), ALU.is_equal))
                v.tensor_tensor(picked[:, 0:NT, :], pick[:, 0], pick[:, 1], ALU.add).then_inc(s_pick, 1)
                v.wait_ge(s_rank, 1)
                link(v.tensor_copy(cnt[:, :, 0], p_rank[:, NT, :]))
                link(v.tensor_scalar(blk_f[:, 0:NT], iota[:, 0:NT], float(P), None, ALU.mult))
                link(v.tensor_tensor(over[:], cnt[:].to_broadcast([P, E, NT]),
                                     blk_f[:, None, 0:NT].to_broadcast([P, E, NT]), ALU.is_gt))
                link(v.reduce_sum(nblk[:], over[:], AX_X))
                link(v.tensor_tensor_scan(end[:], ones8[:], nblk[:], float(NT), ALU.mult, ALU.add))
                link(v.tensor_tensor(base[:, 0, :], end[:], nblk[:], ALU.subtract))
                link(v.tensor_scalar(base[:], base[:], float(P), None, ALU.mult))
                link(v.tensor_tensor(pos[:], p_rank[:, 0:NT, :], base[:].to_broadcast([P, NT, E]), ALU.add))
                for k in range(TOPK):
                    link(v.tensor_tensor(posk[:], pos[:], pick[:, k], ALU.mult))
                    link(v.reduce_sum(slot_f[:, k, :], posk[:], AX_X))
                v.tensor_copy(slot_idx[:], slot_f[:].rearrange("p k t -> p (k t)")).then_inc(s_slot, 1)
                link(v.tensor_tensor(past[:], iota[:, :, None].to_broadcast([P, NBLK, E]),
                                     end[:, None, :].to_broadcast([P, NBLK, E]), ALU.is_ge))
                link(v.reduce_sum(blk_f[:], past[:], AX_X))
                link(v.tensor_scalar(blk_f[:], blk_f[:], float(E - 1), None, ALU.min))
                link(v.memset(blk_f[:, 0:NT], float(E)))
                link(v.tensor_copy(block_expert[:], blk_f[:]))


def expert_blocks_phase(nc, m, w_sb, s_w, block_expert):
    UP, DN = 0, 2 * KC * F
    with ExitStack() as st:
        xb = m.sb("xb", [P, 2, 2 * D], BF16, st)
        xT = m.sb("xT", [P, 2, 2 * KC * P], BF16, st)
        h32 = m.sb("h32", [P, 2, NF * P], F32, st)
        hT = m.sb("hT", [P, 2, 2, NF * P], BF16, st)
        ysb = m.sb("ysb", [P, 2, D], F32, st)
        p_x = m.pb("p_x", [P, 2, 2 * CH], BF16, st)
        p_h = m.pb("p_h", [P, 2, NF * P], F32, st)
        p_y = m.pb("p_y7", [P, 2, CH], F32, st)
        s_xb = [m.sem(f"xb_in{r}", st) for r in range(2)]
        s_xt, s_xT, s_up = m.sem("x_transposed", st), m.sem("xT_ready", st), m.sem("up_done", st)
        s_ge, s_hh, s_hl = m.sem("gelu_done", st), m.sem("h_high", st), m.sem("h_low", st)
        s_dn, s_ys = m.sem("down_done", st), m.sem("y_copied", st)
        s_yo = [m.sem(f"y_out{r}", st) for r in range(2)]
        with nc.Block() as block:
            @block.sync
            def _(sp):
                def load(b, r):
                    sp.dma_start(xb[:, r, :], m.x_slots[ds(b * P, P), :]).then_inc(s_xb[r], 16)

                def store(b, r):
                    sp.wait_ge(s_ys, 2 + b + 1)
                    sp.dma_start(m.y_slots[ds(b * P, P), :], ysb[:, r, :]).then_inc(s_yo[r], 16)

                for r in range(2):
                    load(r, r)
                    sp.sem_inc(s_yo[r], 16)
                with sp.Fori(0, NBLK // 2 - 1) as q:
                    for r in range(2):
                        sp.wait_ge(s_xt, 2 * q + r + 1)
                        load(2 * q + r + 2, r)
                        store(2 * q + r, r)
                for r in range(2):
                    store(NBLK - 2 + r, r)
                for r in range(2):
                    sp.wait_ge(s_yo[r], 16 * (NBLK // 2 + 1))

            @block.tensor
            def _(pe):
                def up(b, q, r):
                    pe.wait_ge(s_xb[r], 16 * (q + 1))
                    pe.wait_ge(s_xT, b + 1)
                    for n in range(2 * KC):
                        last = pe.transpose(p_x[:, r, n * P:(n + 1) * P], xb[:, r, n * P:(n + 1) * P], m.identb[:])
                    last.then_inc(s_xt, 1)
                    e = pe.value_load(block_expert[0:1, ds(b, 1)], min_val=0, max_val=E)
                    w0 = pe.snap(e * WCOLS)
                    pe.wait_ge(s_xT, 2 + b + 1)
                    pe.wait_ge(s_ge, 2 * b + 2)
                    for f in range(NF):
                        n = 0
                        for wp, xp in PASSES:
                            for k in range(KC):
                                col = UP + wp * KC * F + k * F + f * P
                                last = pe.matmul(p_h[:, r, f * P:(f + 1) * P], flat[:, ds(w0 + col, P)],
                                                 xT[:, r, (xp * KC + k) * P:(xp * KC + k + 1) * P],
                                                 start=(n == 0), stop=(n == 3 * KC - 1))
                                n += 1
                        if f % (NF // 2) == NF // 2 - 1:
                            last.then_inc(s_up, 1)
                    return w0

                def down(b, r, w0):
                    pe.wait_ge(s_ys, b + 1)
                    for f in range(NF):
                        if f % (NF // 2) == 0:
                            pe.wait_ge(s_hl, 4 + 2 * b + f // (NF // 2) + 1)
                        for n, (wp, hp) in enumerate(PASSES):
                            col = DN + wp * NF * D + f * D
                            last = pe.matmul(p_y[:, r, 0:D], hT[:, r, hp, f * P:(f + 1) * P],
                                             flat[:, ds(w0 + col, D)],
                                             start=(f == 0 and n == 0), stop=(f == NF - 1 and n == 2))
                    last.then_inc(s_dn, 1)

                flat = w_sb[:].rearrange("p e n -> p (e n)")
                for e in range(E + 1):
                    pe.wait_ge(s_w[e], 16)
                with pe.Fori(0, NBLK // 2) as q:
                    w0 = up(2 * q, q, 0)
                    w1 = up(2 * q + 1, q, 1)
                    down(2 * q, 0, w0)
                    down(2 * q + 1, 1, w1)

            @block.scalar
            def _(a):
                a.sem_inc(s_xT, 2)
                a.sem_inc(s_ys, 2)
                a.sem_inc(s_ge, 4)

                def copy_xT(b, r):
                    a.wait_ge(s_xt, b + 1)
                    a.wait_ge(s_up, 2 * b + 2)
                    a.copy(xT[:, r, :], p_x[:, r, 0:2 * KC * P]).then_inc(s_xT, 1)

                def gelus(b, r):
                    for z in range(2):
                        half = slice(z * NF * P // 2, (z + 1) * NF * P // 2)
                        a.wait_ge(s_up, 4 + 2 * b + z + 1)
                        a.wait_ge(s_hl, 2 * b + z + 1)
                        a.activation(h32[:, r, half], p_h[:, r, half], ACT.Gelu).then_inc(s_ge, 1)

                def copy_y(b, q, r):
                    a.wait_ge(s_dn, 2 + b + 1)
                    a.wait_ge(s_yo[r], 16 * (q + 1))
                    a.copy(ysb[:, r, :], p_y[:, r, 0:D]).then_inc(s_ys, 1)

                with a.Fori(0, NBLK // 2) as q:
                    copy_xT(2 * q, 0)
                    copy_xT(2 * q + 1, 1)
                    gelus(2 * q, 0)
                    gelus(2 * q + 1, 1)
                    copy_y(2 * q, q, 0)
                    copy_y(2 * q + 1, q, 1)

            @block.vector
            def _(v):
                v.sem_inc(s_up, 4)
                v.sem_inc(s_hl, 4)
                v.sem_inc(s_dn, 2)
                with v.Fori(0, NBLK // 2) as q:
                    for r in range(2):
                        b = 2 * q + r
                        for z in range(2):
                            half = slice(z * NF * P // 2, (z + 1) * NF * P // 2)
                            v.wait_ge(s_ge, 4 + 2 * b + z + 1)
                            v.wait_ge(s_dn, b + 1)
                            v.tensor_copy(hT[:, r, 0, half], h32[:, r, half]).then_inc(s_hh, 1)
                            v.wait_ge(s_hh, 2 * b + z + 1)
                            v.tensor_tensor(hT[:, r, 1, half], h32[:, r, half], hT[:, r, 0, half],
                                            ALU.subtract).then_inc(s_hl, 1)


def combine_phase(nc, m, slot_idx, gates):
    RING = 4
    with ExitStack() as st:
        ya = m.sb("ya", [P, RING, 3, D], F32, st)
        s_sh = [m.sem(f"shared_in{r}", st) for r in range(RING)]
        s_g = [[m.sem(f"gathered{k}_{r}", st) for r in range(RING)] for k in range(TOPK)]
        s_v, s_t, s_out = m.sem("combine_chain", st), m.sem("tile_done", st), m.sem("out_stored", st)
        with nc.Block() as block:
            @block.gpsimd
            def _(g):
                for t in range(NT):
                    r = t % RING
                    if t >= RING:
                        g.wait_ge(s_t, t - RING + 1)
                    for k in range(TOPK):
                        g.indirect_dma_start(ya[:, r, 1 + k, :], None, m.y_slots,
                                             bass.IndirectOffsetOnAxis(ap=slot_idx[:, k * NT + t:k * NT + t + 1], axis=0)
                                             ).then_inc(s_g[k][r], 16)

            @block.sync
            def _(sp):
                for t in range(NT):
                    r = t % RING
                    if t >= RING:
                        sp.wait_ge(s_t, t - RING + 1)
                    sp.dma_start(ya[:, r, 0, :], m.y_slots[t * P:(t + 1) * P, :]).then_inc(s_sh[r], 16)

            @block.scalar
            def _(a):
                for t in range(NT):
                    a.wait_ge(s_t, t + 1)
                    a.dma_start(m.out[0, t * P:(t + 1) * P, :], m.x_res[:, t * D:(t + 1) * D]).then_inc(s_out, 16)
                a.wait_ge(s_out, 16 * NT)

            @block.vector
            def _(v):
                for t in range(NT):
                    r, xs = t % RING, m.x_res[:, t * D:(t + 1) * D]
                    v.wait_ge(s_sh[r], 16 * (t // RING + 1))
                    v.tensor_tensor(xs, xs, ya[:, r, 0, :], ALU.add).then_inc(s_v, 1)
                    v.wait_ge(s_v, 2 * t + 1)
                    v.wait_ge(s_g[0][r], 16 * (t // RING + 1))
                    v.scalar_tensor_tensor(out=xs, in0=ya[:, r, 1, :], scalar=gates[:, t, 0:1], in1=xs,
                                           op0=ALU.mult, op1=ALU.add).then_inc(s_v, 1)
                    v.wait_ge(s_v, 2 * t + 2)
                    v.wait_ge(s_g[1][r], 16 * (t // RING + 1))
                    v.scalar_tensor_tensor(out=xs, in0=ya[:, r, 2, :], scalar=gates[:, t, 1:2], in1=xs,
                                           op0=ALU.mult, op1=ALU.add).then_inc(s_t, 1)


def experts_phase(nc, m):
    with ExitStack() as st:
        w_sb = m.sb("w_sb", [P, E + 1, WCOLS], BF16, st)
        slot_idx = m.sb("slot_idx", [P, TOPK * NT], U32, st)
        gates = m.sb("gates", [P, NT, E], F32, st)
        block_expert = m.sb("block_expert", [P, NBLK], U32, st)
        s_w = [m.sem(f"weights{e}", st) for e in range(E + 1)]
        routing_phase(nc, m, w_sb, s_w, slot_idx, gates, block_expert)
        expert_blocks_phase(nc, m, w_sb, s_w, block_expert)
        combine_phase(nc, m, slot_idx, gates)
def build(nc, x, ctx_in, W_qkv, b_qkv, W_out, b_out, WqT, WkT, WvT, WoT,
          shared_up, shared_down, routed_up, routed_down, router_w, out):
    with ExitStack() as top:
        def sb(name, shape, dt=F32, st=top):
            return st.enter_context(nc.sbuf_tensor(name, shape, dt))

        def pb(name, shape, dt=F32, st=top):
            return st.enter_context(nc.psum_tensor(name, shape, dt))

        def sem(name, st=top):
            return st.enter_context(nc.semaphore(name))

        def dram(name, shape, dt):
            return nc.dram_tensor(name, shape, dt, kind="Internal").ap()

        w_img = dram("w_img", [E + 1, P, WCOLS], BF16)
        q2_parts = dram("q2_parts", [3, HEADS, DK, T], BF16)
        k2_parts = dram("k2_parts", [3, HEADS, DK, T], BF16)
        neg_rows = dram("neg_rows", [NG, 2, GH * NT, P], BF16)
        x_slots = dram("x_slots", [SLOTS, 2 * D], BF16)
        y_slots = dram("y_slots", [SLOTS, D], F32)

        x_res = sb("x_res", [P, NT * D])
        ident = sb("ident", [P, P])
        identb = sb("identb", [P, P], BF16)
        ones_row = sb("ones_row", [1, P])
        b_rows = sb("b_rows", [1, 2 * D])
        b_qk = sb("b_qk", [P, 2 * KC])
        w_rt = sb("w_rt", [P, KC, E])
        stats = sb("stats", [P, NT, 6])
        mv = sb("mv", [P, NT, 2])
        var_eps = sb("var_eps", [P, NT])
        neg_half = sb("neg_half", [P, NT])
        rstd = sb("rstd", [P, NT])

        att = top.enter_context(ExitStack())
        w_qkv = sb("w_qkv", [P, KC, 3 * D], F32, att)
        w_out = sb("w_out", [P, KC, D], F32, att)
        w_x = sb("w_x", [P, 4, KC, D], F32, att)

        m = Shared()
        m.sb, m.pb, m.sem, m.x_res, m.ident = sb, pb, sem, x_res, ident
        m.identb, m.ones_row, m.b_rows, m.b_qk, m.w_qkv = identb, ones_row, b_rows, b_qk, w_qkv
        m.w_out, m.w_x, m.w_rt, m.stats, m.mv = w_out, w_x, w_rt, stats, mv
        m.var_eps, m.neg_half, m.rstd, m.w_img, m.q2_parts = var_eps, neg_half, rstd, w_img, q2_parts
        m.k2_parts, m.neg_rows, m.x_slots, m.y_slots, m.ctx_in = k2_parts, neg_rows, x_slots, y_slots, ctx_in
        m.shared_up, m.shared_down, m.routed_up, m.routed_down, m.out = shared_up, shared_down, routed_up, routed_down, out

        with ExitStack() as st:
            s_in = sem("inputs_in", st)
            s_fill = sem("filled", st)
            s_sel = sem("selected", st)
            with nc.Block() as block:
                @block.sync
                def _(sp):
                    xv = x.rearrange("a (t p) d -> p (a t) d", p=P)
                    xr = x_res[:].rearrange("p (t d) -> p t d", d=D)
                    for c in range(NC):
                        sp.dma_start(xr[:, TPC * c:TPC * (c + 1), :], xv[:, TPC * c:TPC * (c + 1), :]).then_inc(s_in, 16)
                    sp.dma_start(w_qkv[:], W_qkv.rearrange("(k p) n -> p k n", p=P)).then_inc(s_in, 16)
                    sp.dma_start(w_out[:], W_out.rearrange("(k p) n -> p k n", p=P)).then_inc(s_in, 16)
                    for n, w in enumerate((WqT, WkT, WvT, WoT)):
                        sp.dma_start(w_x[:, n], w.rearrange("(k p) n -> p k n", p=P)).then_inc(s_in, 16)
                    sp.dma_start(w_rt[:], router_w.rearrange("(k p) n -> p k n", p=P)).then_inc(s_in, 16)
                    sp.dma_start(b_qk[:], b_qkv[0:2 * D].rearrange("(m p) -> p m", p=P),
                                 allow_slow_non_contiguous=True).then_inc(s_in, 16)
                    sp.dma_start(b_rows[:, 0:D], b_qkv[2 * D:3 * D].rearrange("(a n) -> a n", a=1)).then_inc(s_in, 16)
                    sp.dma_start(b_rows[:, D:2 * D], b_out.rearrange("(a n) -> a n", a=1)).then_inc(s_in, 16)
                    sp.wait_ge(s_in, 16 * 14)

                @block.gpsimd
                def _(g):
                    g.memset(ident[:], 0.0).then_inc(s_fill, 1)
                    g.memset(identb[:], 0.0).then_inc(s_fill, 1)
                    g.memset(ones_row[:], 1.0)
                    g.memset(neg_half[:], -0.5)
                    g.wait_ge(s_fill, 2)
                    for m in (ident, identb):
                        g.affine_select(out=m[:], in_=m[:], compare_op=ALU.not_equal, fill=1.0, base=0,
                                        pattern=[[-1, P]], channel_multiplier=1).then_inc(s_sel, 1)

        with ExitStack() as sa:
            qk = [sb(f"qk{r}", [P, 2 * KC, T], BF16, sa) for r in range(2)]
            vv = [sb(f"vv{r}", [P, NT * D], BF16, sa) for r in range(2)]
            qkv_phase(nc, m, qk, vv)
            self_attention_phase(nc, m, qk, vv)
        with ExitStack() as xa:
            ctx2 = sb("ctx2", [P, NT, HEADS * DK], F32, xa)
            v2 = sb("v2", [P, NT, HEADS, DK + 1], F32, xa)
            cross_projection_phase(nc, m, v2)
            cross_attention_phase(nc, m, v2, ctx2)
            cross_output_phase(nc, m, ctx2)
        att.close()
        experts_phase(nc, m)


_INS = ['x', 'ctx_1024', 'L0_attn_W_qkv', 'L0_attn_b_qkv', 'L0_attn_W_out', 'L0_attn_b_out', 'L0_xattn_Wq',
        'L0_xattn_Wk', 'L0_xattn_Wv', 'L0_xattn_Wo', 'L0_ffn_shared_up', 'L0_ffn_shared_down',
        'L0_ffn_routed_up', 'L0_ffn_routed_down', 'L0_ffn_router_w']
_TRANSPOSED = ['L0_xattn_Wq', 'L0_xattn_Wk', 'L0_xattn_Wv', 'L0_xattn_Wo']


def kernel(**inputs):
    import concourse.bacc as bacc
    from concourse.bass_utils import run_bass_kernel_spmd

    nc = bacc.Bacc("TRN2", target_bir_lowering=False, num_devices=1)
    arrays, args = {}, []
    for name in _INS:
        a = np.asarray(inputs[name])
        a = np.ascontiguousarray(a.T if name in _TRANSPOSED else a)
        arrays[f"in_{name}"] = a
        args.append(nc.dram_tensor(f"in_{name}", a.shape, mybir.dt.from_np(a.dtype), kind="ExternalInput").ap())
    args.append(nc.dram_tensor("out_x", (1, T, D), F32, kind="ExternalOutput").ap())
    build(nc, *args)
    result = run_bass_kernel_spmd(nc, [arrays], core_ids=[0])
    return result.results[0]["out_x"]
```

```python
from contextlib import ExitStack

import numpy as np

import concourse.bass as bass
from concourse import mybir

F32 = mybir.dt.float32
BF16 = mybir.dt.bfloat16
U32 = mybir.dt.uint32
ALU = mybir.AluOpType
ACT = mybir.ActivationFunctionType
AX_X = mybir.AxisListType.X
ds = bass.ds

P = 128
D = 256
KC = D // P
T = 2048
NT = T // P
CH = 512
NC = T // CH
TPC = CH // P
S_CTX = 1601
NTC = (S_CTX + P - 1) // P
CTX_LAST = S_CTX - (NTC - 1) * P
HEADS = 16
DK = D // HEADS
GH = 4
NG = HEADS // GH
F = 1024
NF = F // P
E = 8
TOPK = 2
RB = 2 * P
ROUTED = (T * TOPK + E * (RB - 1)) // RB
SLOTS = ROUTED * RB
WEIGHT_ORDER = [E, *range(E)]
UP, DOWN = 0, 2 * KC * F
WCOLS = 2 * KC * F + 2 * NF * D
EPS = 1e-5
NEG = -1.0e30
LEAD = 0.14
PASSES = ((0, 0), (0, 1), (1, 0))
Q_PARTS = (0, 0, 0, 1, 1, 2)
K_PARTS = (0, 1, 2, 0, 1, 0)
STACK = len(Q_PARTS) * DK
STEPS = [(c, j, max(0, j - TPC * c) * P) for c in range(NC) for j in range(min(TPC * (c + 1), NTC))]
NSTEP = len(STEPS)
DIAG = [s for s, (c, j, _) in enumerate(STEPS) if j >= TPC * c]
LAST_OF = {c: max(s for s, x in enumerate(STEPS) if x[0] == c) for c in range(NC)}
FIRST_OF = {c: min(s for s, x in enumerate(STEPS) if x[0] == c) for c in range(NC)}
UNITS = [[(i, h, k, min(CH, min(P * (i + 1), S_CTX) - k)) for i in range(TPC * c, TPC * (c + 1)) for h in range(GH)
          for k in range(0, min(P * (i + 1), S_CTX), CH)] for c in range(NC)]


def cross_schedule():
    stream = []
    for g in range(NG):
        for c in range(NC):
            row = []
            if stream:
                row = [("row", g * NC + c - 1)]
            units = [("unit", g, c, n) for n in range(len(UNITS[c]))]
            stream += units[:3] + row + units[3:]
    stream.append(("row", NG * NC - 1))

    def vector_work(x):
        return UNITS[x[2]][x[3]][3] + 64 if x[0] == "unit" else 600

    total = sum(vector_work(x) for x in stream)
    main_total = NG * sum(CH - off for _, _, off in STEPS)
    entries, ranges, done, main, at = [], {}, 0, 0, 0
    for step in range(-1, NG * NSTEP + 2):
        for place in range(3):
            first = len(entries)
            if 0 <= step < NG * NSTEP:
                main += (CH - STEPS[step % NSTEP][2]) / 3
            while at < len(stream) and done < (LEAD + main / main_total) * total:
                done += vector_work(stream[at])
                entries.append(stream[at])
                at += 1
            if place == 2 and step >= 2 and (step - 2) % NSTEP in LAST_OF.values():
                entries.append(("out", (step - 2) // NSTEP * NC + STEPS[(step - 2) % NSTEP][0]))
            ranges[step, place] = (first, len(entries))
    assert at == len(stream)
    return entries, ranges


class Shared:
    pass

LN_LINKS = 2 * TPC + 1


def layernorm_stats(v, m, s_ln, c):
    for t in range(c * TPC, (c + 1) * TPC):
        v.bn_stats(m.stats[:, t, :], m.x_res[:, t * D:(t + 1) * D]).then_inc(s_ln, 1)
    for j in range(TPC):
        v.wait_ge(s_ln, c * LN_LINKS + j + 1)
        v.bn_aggr(m.mv[:, c * TPC + j, :], m.stats[:, c * TPC + j, :]).then_inc(s_ln, 1)
    v.wait_ge(s_ln, c * LN_LINKS + 2 * TPC)
    v.tensor_scalar(m.var_eps[:, c * TPC:(c + 1) * TPC], m.mv[:, c * TPC:(c + 1) * TPC, 1], EPS, None,
                    ALU.add).then_inc(s_ln, 1)


def layernorm_power(g, m, s_ln, s_pow):
    for c in range(NC):
        g.wait_ge(s_ln, (c + 1) * LN_LINKS)
        tiles = slice(c * TPC, (c + 1) * TPC)
        g.tensor_tensor(m.rstd[:, tiles], m.var_eps[:, tiles], m.neg_half[:, tiles], ALU.pow).then_inc(s_pow, 1)


def layernorm_rows(v, m, s_xn, xn, c):
    for j in range(TPC):
        t = c * TPC + j
        v.tensor_scalar(xn[:, j * D:(j + 1) * D], m.x_res[:, t * D:(t + 1) * D],
                        m.mv[:, t, 0:1], m.rstd[:, t:t + 1], ALU.subtract, ALU.mult).then_inc(s_xn, 1)


def qkv_phase(nc, m, qk, vv):
    with ExitStack() as st:
        xn = m.sb("xn", [P, NC, TPC * D], F32, st)
        xnT = m.sb("xnT", [P, 2, KC, CH], F32, st)
        p_t = m.pb("p_t", [P, KC, CH], F32, st)
        p_qk = m.pb("p_qk", [P, 2 * KC, CH], F32, st)
        p_v = m.pb("p_v", [P, TPC, D], F32, st)
        s_ln, s_pow, s_xn = m.sem("ln_stats", st), m.sem("ln_pow", st), m.sem("xn_ready", st)
        s_tr, s_xnT = m.sem("transposed", st), m.sem("xnT_ready", st)
        s_mm, s_hi, s_lo = m.sem("projected", st), m.sem("high_ready", st), m.sem("low_ready", st)
        NOUT = 2 * KC + 1
        with nc.Block() as block:
            @block.sync
            def _(sp):
                sp.wait_ge(m.s_later, 16 * m.LATER)

            @block.vector
            def _(v):
                def low(c):
                    for k in range(2 * KC):
                        v.wait_ge(s_hi, c * NOUT + k + 1)
                        v.scalar_tensor_tensor(out=qk[1][:, k, c * CH:(c + 1) * CH], in0=p_qk[:, k, :],
                                               scalar=m.b_qk[:, k:k + 1], in1=qk[0][:, k, c * CH:(c + 1) * CH],
                                               op0=ALU.add, op1=ALU.subtract).then_inc(s_lo, 1)
                    v.wait_ge(s_hi, (c + 1) * NOUT)
                    v.tensor_tensor(vv[1][:, c * TPC * D:(c + 1) * TPC * D], p_v[:].rearrange("p a d -> p (a d)"),
                                    vv[0][:, c * TPC * D:(c + 1) * TPC * D], ALU.subtract).then_inc(s_lo, 1)

                def rows(c):
                    v.wait_ge(s_pow, c + 1)
                    layernorm_rows(v, m, s_xn, xn[:, c], c)

                for c in range(NC):
                    v.wait_ge(m.s_x[c], 16)
                    layernorm_stats(v, m, s_ln, c)
                    if c:
                        rows(c - 1)
                rows(NC - 1)
                v.wait_ge(m.s_w, 16 * m.EARLY)
                for c in range(NC):
                    low(c)

            @block.gpsimd
            def _(g):
                layernorm_power(g, m, s_ln, s_pow)

            @block.scalar
            def _(a):
                def copy_xnT(c):
                    a.wait_ge(s_tr, c + 1)
                    if c >= 2:
                        a.wait_ge(s_mm, (c - 1) * NOUT)
                    a.copy(xnT[:, c % 2], p_t[:]).then_inc(s_xnT, 1)

                copy_xnT(0)
                a.wait_ge(m.s_w, 16 * m.EARLY)
                for c in range(NC):
                    for k in range(2 * KC):
                        a.wait_ge(s_mm, c * NOUT + k + 1)
                        a.activation(qk[0][:, k, c * CH:(c + 1) * CH], p_qk[:, k, :], ACT.Identity,
                                     bias=m.b_qk[:, k:k + 1]).then_inc(s_hi, 1)
                    if c + 1 < NC:
                        copy_xnT(c + 1)
                    a.wait_ge(s_mm, (c + 1) * NOUT)
                    a.copy(vv[0][:, c * TPC * D:(c + 1) * TPC * D],
                           p_v[:].rearrange("p a d -> p (a d)")).then_inc(s_hi, 1)

            @block.tensor
            def _(pe):
                def transposes(c):
                    pe.wait_ge(s_xn, (c + 1) * TPC)
                    if c:
                        pe.wait_ge(s_xnT, c)
                    for k in range(KC):
                        for j in range(TPC):
                            last = pe.transpose(p_t[:, k, j * P:(j + 1) * P],
                                                xn[:, c, j * D + k * P:j * D + (k + 1) * P], m.ident[:])
                    last.then_inc(s_tr, 1)

                transposes(0)
                pe.wait_ge(m.s_w, 16 * m.EARLY)
                for c in range(NC):
                    pe.wait_ge(s_xnT, c + 1)
                    for n in range(2 * KC):
                        if c:
                            pe.wait_ge(s_lo, (c - 1) * NOUT + n + 1)
                        for k in range(KC):
                            last = pe.matmul(p_qk[:, n, :], m.w_qkv[:, k, n * P:(n + 1) * P], xnT[:, c % 2, k, :],
                                             start=(k == 0), stop=(k == KC - 1))
                        last.then_inc(s_mm, 1)
                    if c + 1 < NC:
                        transposes(c + 1)
                    if c:
                        pe.wait_ge(s_lo, c * NOUT)
                    for j in range(TPC):
                        pe.matmul(p_v[:, j, :], m.ones_row[:], m.b_rows[:, 0:D], start=True, stop=False)
                        for k in range(KC):
                            last = pe.matmul(p_v[:, j, :], xnT[:, c % 2, k, j * P:(j + 1) * P], m.w_qkv[:, k, 2 * D:],
                                             start=False, stop=(k == KC - 1))
                    last.then_inc(s_mm, 1)

def self_attention_phase(nc, m, qk, vv):
    with ExitStack() as st:
        p32 = m.sb("p32", [P, T], F32, st)
        pp = [m.sb(f"pp{r}", [P, T], BF16, st) for r in range(2)]
        ppT = m.sb("ppT", [P, NC, 2, TPC * P], BF16, st)
        ctx_n = m.sb("ctx_n", [P, D], F32, st)
        ctxT = m.sb("ctxT", [P, KC, P], F32, st)
        mx4 = m.sb("mx4", [P, NC], F32, st)
        mx1 = m.sb("mx1", [P, 1], F32, st)
        neg_max = m.sb("neg_max", [P, 1], F32, st)
        sums = m.sb("sums", [P, NC], F32, st)
        sum1 = m.sb("sum1", [P, 1], F32, st)
        rsum = m.sb("rsum", [P, 1], F32, st)
        w32 = m.sb("w32", [P, 2, 2 * KC * F // 2], F32, st)
        zeros = m.sb("zeros", [P, KC * F], F32, st)
        whl = m.sb("whl", [P, 2, 2, KC * F], BF16, st)
        p_s = m.pb("p_s", [P, NC, CH], F32, st)
        p_t = m.pb("p_pt", [P, 2, 2 * TPC * P], BF16, st)
        p_o = m.pb("p_o", [P, D], F32, st)
        p_y = m.pb("p_y", [P, 2, D], F32, st)
        s_s, s_max, s_exp = m.sem("scores", st), m.sem("max_ready", st), m.sem("exp_done", st)
        s_split, s_tr, s_pt = m.sem("split", st), m.sem("p_transposed", st), m.sem("pT_ready", st)
        s_pv, s_ctx, s_ct = m.sem("pv_done", st), m.sem("ctx_ready", st), m.sem("ctx_transposed", st)
        s_ctT, s_y, s_add = m.sem("ctxT_ready", st), m.sem("y_ready", st), m.sem("added", st)
        s_v = m.sem("dve_chain", st)
        NV = 10
        s_wl = [m.sem(f"weights_in{r}", st) for r in range(2)]
        s_wh, s_wlo = m.sem("weights_high", st), m.sem("weights_low", st)
        s_ws = [m.sem(f"weights_stored{r}", st) for r in range(2)]
        s_zero, s_zs = m.sem("zeroed", st), m.sem("slots_zeroed", st)
        NW = KC * F
        SCALE = 1.0 / 16.0
        assert SCALE * SCALE * D == 1.0

        with nc.Block() as block:
            @block.tensor
            def _(pe):
                def scores(i):
                    for c in range(NC):
                        pe.wait_ge(s_exp, i * NC + c + 1)
                        n = 0
                        for a, b in PASSES:
                            for k in range(KC):
                                last = pe.matmul(p_s[:, c, :], qk[a][:, k, ds(i * P, P)],
                                                 qk[b][:, KC + k, c * CH:(c + 1) * CH],
                                                 start=(n == 0), stop=(n == 3 * KC - 1))
                                n += 1
                        last.then_inc(s_s, 1)

                def transposes(i, g):
                    pe.wait_ge(s_split, NC + i * NC + g + 1)
                    pe.wait_ge(s_pt, i * NC + g + 1)
                    for r in range(2):
                        for b in range(TPC):
                            last = pe.transpose(p_t[:, g % 2, (r * TPC + b) * P:(r * TPC + b + 1) * P],
                                                pp[r][:, g * CH + b * P:g * CH + (b + 1) * P], m.identb[:])
                    last.then_inc(s_tr, 1)

                def values(i, g):
                    pe.wait_ge(s_pt, 2 + i * NC + g + 1)
                    if g == 0:
                        pe.wait_ge(s_ctx, i + 1)
                    for b in range(TPC):
                        kt = g * TPC + b
                        for n, (a, w) in enumerate(PASSES):
                            last = pe.matmul(p_o[:], ppT[:, g, a, b * P:(b + 1) * P],
                                             vv[w][:, kt * D:(kt + 1) * D],
                                             start=(kt == 0 and n == 0), stop=(kt == NT - 1 and n == 2))
                    last.then_inc(s_pv, 1)

                def weigh(i):
                    transposes(i, 0)
                    for g in range(NC):
                        if g + 1 < NC:
                            transposes(i, g + 1)
                        values(i, g)

                def context_T(i):
                    pe.wait_ge(s_ctx, 1 + i + 1)
                    pe.wait_ge(s_add, i + 1)
                    for k in range(KC):
                        last = pe.transpose(p_y[:, 0, k * P:(k + 1) * P], ctx_n[:, k * P:(k + 1) * P], m.ident[:])
                    last.then_inc(s_ct, 1)

                def project(i):
                    pe.wait_ge(s_ctT, i + 1)
                    pe.matmul(p_y[:, 1, :], m.ones_row[:], m.b_rows[:, D:2 * D], start=True, stop=False)
                    for k in range(KC):
                        last = pe.matmul(p_y[:, 1, :], ctxT[:, k, :], m.w_out[:, k, :],
                                         start=False, stop=(k == KC - 1))
                    last.then_inc(s_y, 1)

                scores(0)
                scores(1)
                weigh(0)
                with pe.Fori(2, NT) as i:
                    scores(i)
                    context_T(i - 2)
                    weigh(i - 1)
                    project(i - 2)
                context_T(NT - 2)
                weigh(NT - 1)
                project(NT - 2)
                context_T(NT - 1)
                project(NT - 1)

            @block.vector
            def _(v):
                v.sem_inc(s_split, NC)
                v.sem_inc(s_ctx, 1)
                v.sem_inc(s_add, 1)

                def maxima(i):
                    for c in range(NC):
                        v.wait_ge(s_s, i * NC + c + 1)
                        v.reduce_max(mx4[:, c:c + 1], p_s[:, c, :], AX_X).then_inc(s_v, 1)
                    v.wait_ge(s_v, i * NV + NC)
                    v.reduce_max(mx1[:], mx4[:], AX_X).then_inc(s_v, 1)
                    v.wait_ge(s_v, i * NV + NC + 1)
                    v.tensor_scalar(neg_max[:], mx1[:], -SCALE, None, ALU.mult).then_inc(s_max, 1)

                def split(i):
                    for g in range(NC):
                        cols = slice(g * CH, (g + 1) * CH)
                        v.wait_ge(s_exp, NC + i * NC + g + 1)
                        v.wait_ge(s_tr, i * NC + g + 1)
                        v.tensor_copy(pp[0][:, cols], p32[:, cols]).then_inc(s_v, 1)
                        v.wait_ge(s_v, i * NV + NC + 2 + g)
                        v.tensor_tensor(pp[1][:, cols], p32[:, cols], pp[0][:, cols], ALU.subtract).then_inc(s_split, 1)

                def normalise(i):
                    v.wait_ge(s_pv, NC + i * NC + NC)
                    v.wait_ge(s_ct, i + 1)
                    v.tensor_scalar(ctx_n[:], p_o[:], rsum[:], None, ALU.mult).then_inc(s_ctx, 1)

                def row_sums(i):
                    v.reduce_sum(sum1[:], sums[:], AX_X).then_inc(s_v, 1)
                    v.wait_ge(s_v, i * NV + NV)
                    v.reciprocal(rsum[:], sum1[:]).then_inc(s_rs, 1)

                def add(i):
                    v.wait_ge(s_y, 1 + i + 1)
                    xs = m.x_res[:, ds(i * D, D)]
                    v.tensor_tensor(xs, p_y[:, 1, :], xs, ALU.add).then_inc(s_add, 1)

                s_rs = m.sem("row_sums", st)
                maxima(0)
                split(0)
                row_sums(0)
                maxima(1)
                split(1)
                v.wait_ge(s_rs, 1)
                normalise(0)
                v.wait_ge(s_ctx, 2)
                row_sums(1)
                with v.Fori(2, NT) as i:
                    maxima(i)
                    split(i)
                    v.wait_ge(s_rs, i)
                    normalise(i - 1)
                    v.wait_ge(s_ctx, i + 1)
                    row_sums(i)
                    add(i - 2)
                v.wait_ge(s_rs, NT)
                normalise(NT - 1)
                add(NT - 2)
                add(NT - 1)

            @block.scalar
            def _(a):
                a.sem_inc(s_exp, NC)
                a.sem_inc(s_pt, 2)

                def exps(i, c):
                    if c == 0:
                        a.wait_ge(s_max, i + 1)
                    a.wait_ge(s_split, i * NC + c + 1)
                    a.activation(p32[:, c * CH:(c + 1) * CH], p_s[:, c, :], ACT.Exp, bias=neg_max[:],
                                 scale=SCALE, accum_out=sums[:, c:c + 1]).then_inc(s_exp, 1)

                def copy_pT(i, g):
                    a.wait_ge(s_tr, NC + i * NC + g + 1)
                    a.wait_ge(s_pv, i * NC + g + 1)
                    a.copy(ppT[:, g].rearrange("p r n -> p (r n)"), p_t[:, g % 2, :]).then_inc(s_pt, 1)

                def copy_ctxT(i):
                    a.wait_ge(s_ct, 1 + i + 1)
                    a.wait_ge(s_y, i + 1)
                    a.copy(ctxT[:].rearrange("p k n -> p (k n)"), p_y[:, 0, :]).then_inc(s_ctT, 1)

                def mixed(i):
                    copy_pT(i - 1, 0)
                    copy_pT(i - 1, 1)
                    exps(i, 0)
                    copy_pT(i - 1, 2)
                    exps(i, 1)
                    copy_pT(i - 1, 3)
                    exps(i, 2)
                    exps(i, 3)

                for c in range(NC):
                    exps(0, c)
                mixed(1)
                with a.Fori(2, NT) as i:
                    copy_ctxT(i - 2)
                    mixed(i)
                copy_ctxT(NT - 2)
                for g in range(NC):
                    copy_pT(NT - 1, g)
                copy_ctxT(NT - 1)

            @block.gpsimd
            def _(g):
                for s, n in ((s_tr, NC), (s_pv, NC), (s_ct, 1), (s_y, 1)):
                    g.sem_inc(s, n)

                g.memset(zeros[:], 0.0).then_inc(s_zero, 1)
                g.wait_ge(s_zero, 1)

                def split_weights(e, r):
                    g.wait_ge(s_wl[r], (e + 1) * 16)
                    g.wait_ge(s_ws[r], (e + 1) * 16)
                    g.tensor_tensor(whl[:, r, 0, :], w32[:, r, :], zeros[:], ALU.add).then_inc(s_wh, 1)
                    g.wait_ge(s_wh, 2 * e + r + 1)
                    g.tensor_tensor(whl[:, r, 1, :], w32[:, r, :], whl[:, r, 0, :], ALU.subtract).then_inc(s_wlo, 1)

                with g.Fori(0, E + 1) as e:
                    split_weights(e, 0)
                    split_weights(e, 1)

            @block.sync
            def _(sp):
                def load(r, src):
                    sp.dma_start(w32[:, r, :].rearrange("p (k n) -> p k n", k=src.shape[0] // P),
                                 src.rearrange("(k p) n -> p k n", p=P)).then_inc(s_wl[r], 16)

                def store(e, r):
                    sp.wait_ge(s_wlo, 2 * e + r + 1)
                    sp.dma_start(m.w_img[ds(e, 1), :, r * 2 * NW:(r + 1) * 2 * NW].rearrange("e p n -> (e p) n"),
                                 whl[:, r].rearrange("p h n -> p (h n)")).then_inc(s_ws[r], 16)

                sp.wait_ge(s_zero, 1)
                zv = zeros[:, 0:RB // P * D].bitcast(BF16).rearrange("p (a n) -> p a n", n=2 * D)
                for b in range(ROUTED):
                    sp.dma_start(m.x_slots[b * RB:(b + 1) * RB, :].rearrange("(a p) n -> p a n", p=P), zv).then_inc(s_zs, 16)
                sp.sem_inc(s_ws[0], 16)
                sp.sem_inc(s_ws[1], 16)
                load(0, m.routed_up[0])
                load(1, m.routed_down[0])
                with sp.Fori(0, E - 1) as e:
                    store(e, 0)
                    load(0, m.routed_up[ds(e + 1, 1)].rearrange("e k n -> (e k) n"))
                    store(e, 1)
                    load(1, m.routed_down[ds(e + 1, 1)].rearrange("e k n -> (e k) n"))
                store(E - 1, 0)
                load(0, m.shared_up[0])
                store(E - 1, 1)
                load(1, m.shared_down[0])
                store(E, 0)
                store(E, 1)
                sp.wait_ge(s_zs, 16 * ROUTED)
                sp.wait_ge(s_ws[0], 16 * (E + 2))
                sp.wait_ge(s_ws[1], 16 * (E + 2))


def cross_projection_phase(nc, m, v2):
    with ExitStack() as st:
        xn = m.sb("xn2", [P, NC, TPC * D], F32, st)
        ctx_sb = m.sb("ctx_sb", [P, NC, TPC * D], F32, st)
        rT = m.sb("rT2", [P, 2, KC, CH], F32, st)
        parts = m.sb("parts", [P, 2, 3, KC, CH], BF16, st)
        rest = m.sb("rest", [P, 2, KC, CH], F32, st)
        p_t = m.pb("p_t2", [P, KC, CH], F32, st)
        p_m = m.pb("p_m2", [P, 2, KC, CH], F32, st)
        p_v = m.pb("p_v2", [P, TPC, D], F32, st)
        s_ln, s_pow, s_xn = m.sem("ln2_stats", st), m.sem("ln2_pow", st), m.sem("xn2_ready", st)
        s_z, s_one = m.sem("ctx_zeroed", st), m.sem("ones_set", st)
        s_cx = [m.sem(f"ctx_in{c}", st) for c in range(NC)]
        s_tr, s_rT = m.sem("transposed2", st), m.sem("rT2_ready", st)
        s_mm, s_p0, s_r1 = m.sem("projected2", st), m.sem("part0", st), m.sem("rest1", st)
        s_p1, s_p2 = m.sem("part1", st), m.sem("part2", st)
        s_st = [m.sem(f"parts_stored{r}", st) for r in range(2)]
        s_vm, s_vd = m.sem("values_done", st), m.sem("values_copied", st)
        q_dst = m.q2_parts.rearrange("r (m h) k t -> (h k) (r m) t", m=KC)
        k_dst = m.k2_parts.rearrange("r (m h) k t -> (h k) (r m) t", m=KC)
        WHOLE = S_CTX - CTX_LAST
        with nc.Block() as block:
            @block.sync
            def _(sp):
                for c in range(NC - 1):
                    sp.dma_start(ctx_sb[:, c].rearrange("p (t d) -> p t d", d=D),
                                 m.ctx_in[0, c * CH:(c + 1) * CH].rearrange("(t p) d -> p t d", p=P)).then_inc(s_cx[c], 16)
                sp.wait_ge(s_z, 1)
                sp.dma_start(ctx_sb[0:CTX_LAST, NC - 1, 0:D], m.ctx_in[0, WHOLE:S_CTX, :]).then_inc(s_cx[NC - 1], 16)
                for n in range(2 * NC):
                    dst, c = (k_dst, n) if n < NC else (q_dst, n - NC)
                    sp.wait_ge(s_p2, (n + 1) * KC)
                    sp.dma_start(dst[:, :, c * CH:(c + 1) * CH],
                                 parts[:, n % 2].rearrange("p r m t -> p (r m) t")).then_inc(s_st[n % 2], 16)
                for r in range(2):
                    sp.wait_ge(s_st[r], 16 * NC)

            @block.gpsimd
            def _(g):
                assert (NC - 1) * TPC == NTC - 1
                g.memset(ctx_sb[:, NC - 1], 0.0).then_inc(s_z, 1)
                layernorm_power(g, m, s_ln, s_pow)

            @block.scalar
            def _(a):
                def copy_rT(n):
                    a.wait_ge(s_tr, n + 1)
                    if n >= 2:
                        a.wait_ge(s_mm, (n - 1) * KC)
                        a.wait_ge(s_vm, min(n - 1, NC))
                    a.copy(rT[:, n % 2], p_t[:]).then_inc(s_rT, 1)

                copy_rT(0)
                for n in range(2 * NC):
                    for k in range(KC):
                        if n >= 2:
                            a.wait_ge(s_st[n % 2], 16 * (n // 2))
                        a.wait_ge(s_mm, n * KC + k + 1)
                        a.copy(parts[:, n % 2, 0, k, :], p_m[:, n % 2, k, :]).then_inc(s_p0, 1)
                    if n + 1 < 2 * NC:
                        copy_rT(n + 1)
                    if n < NC:
                        a.wait_ge(s_vm, n + 1)
                        a.copy(v2[:, n * TPC:(n + 1) * TPC, :, 0:DK],
                               p_v[:].rearrange("p a (h k) -> p a h k", k=DK)).then_inc(s_vd, 1)

            @block.vector
            def _(v):
                def lower_parts(n):
                    r = n % 2
                    for k in range(KC):
                        v.wait_ge(s_p0, n * KC + k + 1)
                        v.tensor_tensor(rest[:, r, k, :], p_m[:, r, k, :], parts[:, r, 0, k, :],
                                        ALU.subtract).then_inc(s_r1, 1)
                        v.wait_ge(s_r1, n * KC + k + 1)
                        v.tensor_copy(parts[:, r, 1, k, :], rest[:, r, k, :]).then_inc(s_p1, 1)
                        v.wait_ge(s_p1, n * KC + k + 1)
                        v.tensor_tensor(parts[:, r, 2, k, :], rest[:, r, k, :], parts[:, r, 1, k, :],
                                        ALU.subtract).then_inc(s_p2, 1)

                v.memset(v2[:, :, :, DK:DK + 1], 1.0).then_inc(s_one, 1)
                layernorm_stats(v, m, s_ln, 0)
                for c in range(NC):
                    if c + 1 < NC:
                        layernorm_stats(v, m, s_ln, c + 1)
                    v.wait_ge(s_pow, c + 1)
                    layernorm_rows(v, m, s_xn, xn[:, c], c)
                    lower_parts(c)
                for c in range(NC):
                    lower_parts(NC + c)

            @block.tensor
            def _(pe):
                def transposes(n):
                    if n < NC:
                        pe.wait_ge(s_cx[n], 16)
                        if n == NC - 1:
                            pe.wait_ge(s_z, 1)
                    else:
                        pe.wait_ge(s_xn, (n - NC + 1) * TPC)
                    if n:
                        pe.wait_ge(s_rT, n)
                    src = ctx_sb if n < NC else xn
                    for k in range(KC):
                        for j in range(TPC):
                            last = pe.transpose(p_t[:, k, j * P:(j + 1) * P],
                                                src[:, n % NC, j * D + k * P:j * D + (k + 1) * P], m.ident[:])
                    last.then_inc(s_tr, 1)

                transposes(0)
                for n in range(2 * NC):
                    pe.wait_ge(s_rT, n + 1)
                    for o in range(KC):
                        if n >= 2:
                            pe.wait_ge(s_r1, (n - 2) * KC + o + 1)
                        for k in range(KC):
                            last = pe.matmul(p_m[:, n % 2, o, :], m.w_x[:, 1 if n < NC else 0, k, o * P:(o + 1) * P],
                                             rT[:, n % 2, k, :], start=(k == 0), stop=(k == KC - 1))
                        last.then_inc(s_mm, 1)
                    if n + 1 < 2 * NC:
                        transposes(n + 1)
                    if n < NC:
                        if n:
                            pe.wait_ge(s_vd, n)
                        for j in range(TPC):
                            for k in range(KC):
                                last = pe.matmul(p_v[:, j, :], rT[:, n % 2, k, j * P:(j + 1) * P], m.w_x[:, 2, k, :],
                                                 start=(k == 0), stop=(k == KC - 1))
                        last.then_inc(s_vm, 1)

def cross_attention_phase(nc, m, v2, ctx2):
    KT = NTC * P
    PRING, RING = 4, 3
    entries, ranges = cross_schedule()
    index = {x: n for n, x in enumerate(entries)}
    steps = [(n, n // NSTEP, n % NSTEP, *STEPS[n % NSTEP]) for n in range(NG * NSTEP)]
    keys = [min(P, S_CTX - j * P) for j in range(NTC)]
    diagonal = [n for n, _, s, *_ in steps if s in DIAG]
    last_step = [n for n, _, s, *_ in steps if s in LAST_OF.values()]

    with ExitStack() as st:
        qs = m.sb("qs", [STACK + 2, 2, GH * T], BF16, st)
        ks = m.sb("ks", [STACK + 2, 2, GH * KT], BF16, st)
        pw = m.sb("pw", [P, PRING, GH, CH], F32, st)
        vg = m.sb("vg", [P, 2, NTC, GH, 32], F32, st)
        oT = m.sb("oT", [P, CH], F32, st)
        mask = m.sb("mask", [P, P], BF16, st)
        mx_part = m.sb("mx_part", [P, GH * TPC, NC], F32, st)
        mx = m.sb("mx", [P, GH * TPC], F32, st)
        neg = m.sb("neg", [GH * TPC, 2, 2, P], BF16, st)
        rden = m.sb("rden", [P, 2, TPC, GH, 1], F32, st)
        p_st = m.pb("p_st", [P, 2, 2, CH], F32, st)
        p_ring = m.pb("p_ring", [P, RING, CH], F32, st)
        p_acc = m.pb("p_acc", [P, CH], F32, st)
        s_zero, s_set = m.sem("mask_zeroed", st), m.sem("masks_set", st)
        s_stack = [m.sem(f"stacks_in{r}", st) for r in range(2)]
        s_ns = [m.sem(f"neg_stored{r}", st) for r in range(2)]
        s_rows = [m.sem(f"neg_rows_in{r}", st) for r in range(2)]
        s_st, s_exp, s_mask = m.sem("st_scores", st), m.sem("weights_ready", st), m.sem("masked", st)
        s_pv, s_acc, s_vg = m.sem("xpv_done", st), m.sem("acc_copied", st), m.sem("values_staged", st)
        s_entry, s_taken = m.sem("entry_ready", st), m.sem("entry_taken", st)
        s_mx, s_nh, s_rd = m.sem("chunk_max", st), m.sem("neg_high", st), m.sem("rden_ready", st)

        with nc.Block() as block:
            @block.tensor
            def _(pe):
                def transposed_scores(n, pair):
                    _, g, s, c, j, off = steps[n]
                    if pair == 0 and s in FIRST_OF.values():
                        rho = g * NC + c
                        pe.wait_ge(s_rows[rho % 2], 16 * (rho // 2 + 1))
                    if n >= 1:
                        pe.wait_ge(s_exp, 2 * n + pair - 1)
                    for h in (0, 1):
                        hh = 2 * pair + h
                        last = pe.matmul(p_st[0:keys[j], pair, h, off:CH],
                                         ks[:, g % 2, hh * KT + j * P:hh * KT + j * P + keys[j]],
                                         qs[:, g % 2, hh * T + c * CH + off:hh * T + (c + 1) * CH],
                                         start=True, stop=True)
                    last.then_inc(s_st, 1)

                def values(n):
                    _, g, s, c, j, off = steps[n]
                    if s == 0:
                        pe.wait_ge(s_vg, g + 1)
                    if j == 0 and n:
                        pe.wait_ge(s_acc, g * NC + c)
                    if n in diagonal:
                        pe.wait_ge(s_mask, diagonal.index(n) + 1)
                    else:
                        pe.wait_ge(s_exp, 2 * n + 2)
                    for hh in range(GH):
                        last = pe.matmul(p_acc[32 * hh:32 * hh + 32, off:CH], vg[0:keys[j], g % 2, j, hh, :],
                                         pw[0:keys[j], n % PRING, hh, off:CH], start=(j == 0), stop=(n in last_step))
                    last.then_inc(s_pv, 1)

                def unit(bank, g, c, u):
                    i, h, k0, w = UNITS[c][u]
                    if c == 0 and u == 0:
                        pe.wait_ge(s_stack[g % 2], 16 * 2 * len(Q_PARTS) * (g // 2 + 1))
                    diag = k0 <= i * P < k0 + w
                    last = pe.matmul(bank[:, 0:w], qs[0:STACK, g % 2, h * T + i * P:h * T + (i + 1) * P],
                                     ks[0:STACK, g % 2, h * KT + k0:h * KT + k0 + w], start=True, stop=not diag)
                    if diag:
                        last = pe.matmul(bank[:, i * P - k0:w], m.identb[:], mask[:, 0:w - (i * P - k0)],
                                         start=False, stop=True)
                    return last

                def ring(n, place):
                    for e in range(*ranges[n, place]):
                        kind, *what = entries[e]
                        bank = p_ring[:, e % RING, :]
                        if e >= RING:
                            pe.wait_ge(s_taken, e - RING + 1)
                        if kind == "unit":
                            last = unit(bank, *what)
                        elif kind == "row":
                            pe.wait_ge(s_mx, what[0] + 1)
                            last = pe.transpose(bank[0:GH * TPC, 0:P], mx[:], m.ident[:])
                        else:
                            pe.wait_ge(s_acc, what[0] + 1)
                            for a in range(TPC):
                                last = pe.transpose(bank[:, a * P:(a + 1) * P], oT[:, a * P:(a + 1) * P], m.ident[:])
                        last.then_inc(s_entry, 1)

                pe.wait_ge(s_set, 3)
                for place in range(3):
                    ring(-1, place)
                for n in range(NG * NSTEP + 2):
                    for pair in range(2):
                        if n < NG * NSTEP:
                            transposed_scores(n, pair)
                        ring(n, pair)
                    if 1 <= n <= NG * NSTEP:
                        values(n - 1)
                    ring(n, 2)

            @block.scalar
            def _(a):
                def stage_values(g):
                    if g >= 2:
                        a.wait_ge(s_pv, (g - 1) * NSTEP)
                    a.copy(vg[:, g % 2, :, :, 0:DK + 1], v2[:, 0:NTC, g * GH:(g + 1) * GH, :]).then_inc(s_vg, 1)

                a.wait_ge(s_set, 3)
                stage_values(0)
                for n, g, s, c, j, off in steps:
                    if n >= PRING:
                        a.wait_ge(s_pv, n - PRING + 1)
                    for pair in range(2):
                        a.wait_ge(s_st, 2 * n + pair + 1)
                        a.activation(pw[0:keys[j], n % PRING, 2 * pair:2 * pair + 2, off:CH],
                                     p_st[0:keys[j], pair, :, off:CH], ACT.Exp, scale=1.0 / 4.0).then_inc(s_exp, 1)
                    if s == NSTEP // 2 and g + 1 < NG:
                        stage_values(g + 1)
                    if n - 1 in last_step or n == NG * NSTEP - 1:
                        done = [x for x in (n - 1, n) if x in last_step and (x < n or n == NG * NSTEP - 1)]
                        for x in done:
                            rho = last_step.index(x)
                            a.wait_ge(s_pv, x + 1)
                            if rho:
                                a.wait_ge(s_entry, index["out", rho - 1] + 1)
                            a.copy(oT[:], p_acc[:]).then_inc(s_acc, 1)

            @block.gpsimd
            def _(g):
                g.memset(mask[:], 0.0).then_inc(s_zero, 1)
                g.wait_ge(s_zero, 1)
                g.affine_select(out=mask[:], in_=mask[:], compare_op=ALU.is_ge, fill=NEG, base=0,
                                pattern=[[-1, P]], channel_multiplier=1).then_inc(s_set, 1)
                g.memset(vg[:], 0.0).then_inc(s_set, 1)
                for n in diagonal:
                    _, _, _, c, j, off = steps[n]
                    blk = pw[0:keys[j], n % PRING, :, off:off + P]
                    g.wait_ge(s_exp, 2 * n + 2)
                    g.affine_select(out=blk, in_=blk, compare_op=ALU.is_ge, fill=0.0, base=0,
                                    pattern=[[0, GH], [1, P]], channel_multiplier=-1).then_inc(s_mask, 1)

            @block.vector
            def _(v):
                v.memset(ks[STACK:STACK + 2], 1.0).then_inc(s_set, 1)
                for e, (kind, *what) in enumerate(entries):
                    bank = p_ring[:, e % RING, :]
                    v.wait_ge(s_entry, e + 1)
                    if kind == "unit":
                        g, c, u = what
                        i, h, k0, w = UNITS[c][u]
                        if u == 0 and g + c:
                            v.wait_ge(s_mx, g * NC + c)
                        v.reduce_max(mx_part[:, h * TPC + i % TPC, k0 // CH:k0 // CH + 1], bank[:, 0:w],
                                     AX_X).then_inc(s_taken, 1)
                        if u == len(UNITS[c]) - 1:
                            v.wait_ge(s_taken, e + 1)
                            v.reduce_max(mx[:], mx_part[:, :, 0:c + 1], AX_X).then_inc(s_mx, 1)
                    elif kind == "row":
                        rho = what[0]
                        if rho >= 2:
                            v.wait_ge(s_ns[rho % 2], 16 * (rho // 2))
                        v.tensor_scalar(neg[:, rho % 2, 0, :], bank[0:GH * TPC, 0:P], -1.0, None,
                                        ALU.mult).then_inc(s_nh, 1)
                        v.wait_ge(s_nh, rho + 1)
                        v.scalar_tensor_tensor(out=neg[:, rho % 2, 1, :], in0=bank[0:GH * TPC, 0:P], scalar=-1.0,
                                               in1=neg[:, rho % 2, 0, :], op0=ALU.mult,
                                               op1=ALU.subtract).then_inc(s_taken, 1)
                    else:
                        g, c = divmod(what[0], NC)
                        po = bank.rearrange("p (a h w) -> p a h w", a=TPC, w=32)
                        par = what[0] % 2
                        v.reciprocal(rden[:, par], po[:, :, :, DK:DK + 1]).then_inc(s_rd, 1)
                        v.wait_ge(s_rd, what[0] + 1)
                        v.tensor_tensor(ctx2[:, c * TPC:(c + 1) * TPC, g * GH * DK:(g + 1) * GH * DK]
                                        .rearrange("p a (h k) -> p a h k", k=DK),
                                        po[:, :, :, 0:DK], rden[:, par].to_broadcast([P, TPC, GH, DK]),
                                        ALU.mult).then_inc(s_taken, 1)

            @block.sync
            def _(sp):
                def stacks(g):
                    for dst, src, parts, w in ((qs, m.q2_parts, Q_PARTS, T), (ks, m.k2_parts, K_PARTS, KT)):
                        for r, part in enumerate(parts):
                            sp.dma_start(dst[r * DK:(r + 1) * DK, g % 2, :].rearrange("k (h t) -> k h t", h=GH),
                                         src[part, g * GH:(g + 1) * GH, :, 0:w].rearrange("h k t -> k h t")
                                         ).then_inc(s_stack[g % 2], 16)

                def rows(rho):
                    g, c = divmod(rho, NC)
                    par = rho % 2
                    sp.wait_ge(s_taken, index["row", rho] + 1)
                    sp.dma_start(m.neg_rows[rho].rearrange("r a q -> a r q"), neg[:, par]).then_inc(s_ns[par], 16)
                    sp.wait_ge(s_ns[par], 16 * (rho // 2 + 1))
                    if rho >= 2:
                        sp.wait_ge(s_rows[par], 16 * (rho // 2))
                    sp.dma_start(qs[STACK:STACK + 2, g % 2, :].rearrange("r (h t) -> r h t", h=GH)
                                 [:, :, c * CH:(c + 1) * CH],
                                 m.neg_rows[rho].rearrange("r (h a) q -> r h (a q)", h=GH)).then_inc(s_rows[par], 16)

                stacks(0)
                stacks(1)
                row_at = {x[1]: n for (n, place), (a, b) in ranges.items() for x in entries[a:b] if x[0] == "row"}
                events = [(row_at[rho], rows, rho) for rho in range(NG * NC)]
                events += [((g - 1) * NSTEP, stacks, g) for g in range(2, NG)]
                for at, what, n in sorted(events, key=lambda x: (x[0], x[2])):
                    if what is stacks:
                        sp.wait_ge(s_st, 2 * (n - 1) * NSTEP)
                    what(n)


def cross_output_phase(nc, m, ctx2):
    with ExitStack() as st:
        rT = m.sb("rT5", [P, 2, KC, CH], F32, st)
        p_t = m.pb("p_t5", [P, 2, KC, CH], F32, st)
        p_y = m.pb("p_y5", [P, 2, TPC, D], F32, st)
        s_tr, s_rT = m.sem("transposed5", st), m.sem("rT5_ready", st)
        s_y, s_add = m.sem("y5_ready", st), m.sem("added5", st)
        s_ln, s_pow = m.sem("ln3_stats", st), m.sem("ln3_pow", st)
        with nc.Block() as block:
            @block.scalar
            def _(a):
                for c in range(NC):
                    a.wait_ge(s_tr, c + 1)
                    if c >= 2:
                        a.wait_ge(s_y, c - 1)
                    a.copy(rT[:, c % 2], p_t[:, c % 2]).then_inc(s_rT, 1)

            @block.tensor
            def _(pe):
                def transposes(c):
                    if c >= 2:
                        pe.wait_ge(s_rT, c - 1)
                    for k in range(KC):
                        for j in range(TPC):
                            last = pe.transpose(p_t[:, c % 2, k, j * P:(j + 1) * P],
                                                ctx2[:, c * TPC + j, k * P:(k + 1) * P], m.ident[:])
                    last.then_inc(s_tr, 1)

                transposes(0)
                for c in range(NC):
                    if c + 1 < NC:
                        transposes(c + 1)
                    pe.wait_ge(s_rT, c + 1)
                    if c >= 2:
                        pe.wait_ge(s_add, c - 1)
                    for j in range(TPC):
                        for k in range(KC):
                            last = pe.matmul(p_y[:, c % 2, j, :], rT[:, c % 2, k, j * P:(j + 1) * P], m.w_x[:, 3, k, :],
                                             start=(k == 0), stop=(k == KC - 1))
                    last.then_inc(s_y, 1)

            @block.gpsimd
            def _(g):
                layernorm_power(g, m, s_ln, s_pow)

            @block.vector
            def _(v):
                for c in range(NC):
                    xs = m.x_res[:, c * TPC * D:(c + 1) * TPC * D]
                    v.wait_ge(s_y, c + 1)
                    v.tensor_tensor(xs, p_y[:, c % 2].rearrange("p a d -> p (a d)"), xs, ALU.add).then_inc(s_add, 1)
                    v.wait_ge(s_add, c + 1)
                    layernorm_stats(v, m, s_ln, c)
def up_products(pe, p_h, w, w0, xT, half):
    rows = xT.shape[-1] // (2 * KC)
    for f in range(half * NF // 2, (half + 1) * NF // 2):
        n = 0
        for wp, xp in PASSES:
            for k in range(KC):
                last = pe.matmul(p_h[:, f * rows:(f + 1) * rows], w[:, ds(w0 + UP + (wp * KC + k) * F + f * P, P)],
                                 xT[:, (xp * KC + k) * rows:(xp * KC + k + 1) * rows],
                                 start=(n == 0), stop=(n == 3 * KC - 1))
                n += 1
    return last


def down_products(pe, p_y, w, w0, hT, half):
    rows = hT.shape[-1] // NF
    for f in range(half * NF // 2, (half + 1) * NF // 2):
        for n, (wp, hp) in enumerate(PASSES):
            for a in range(rows // P):
                last = pe.matmul(p_y[:, a, 0:D], hT[:, hp, f * rows + a * P:f * rows + (a + 1) * P],
                                 w[:, ds(w0 + DOWN + (wp * NF + f) * D, D)],
                                 start=(f == 0 and n == 0), stop=(f == NF - 1 and n == 2))
    return last


def router_phase(nc, m, w_sb, s_w, xhl, p_lg):
    with ExitStack() as st:
        rows = m.sb("rows6", [P, 2, TPC * D], F32, st)
        rT = m.sb("rT6", [P, KC, CH], F32, st)
        p_t = m.pb("p_t6", [P, 2, KC, CH], F32, st)
        s_xn = m.sem("xn3_ready", st)
        s_tr, s_rT, s_lg = m.sem("transposed6", st), m.sem("rT6_ready", st), m.sem("logits", st)
        s_xh, s_xl, s_res = m.sem("x_high", st), m.sem("x_low", st), m.sem("residual_added", st)
        with nc.Block() as block:
            @block.sync
            def _(sp):
                for e in WEIGHT_ORDER:
                    sp.dma_start(w_sb[:, e, :], m.w_img[e]).then_inc(s_w[e], 16)

            @block.tensor
            def _(pe):
                def transposes(c):
                    pe.wait_ge(s_xn, (c + 1) * TPC)
                    if c >= 2:
                        pe.wait_ge(s_rT, c - 1)
                    for k in range(KC):
                        for j in range(TPC):
                            last = pe.transpose(p_t[:, c % 2, k, j * P:(j + 1) * P],
                                                rows[:, c % 2, j * D + k * P:j * D + (k + 1) * P], m.ident[:])
                    last.then_inc(s_tr, 1)

                transposes(0)
                for c in range(NC):
                    if c + 1 < NC:
                        transposes(c + 1)
                    pe.wait_ge(s_rT, c + 1)
                    for j in range(TPC):
                        for k in range(KC):
                            last = pe.matmul(p_lg[:, c * TPC + j, :], rT[:, k, j * P:(j + 1) * P], m.w_rt[:, k, :],
                                             start=(k == 0), stop=(k == KC - 1))
                    last.then_inc(s_lg, 1)

            @block.scalar
            def _(a):
                for c in range(NC):
                    a.wait_ge(s_tr, c + 1)
                    if c:
                        a.wait_ge(s_lg, c)
                    a.copy(rT[:], p_t[:, c % 2]).then_inc(s_rT, 1)
                    a.wait_ge(s_xn, (c + 1) * TPC)
                    a.copy(xhl[:, c * TPC:(c + 1) * TPC, 0, :],
                           rows[:, c % 2, :].rearrange("p (t d) -> p t d", d=D)).then_inc(s_xh, 1)

            @block.vector
            def _(v):
                for c in range(NC):
                    if c >= 2:
                        v.wait_ge(s_tr, c - 1)
                    layernorm_rows(v, m, s_xn, rows[:, c % 2], c)
                    v.wait_ge(s_xh, c + 1)
                    v.tensor_tensor(xhl[:, c * TPC:(c + 1) * TPC, 1, :],
                                    rows[:, c % 2, :].rearrange("p (t d) -> p t d", d=D),
                                    xhl[:, c * TPC:(c + 1) * TPC, 0, :], ALU.subtract).then_inc(s_xl, 1)
                    xs = m.x_res[:, c * TPC * D:(c + 1) * TPC * D]
                    v.wait_ge(s_xn, (c + 1) * TPC)
                    v.tensor_tensor(xs, xs, rows[:, c % 2, :], ALU.add).then_inc(s_res, 1)


def shared_expert_phase(nc, m, w_sb, s_w, xhl, p_lg, slot_idx, gates, block_expert):
    with ExitStack() as st:
        logit = m.sb("logit", [P, NT, E], F32, st)
        prob = m.sb("prob", [P, NT, E], F32, st)
        top1 = m.sb("top1", [P, NT, 1], F32, st)
        psum_ = m.sb("prob_sum", [P, NT, 1], F32, st)
        best_i = m.sb("best_i", [P, NT, E], U32, st)
        idx_f = m.sb("idx_f", [P, NT, TOPK], F32, st)
        pick = m.sb("pick", [P, TOPK, NT, E], F32, st)
        picked = m.sb("picked", [P, NT + 1, E], BF16, st)
        before = m.sb("before", [P, P], BF16, st)
        onesb = m.sb("onesb", [P, P], BF16, st)
        iota_i = m.sb("iota_i", [P, ROUTED], mybir.dt.int32, st)
        iota = m.sb("iota", [P, ROUTED], F32, st)
        ones8 = m.sb("ones8", [P, E], F32, st)
        cnt = m.sb("cnt", [P, E, 1], F32, st)
        over = m.sb("over", [P, E, T // RB], F32, st)
        nblk = m.sb("nblk", [P, E], F32, st)
        end = m.sb("end", [P, E], F32, st)
        base = m.sb("base", [P, 1, E], F32, st)
        pos = m.sb("pos", [P, NT, E], F32, st)
        posk = m.sb("posk", [P, NT, E], F32, st)
        slot_f = m.sb("slot_f", [P, TOPK, NT], F32, st)
        past = m.sb("past", [P, ROUTED, E], F32, st)
        blk_f = m.sb("blk_f", [P, ROUTED], F32, st)
        xT = m.sb("xT6", [P, 2, 2 * KC * P], BF16, st)
        h32 = m.sb("h32_6", [P, 2, NF * P], F32, st)
        hT = m.sb("hT6", [P, 2, 2, NF * P], BF16, st)
        p_x = m.pb("p_x6", [P, 2 * KC * P], BF16, st)
        p_h = m.pb("p_h6", [P, 2, NF * P], F32, st)
        p_y = m.pb("p_y6", [P, 2, CH], F32, st)
        p_rank = p_lg[:, NT:]
        s_c, s_v, s_sub, s_ex = m.sem("constants", st), m.sem("routing_chain", st), m.sem("logits_shifted", st), m.sem("prob_exp", st)
        s_pick, s_rank, s_slot = m.sem("picked_ready", st), m.sem("ranked", st), m.sem("slots_ready", st)
        s_sc = m.sem("rows_scattered", st)
        s_xt, s_xT, s_up = m.sem("x6_transposed", st), m.sem("xT6_ready", st), m.sem("up6_done", st)
        s_ge, s_hh, s_hl = m.sem("gelu6_done", st), m.sem("h6_high", st), m.sem("h6_low", st)
        s_dn, s_add = m.sem("down6_done", st), m.sem("shared_added", st)
        w = w_sb[:].rearrange("p e n -> p (e n)")
        w0 = E * WCOLS
        with nc.Block() as block:
            @block.gpsimd
            def _(g):
                g.memset(onesb[:], 1.0).then_inc(s_c, 1)
                g.memset(before[:], 1.0).then_inc(s_c, 1)
                g.memset(ones8[:], 1.0).then_inc(s_c, 1)
                g.iota(iota_i[:], pattern=[[1, ROUTED]], base=0, channel_multiplier=0).then_inc(s_c, 1)
                g.wait_ge(s_c, 2)
                g.affine_select(out=before[:], in_=before[:], compare_op=ALU.is_gt, fill=0.0, base=0,
                                pattern=[[1, P]], channel_multiplier=-1).then_inc(s_c, 1)
                g.wait_ge(s_slot, 1)
                for t in range(NT):
                    for k in range(TOPK):
                        g.indirect_dma_start(m.x_slots,
                                             bass.IndirectOffsetOnAxis(ap=slot_idx[:, k * NT + t:k * NT + t + 1], axis=0),
                                             xhl[:, t].rearrange("p r d -> p (r d)"), None).then_inc(s_sc, 16)
                g.wait_ge(s_sc, 16 * NT * TOPK)

            @block.tensor
            def _(pe):
                def transposes(b):
                    if b >= 1:
                        pe.wait_ge(s_xT, b)
                    for n in range(2 * KC):
                        last = pe.transpose(p_x[:, n * P:(n + 1) * P],
                                            xhl[:, b, n // KC, n % KC * P:(n % KC + 1) * P], m.identb[:])
                    last.then_inc(s_xt, 1)

                def ranks():
                    pe.wait_ge(s_c, 5)
                    pe.wait_ge(s_pick, 1)
                    pe.matmul(p_rank, before[:], picked[:], start=True, stop=False)
                    for t in range(NT):
                        last = pe.matmul(p_rank[:, t + 1:, :], onesb[:],
                                         picked[:, t:t + 1, :].to_broadcast([P, NT - t, E]),
                                         start=False, stop=(t == NT - 1))
                    last.then_inc(s_rank, 1)

                pe.wait_ge(s_w[E], 16)
                transposes(0)
                transposes(1)
                for b in range(NT + 1):
                    if b < NT:
                        pe.wait_ge(s_xT, b + 1)
                        if b >= 2:
                            pe.wait_ge(s_ge, 2 * b - 2)
                        for half in range(2):
                            up_products(pe, p_h[:, b % 2], w, w0, xT[:, b % 2], half).then_inc(s_up, 1)
                    if b + 2 < NT:
                        transposes(b + 2)
                    if b == 1:
                        ranks()
                    if b >= 1:
                        if b >= 3:
                            pe.wait_ge(s_add, b - 2)
                        for half in range(2):
                            pe.wait_ge(s_hl, 2 * (b - 1) + half + 1)
                            last = down_products(pe, p_y[:, (b - 1) % 2:(b - 1) % 2 + 1], w, w0, hT[:, (b - 1) % 2], half)
                        last.then_inc(s_dn, 1)

            @block.scalar
            def _(a):
                a.wait_ge(s_sub, 1)
                a.activation(prob[:], logit[:], ACT.Exp).then_inc(s_ex, 1)
                for b in range(NT):
                    for z in range(2):
                        half = slice(z * NF * P // 2, (z + 1) * NF * P // 2)
                        a.wait_ge(s_up, 2 * b + z + 1)
                        if b >= 2:
                            a.wait_ge(s_hl, 2 * b + z - 3)
                        a.activation(h32[:, b % 2, half], p_h[:, b % 2, half], ACT.Gelu).then_inc(s_ge, 1)

            @block.vector
            def _(v):
                n = [0]

                def link(ins):
                    n[0] += 1
                    ins.then_inc(s_v, 1)
                    v.wait_ge(s_v, n[0])

                def choose_experts():
                    v.wait_ge(s_c, 5)
                    link(v.tensor_copy(iota[:], iota_i[:]))
                    link(v.memset(picked[:, NT, :], 0.0))
                    link(v.reduce_max(top1[:], p_lg[:, 0:NT], AX_X))
                    v.tensor_tensor(logit[:], p_lg[:, 0:NT], top1[:].to_broadcast([P, NT, E]), ALU.subtract).then_inc(s_sub, 1)
                    v.wait_ge(s_ex, 1)
                    link(v.reduce_sum(psum_[:], prob[:], AX_X))
                    link(v.reciprocal(top1[:], psum_[:]))
                    link(v.tensor_tensor(prob[:], prob[:], top1[:].to_broadcast([P, NT, E]), ALU.mult))
                    for t in range(NT):
                        v.max(gates[:, t, :], prob[:, t, :]).then_inc(s_v, 1)
                    n[0] += NT
                    for t in range(NT):
                        v.wait_ge(s_v, n[0] - NT + t + 1)
                        v.max_index(best_i[:, t, :], gates[:, t, :], prob[:, t, :]).then_inc(s_v, 1)
                    n[0] += NT
                    v.wait_ge(s_v, n[0])
                    link(v.tensor_copy(idx_f[:], best_i[:, :, 0:TOPK]))
                    for k in range(TOPK):
                        link(v.tensor_tensor(pick[:, k], iota[:, None, 0:E].to_broadcast([P, NT, E]),
                                             idx_f[:, :, k:k + 1].to_broadcast([P, NT, E]), ALU.is_equal))
                    v.tensor_tensor(picked[:, 0:NT, :], pick[:, 0], pick[:, 1], ALU.add).then_inc(s_pick, 1)

                def assign_slots():
                    v.wait_ge(s_rank, 1)
                    link(v.tensor_copy(cnt[:, :, 0], p_rank[:, NT, :]))
                    link(v.tensor_scalar(blk_f[:, 0:T // RB], iota[:, 0:T // RB], float(RB), None, ALU.mult))
                    link(v.tensor_tensor(over[:], cnt[:].to_broadcast([P, E, T // RB]),
                                         blk_f[:, None, 0:T // RB].to_broadcast([P, E, T // RB]), ALU.is_gt))
                    link(v.reduce_sum(nblk[:], over[:], AX_X))
                    link(v.tensor_tensor_scan(end[:], ones8[:], nblk[:], 0.0, ALU.mult, ALU.add))
                    link(v.tensor_tensor(base[:, 0, :], end[:], nblk[:], ALU.subtract))
                    link(v.tensor_scalar(base[:], base[:], float(RB), None, ALU.mult))
                    link(v.tensor_tensor(pos[:], p_rank[:, 0:NT, :], base[:].to_broadcast([P, NT, E]), ALU.add))
                    for k in range(TOPK):
                        link(v.tensor_tensor(posk[:], pos[:], pick[:, k], ALU.mult))
                        link(v.reduce_sum(slot_f[:, k, :], posk[:], AX_X))
                    v.tensor_copy(slot_idx[:], slot_f[:].rearrange("p k t -> p (k t)")).then_inc(s_slot, 1)

                def list_blocks():
                    link(v.tensor_tensor(past[:], iota[:, :, None].to_broadcast([P, ROUTED, E]),
                                         end[:, None, :].to_broadcast([P, ROUTED, E]), ALU.is_ge))
                    link(v.reduce_sum(blk_f[:], past[:], AX_X))
                    link(v.tensor_scalar(blk_f[:], blk_f[:], float(E - 1), None, ALU.min))
                    link(v.tensor_copy(block_expert[:], blk_f[:]))

                def copy_xT(b):
                    v.wait_ge(s_xt, b + 1)
                    if b >= 2:
                        v.wait_ge(s_up, 2 * b - 2)
                    v.tensor_copy(xT[:, b % 2, :], p_x[:]).then_inc(s_xT, 1)

                copy_xT(0)
                copy_xT(1)
                choose_experts()
                for b in range(NT + 1):
                    if b < NT:
                        for z in range(2):
                            half = slice(z * NF * P // 2, (z + 1) * NF * P // 2)
                            v.wait_ge(s_ge, 2 * b + z + 1)
                            if b >= 2:
                                v.wait_ge(s_dn, b - 1)
                            v.tensor_copy(hT[:, b % 2, 0, half], h32[:, b % 2, half]).then_inc(s_hh, 1)
                            v.wait_ge(s_hh, 2 * b + z + 1)
                            v.tensor_tensor(hT[:, b % 2, 1, half], h32[:, b % 2, half], hT[:, b % 2, 0, half],
                                            ALU.subtract).then_inc(s_hl, 1)
                    if b + 2 < NT:
                        copy_xT(b + 2)
                    if b == 1:
                        assign_slots()
                    if b == 3:
                        list_blocks()
                    if b >= 1:
                        v.wait_ge(s_dn, b)
                        xs = m.x_res[:, (b - 1) * D:b * D]
                        v.tensor_tensor(xs, p_y[:, (b - 1) % 2, 0:D], xs, ALU.add).then_inc(s_add, 1)


def routed_experts_phase(nc, m, w_sb, s_w, block_expert):
    A = RB // P
    HALF = NF * RB // 2
    LAST = ROUTED - 1
    assert ROUTED % 2 == 1
    with ExitStack() as st:
        xb = m.sb("xb", [P, 2, A, 2 * D], BF16, st)
        xT = m.sb("xT", [P, 2, 2 * KC * RB], BF16, st)
        h32 = m.sb("h32", [P, NF * RB], F32, st)
        hT = m.sb("hT", [P, 2, 2, NF * RB], BF16, st)
        ysb = m.sb("ysb", [P, 2, A, D], F32, st)
        p_x = m.pb("p_x", [P, 2, 2 * KC * RB], BF16, st)
        p_h = m.pb("p_h", [P, NF * RB], F32, st)
        p_y = m.pb("p_y7", [P, A, CH], F32, st)
        s_xb = [m.sem(f"xb_in{r}", st) for r in range(2)]
        s_xt, s_xT, s_up = m.sem("x_transposed", st), m.sem("xT_ready", st), m.sem("up_done", st)
        s_ge, s_hh, s_hl = m.sem("gelu_done", st), m.sem("h_high", st), m.sem("h_low", st)
        s_dn, s_ys = m.sem("down_done", st), m.sem("y_copied", st)
        s_yo = [m.sem(f"y_out{r}", st) for r in range(2)]
        w = w_sb[:].rearrange("p e n -> p (e n)")
        with nc.Block() as block:
            @block.sync
            def _(sp):
                def load(b, r):
                    sp.dma_start(xb[:, r], m.x_slots[ds(b * RB, RB), :].rearrange("(a p) n -> p a n", p=P)
                                 ).then_inc(s_xb[r], 16)

                def store(b, r):
                    sp.wait_ge(s_ys, b + 1)
                    sp.dma_start(m.y_slots[ds(b * RB, RB), :].rearrange("(a p) n -> p a n", p=P), ysb[:, r]
                                 ).then_inc(s_yo[r], 16)

                load(0, 0)
                load(1, 1)
                for b in range(3):
                    sp.wait_ge(s_xt, b + 1)
                    load(b + 2, b % 2)
                with sp.Fori(0, (LAST - 4) // 2) as q:
                    for r in range(2):
                        b = 2 * q + 1 + r
                        sp.wait_ge(s_xt, b + 3)
                        load(b + 4, 1 - r)
                        store(b - 1, r)
                for b in range(LAST - 4, LAST + 1):
                    store(b, b % 2)
                for r in range(2):
                    sp.wait_ge(s_yo[r], 16 * ((ROUTED + 1 - r) // 2))

            @block.tensor
            def _(pe):
                def transposes(b, r, nth, first=False):
                    pe.wait_ge(s_xb[r], 16 * (nth + 1))
                    if not first:
                        pe.wait_ge(s_xT, b - 1)
                    for n in range(2 * KC):
                        for a in range(A):
                            last = pe.transpose(p_x[:, r, n * RB + a * P:n * RB + (a + 1) * P],
                                                xb[:, r, a, n * P:(n + 1) * P], m.identb[:])
                    last.then_inc(s_xt, 1)

                def weights_of(b):
                    return pe.snap(pe.value_load(block_expert[0:1, ds(b, 1)], min_val=0, max_val=E - 1) * WCOLS)

                def up(b, r, w0, first=False):
                    pe.wait_ge(s_xT, b + 1)
                    for half in range(2):
                        if not first:
                            pe.wait_ge(s_ge, 2 * b + half - 1)
                        up_products(pe, p_h, w, w0, xT[:, r], half).then_inc(s_up, 1)

                def down(b, r, w0, first=False):
                    if not first:
                        pe.wait_ge(s_ys, b)
                    for half in range(2):
                        pe.wait_ge(s_hl, 2 * b + half + 1)
                        last = down_products(pe, p_y, w, w0, hT[:, r], half)
                    last.then_inc(s_dn, 1)

                for e in range(E):
                    pe.wait_ge(s_w[e], 16)
                transposes(0, 0, 0, first=True)
                transposes(1, 1, 0, first=True)
                up(0, 0, weights_of(0), first=True)
                transposes(2, 0, 1)
                up(1, 1, weights_of(1))
                transposes(3, 1, 1)
                down(0, 0, weights_of(0), first=True)
                with pe.Fori(0, (LAST - 4) // 2) as q:
                    before = weights_of(2 * q + 1)
                    for r in range(2):
                        b = 2 * q + 2 + r
                        w0 = weights_of(b)
                        up(b, r, w0)
                        transposes(b + 2, r, q + 2)
                        down(b - 1, 1 - r, before)
                        before = w0
                before = weights_of(LAST - 3)
                for b in range(LAST - 2, LAST + 1):
                    w0 = weights_of(b)
                    up(b, b % 2, w0)
                    if b + 2 <= LAST:
                        transposes(b + 2, b % 2, (b + 2) // 2)
                    down(b - 1, 1 - b % 2, before)
                    before = w0
                down(LAST, LAST % 2, before)

            @block.scalar
            def _(a):
                def gelus(b, first=False):
                    for z in range(2):
                        half = slice(z * HALF, (z + 1) * HALF)
                        a.wait_ge(s_up, 2 * b + z + 1)
                        if not first:
                            a.wait_ge(s_hl, 2 * b + z - 1)
                        a.activation(h32[:, half], p_h[:, half], ACT.Gelu).then_inc(s_ge, 1)

                gelus(0, first=True)
                with a.Fori(0, LAST) as q:
                    gelus(q + 1)

            @block.vector
            def _(v):
                def copy_xT(b, r, first=False):
                    v.wait_ge(s_xt, b + 1)
                    if not first:
                        v.wait_ge(s_up, 2 * b - 2)
                    v.tensor_copy(xT[:, r, :], p_x[:, r, :]).then_inc(s_xT, 1)

                def split(b, r, first=False):
                    for z in range(2):
                        half = slice(z * HALF, (z + 1) * HALF)
                        v.wait_ge(s_ge, 2 * b + z + 1)
                        if not first:
                            v.wait_ge(s_dn, b - 1)
                        v.tensor_copy(hT[:, r, 0, half], h32[:, half]).then_inc(s_hh, 1)
                        v.wait_ge(s_hh, 2 * b + z + 1)
                        v.tensor_tensor(hT[:, r, 1, half], h32[:, half], hT[:, r, 0, half],
                                        ALU.subtract).then_inc(s_hl, 1)

                def copy_y(b, r, nth, first=False):
                    v.wait_ge(s_dn, b + 1)
                    if not first:
                        v.wait_ge(s_yo[r], 16 * nth)
                    v.tensor_copy(ysb[:, r], p_y[:, :, 0:D]).then_inc(s_ys, 1)

                copy_xT(0, 0, first=True)
                copy_xT(1, 1, first=True)
                split(0, 0, first=True)
                copy_xT(2, 0)
                split(1, 1, first=True)
                copy_xT(3, 1)
                copy_y(0, 0, 0, first=True)
                split(2, 0)
                copy_xT(4, 0)
                copy_y(1, 1, 0, first=True)
                with v.Fori(0, (LAST - 4) // 2) as q:
                    for r in range(2):
                        b = 2 * q + 3 + r
                        split(b, 1 - r)
                        copy_xT(b + 2, 1 - r)
                        copy_y(b - 1, r, q + 1)
                for b in range(LAST - 1, LAST + 1):
                    split(b, b % 2)
                    copy_y(b - 1, 1 - b % 2, (b - 1) // 2)
                copy_y(LAST, LAST % 2, LAST // 2)


def combine_phase(nc, m, slot_idx, gates):
    RING = 8
    with ExitStack() as st:
        ya = m.sb("ya", [P, RING, TOPK, D], F32, st)
        s_g = [[m.sem(f"gathered{k}_{r}", st) for r in range(RING)] for k in range(TOPK)]
        s_v, s_t, s_out = m.sem("combine_chain", st), m.sem("tile_done", st), m.sem("out_stored", st)
        with nc.Block() as block:
            @block.gpsimd
            def _(g):
                for t in range(NT):
                    r = t % RING
                    if t >= RING:
                        g.wait_ge(s_t, t - RING + 1)
                    for k in range(TOPK):
                        g.indirect_dma_start(ya[:, r, k, :], None, m.y_slots,
                                             bass.IndirectOffsetOnAxis(ap=slot_idx[:, k * NT + t:k * NT + t + 1], axis=0)
                                             ).then_inc(s_g[k][r], 16)

            @block.scalar
            def _(a):
                for t in range(NT):
                    a.wait_ge(s_t, t + 1)
                    a.dma_start(m.out[0, t * P:(t + 1) * P, :], m.x_res[:, t * D:(t + 1) * D]).then_inc(s_out, 16)
                a.wait_ge(s_out, 16 * NT)

            @block.vector
            def _(v):
                for t in range(NT):
                    r, xs = t % RING, m.x_res[:, t * D:(t + 1) * D]
                    v.wait_ge(s_g[0][r], 16 * (t // RING + 1))
                    v.scalar_tensor_tensor(out=xs, in0=ya[:, r, 0, :], scalar=gates[:, t, 0:1], in1=xs,
                                           op0=ALU.mult, op1=ALU.add).then_inc(s_v, 1)
                    v.wait_ge(s_v, t + 1)
                    v.wait_ge(s_g[1][r], 16 * (t // RING + 1))
                    v.scalar_tensor_tensor(out=xs, in0=ya[:, r, 1, :], scalar=gates[:, t, 1:2], in1=xs,
                                           op0=ALU.mult, op1=ALU.add).then_inc(s_t, 1)


def experts_phase(nc, m):
    with ExitStack() as st:
        w_sb = m.sb("w_sb", [P, E + 1, WCOLS], BF16, st)
        slot_idx = m.sb("slot_idx", [P, TOPK * NT], U32, st)
        gates = m.sb("gates", [P, NT, E], F32, st)
        block_expert = m.sb("block_expert", [P, ROUTED], U32, st)
        s_w = [m.sem(f"weights{e}", st) for e in range(E + 1)]
        with ExitStack() as rt:
            xhl = m.sb("xhl", [P, NT, 2, D], BF16, rt)
            p_lg = m.pb("p_lg", [P, 2 * NT + 1, E], F32, rt)
            router_phase(nc, m, w_sb, s_w, xhl, p_lg)
            shared_expert_phase(nc, m, w_sb, s_w, xhl, p_lg, slot_idx, gates, block_expert)
        routed_experts_phase(nc, m, w_sb, s_w, block_expert)
        combine_phase(nc, m, slot_idx, gates)
def build(nc, x, ctx_in, W_qkv, b_qkv, W_out, b_out, WqT, WkT, WvT, WoT,
          shared_up, shared_down, routed_up, routed_down, router_w, out):
    with ExitStack() as top:
        def sb(name, shape, dt=F32, st=top):
            return st.enter_context(nc.sbuf_tensor(name, shape, dt))

        def pb(name, shape, dt=F32, st=top):
            return st.enter_context(nc.psum_tensor(name, shape, dt))

        def sem(name, st=top):
            return st.enter_context(nc.semaphore(name))

        def dram(name, shape, dt):
            return nc.dram_tensor(name, shape, dt, kind="Internal").ap()

        w_img = dram("w_img", [E + 1, P, WCOLS], BF16)
        q2_parts = dram("q2_parts", [3, HEADS, DK, T], BF16)
        k2_parts = dram("k2_parts", [3, HEADS, DK, T], BF16)
        neg_rows = dram("neg_rows", [NG * NC, 2, GH * TPC, P], BF16)
        x_slots = dram("x_slots", [SLOTS, 2 * D], BF16)
        y_slots = dram("y_slots", [SLOTS, D], F32)

        x_res = sb("x_res", [P, NT * D])
        ident = sb("ident", [P, P])
        identb = sb("identb", [P, P], BF16)
        ones_row = sb("ones_row", [1, P])
        b_rows = sb("b_rows", [1, 2 * D])
        b_qk = sb("b_qk", [P, 2 * KC])
        w_rt = sb("w_rt", [P, KC, E])
        stats = sb("stats", [P, NT, 6])
        mv = sb("mv", [P, NT, 2])
        var_eps = sb("var_eps", [P, NT])
        neg_half = sb("neg_half", [P, NT])
        rstd = sb("rstd", [P, NT])

        att = top.enter_context(ExitStack())
        w_qkv = sb("w_qkv", [P, KC, 3 * D], F32, att)
        w_out = sb("w_out", [P, KC, D], F32, att)
        w_x = sb("w_x", [P, 4, KC, D], F32, att)

        m = Shared()
        m.sb, m.pb, m.sem, m.x_res, m.ident = sb, pb, sem, x_res, ident
        m.identb, m.ones_row, m.b_rows, m.b_qk, m.w_qkv = identb, ones_row, b_rows, b_qk, w_qkv
        m.w_out, m.w_x, m.w_rt, m.stats, m.mv = w_out, w_x, w_rt, stats, mv
        m.var_eps, m.neg_half, m.rstd, m.w_img, m.q2_parts = var_eps, neg_half, rstd, w_img, q2_parts
        m.k2_parts, m.neg_rows, m.x_slots, m.y_slots, m.ctx_in = k2_parts, neg_rows, x_slots, y_slots, ctx_in
        m.shared_up, m.shared_down, m.routed_up, m.routed_down, m.out = shared_up, shared_down, routed_up, routed_down, out

        m.s_x = [sem(f"x_in{c}") for c in range(NC)]
        m.s_w, m.s_later = sem("qkv_weights_in"), sem("later_inputs_in")
        m.EARLY, m.LATER = 4, 6
        with ExitStack() as st:
            s_fill = sem("filled", st)
            s_sel = sem("selected", st)
            with nc.Block() as block:
                @block.sync
                def _(sp):
                    xv = x.rearrange("a (t p) d -> p (a t) d", p=P)
                    xr = x_res[:].rearrange("p (t d) -> p t d", d=D)
                    for c in range(NC):
                        sp.dma_start(xr[:, TPC * c:TPC * (c + 1), :], xv[:, TPC * c:TPC * (c + 1), :]).then_inc(m.s_x[c], 16)
                    sp.dma_start(w_qkv[:], W_qkv.rearrange("(k p) n -> p k n", p=P)).then_inc(m.s_w, 16)
                    sp.dma_start(b_qk[:], b_qkv[0:2 * D].rearrange("(m p) -> p m", p=P),
                                 allow_slow_non_contiguous=True).then_inc(m.s_w, 16)
                    sp.dma_start(b_rows[:, 0:D], b_qkv[2 * D:3 * D].rearrange("(a n) -> a n", a=1)).then_inc(m.s_w, 16)
                    sp.dma_start(b_rows[:, D:2 * D], b_out.rearrange("(a n) -> a n", a=1)).then_inc(m.s_w, 16)
                    sp.dma_start(w_out[:], W_out.rearrange("(k p) n -> p k n", p=P)).then_inc(m.s_later, 16)
                    for n, w in enumerate((WqT, WkT, WvT, WoT)):
                        sp.dma_start(w_x[:, n], w.rearrange("(k p) n -> p k n", p=P)).then_inc(m.s_later, 16)
                    sp.dma_start(w_rt[:], router_w.rearrange("(k p) n -> p k n", p=P)).then_inc(m.s_later, 16)

                @block.gpsimd
                def _(g):
                    g.memset(ident[:], 0.0).then_inc(s_fill, 1)
                    g.memset(identb[:], 0.0).then_inc(s_fill, 1)
                    g.memset(ones_row[:], 1.0)
                    g.memset(neg_half[:], -0.5)
                    g.wait_ge(s_fill, 2)
                    for eye in (ident, identb):
                        g.affine_select(out=eye[:], in_=eye[:], compare_op=ALU.not_equal, fill=1.0, base=0,
                                        pattern=[[-1, P]], channel_multiplier=1).then_inc(s_sel, 1)

        with ExitStack() as sa:
            qk = [sb(f"qk{r}", [P, 2 * KC, T], BF16, sa) for r in range(2)]
            vv = [sb(f"vv{r}", [P, NT * D], BF16, sa) for r in range(2)]
            qkv_phase(nc, m, qk, vv)
            self_attention_phase(nc, m, qk, vv)
        with ExitStack() as xa:
            ctx2 = sb("ctx2", [P, NT, HEADS * DK], F32, xa)
            v2 = sb("v2", [P, NT, HEADS, DK + 1], F32, xa)
            cross_projection_phase(nc, m, v2)
            cross_attention_phase(nc, m, v2, ctx2)
            cross_output_phase(nc, m, ctx2)
        att.close()
        experts_phase(nc, m)


_INS = ['x', 'ctx_1024', 'L0_attn_W_qkv', 'L0_attn_b_qkv', 'L0_attn_W_out', 'L0_attn_b_out', 'L0_xattn_Wq',
        'L0_xattn_Wk', 'L0_xattn_Wv', 'L0_xattn_Wo', 'L0_ffn_shared_up', 'L0_ffn_shared_down',
        'L0_ffn_routed_up', 'L0_ffn_routed_down', 'L0_ffn_router_w']
_TRANSPOSED = ['L0_xattn_Wq', 'L0_xattn_Wk', 'L0_xattn_Wv', 'L0_xattn_Wo']


def kernel(**inputs):
    import concourse.bacc as bacc
    from concourse.bass_utils import run_bass_kernel_spmd

    nc = bacc.Bacc("TRN2", target_bir_lowering=False, num_devices=1)
    arrays, args = {}, []
    for name in _INS:
        a = np.asarray(inputs[name])
        a = np.ascontiguousarray(a.T if name in _TRANSPOSED else a)
        arrays[f"in_{name}"] = a
        args.append(nc.dram_tensor(f"in_{name}", a.shape, mybir.dt.from_np(a.dtype), kind="ExternalInput").ap())
    args.append(nc.dram_tensor("out_x", (1, T, D), F32, kind="ExternalOutput").ap())
    build(nc, *args)
    result = run_bass_kernel_spmd(nc, [arrays], core_ids=[0])
    return result.results[0]["out_x"]
```

```python
from contextlib import ExitStack

import numpy as np

import concourse.bass as bass
from concourse import mybir

F32 = mybir.dt.float32
BF16 = mybir.dt.bfloat16
U32 = mybir.dt.uint32
ALU = mybir.AluOpType
ACT = mybir.ActivationFunctionType
AX_X = mybir.AxisListType.X
ds = bass.ds

P = 128
D = 256
KC = D // P
T = 2048
NT = T // P
CH = 512
NC = T // CH
TPC = CH // P
S_CTX = 1601
NTC = (S_CTX + P - 1) // P
CTX_LAST = S_CTX - (NTC - 1) * P
HEADS = 16
DK = D // HEADS
GH = 4
NG = HEADS // GH
F = 1024
NF = F // P
E = 8
TOPK = 2
RB = 2 * P
ROUTED = (T * TOPK + E * (RB - 1)) // RB
TAIL = 3
SHARED = NT - TAIL * RB // P
SLOTS = (ROUTED + TAIL) * RB
UP, DOWN = 0, 2 * KC * F
WCOLS = 2 * KC * F + 2 * NF * D
EPS = 1e-5
NEG = -1.0e30
PASSES = ((0, 0), (0, 1), (1, 0))
Q_PARTS = (0, 0, 0, 1, 1, 2)
K_PARTS = (0, 1, 2, 0, 1, 0)
STACK = len(Q_PARTS) * DK
CHUNKS = [(g, c) for g in range(NG) for c in range(NC)]
STEPS = [(rho, j, max(0, j - TPC * c) * P) for rho, (_, c) in enumerate(CHUNKS) for j in range(min(TPC * (c + 1), NTC))]
NSTEP = len(STEPS)
FIRST_OF = [min(s for s, x in enumerate(STEPS) if x[0] == rho) for rho in range(NG * NC)]
LAST_OF = [max(s for s, x in enumerate(STEPS) if x[0] == rho) for rho in range(NG * NC)]
LEAD = 0.12
START, RAMP = 0.08, 0.5
AHEAD = 4
UNITS = [[(i, h, k, min(CH, min(P * (i + 1), S_CTX) - k)) for i in range(TPC * c, TPC * (c + 1)) for h in range(GH)
          for k in range(0, min(P * (i + 1), S_CTX), CH)] for c in range(NC)]


def cross_schedule():
    stream = []
    for rho, (_, c) in enumerate(CHUNKS):
        units = [("unit", rho, n) for n in range(len(UNITS[c]))]
        stream += units[:3] + ([("row", rho - 1)] if rho else []) + units[3:]
    stream.append(("row", len(CHUNKS) - 1))
    row_at = {x[1]: n for n, x in enumerate(stream) if x[0] == "row"}

    def vector_work(x):
        return UNITS[CHUNKS[x[1]][1]][x[2]][3] + 64 if x[0] == "unit" else 600

    total = sum(vector_work(x) for x in stream)
    main_total = sum(CH - off for _, _, off in STEPS)
    entries, ranges, done, main, at = [], {}, 0, 0, 0
    for step in range(-1, NSTEP + 2):
        for place in range(3):
            first = len(entries)
            if 0 <= step < NSTEP:
                main += (CH - STEPS[step][2]) / 3
            share = main / main_total
            goal = (share + min(LEAD, START + RAMP * share)) * total
            must = row_at[STEPS[min(step + AHEAD, NSTEP - 1)][0]]
            while at < len(stream) and (done < goal or at <= must):
                done += vector_work(stream[at])
                entries.append(stream[at])
                at += 1
            if place == 2 and step - 2 in LAST_OF:
                entries.append(("out", STEPS[step - 2][0]))
            ranges[step, place] = (first, len(entries))
    assert at == len(stream)
    return entries, ranges


class Shared:
    pass

LN_LINKS = 2 * TPC + 1


def layernorm_stats(v, m, s_ln, c):
    for t in range(c * TPC, (c + 1) * TPC):
        v.bn_stats(m.stats[:, t, :], m.x_res[:, t * D:(t + 1) * D]).then_inc(s_ln, 1)
    for j in range(TPC):
        v.wait_ge(s_ln, c * LN_LINKS + j + 1)
        v.bn_aggr(m.mv[:, c * TPC + j, :], m.stats[:, c * TPC + j, :]).then_inc(s_ln, 1)
    v.wait_ge(s_ln, c * LN_LINKS + 2 * TPC)
    v.tensor_scalar(m.var_eps[:, c * TPC:(c + 1) * TPC], m.mv[:, c * TPC:(c + 1) * TPC, 1], EPS, None,
                    ALU.add).then_inc(s_ln, 1)


def layernorm_power(g, m, s_ln, s_pow, c):
    tiles = slice(c * TPC, (c + 1) * TPC)
    g.wait_ge(s_ln, (c + 1) * LN_LINKS)
    g.tensor_tensor(m.rstd[:, tiles], m.var_eps[:, tiles], m.neg_half[:, tiles], ALU.pow).then_inc(s_pow, 1)


def layernorm_rows(v, m, s_xn, xn, c):
    for j in range(TPC):
        t = c * TPC + j
        v.tensor_scalar(xn[:, j * D:(j + 1) * D], m.x_res[:, t * D:(t + 1) * D],
                        m.mv[:, t, 0:1], m.rstd[:, t:t + 1], ALU.subtract, ALU.mult).then_inc(s_xn, 1)


def qkv_phase(nc, m, qk, vv):
    with ExitStack() as st:
        xn = m.sb("xn", [P, NC, TPC * D], F32, st)
        xnT = m.sb("xnT", [P, 2, 2, KC, CH], BF16, st)
        whl = m.sb("w_qkv_hl", [P, 2, KC, 3 * D], BF16, st)
        p_t = m.pb("p_t", [P, KC, CH], F32, st)
        p_qk = m.pb("p_qk", [P, 2 * KC, CH], F32, st)
        p_v = m.pb("p_v", [P, TPC, D], F32, st)
        s_bias = m.sem("bias_added", st)
        s_ln, s_pow, s_xn = m.sem("ln_stats", st), m.sem("ln_pow", st), m.sem("xn_ready", st)
        s_tr, s_xh, s_xl = m.sem("transposed", st), m.sem("xnT_high", st), m.sem("xnT_low", st)
        s_wh, s_wl = m.sem("w_qkv_high", st), m.sem("w_qkv_low", st)
        s_mm, s_hi, s_lo = m.sem("projected", st), m.sem("high_ready", st), m.sem("low_ready", st)
        NOUT = 2 * KC + 1
        with nc.Block() as block:
            @block.sync
            def _(sp):
                assert (NC - 1) * TPC == NTC - 1
                for c in range(NC - 1):
                    sp.dma_start(m.ctx_sb[:, c].rearrange("p (t d) -> p t d", d=D),
                                 m.ctx_in[0, c * CH:(c + 1) * CH].rearrange("(t p) d -> p t d", p=P)).then_inc(m.s_cx[c], 16)
                sp.dma_start(m.ctx_sb[0:CTX_LAST, NC - 1, 0:D], m.ctx_in[0, S_CTX - CTX_LAST:S_CTX, :]
                             ).then_inc(m.s_cx[NC - 1], 16)
                sp.wait_ge(m.s_later, 16 * m.LATER)

            @block.vector
            def _(v):
                def low(c):
                    for k in range(2 * KC):
                        v.wait_ge(s_hi, c * NOUT + k + 1)
                        v.scalar_tensor_tensor(out=qk[1][:, k, c * CH:(c + 1) * CH], in0=p_qk[:, k, :],
                                               scalar=m.b_qk[:, k:k + 1], in1=qk[0][:, k, c * CH:(c + 1) * CH],
                                               op0=ALU.add, op1=ALU.subtract).then_inc(s_lo, 1)
                    if c + 1 < NC:
                        low_xnT(c + 1)
                    v.wait_ge(s_hi, (c + 1) * NOUT)
                    v.tensor_tensor(vv[1][:, c * TPC * D:(c + 1) * TPC * D], p_v[:].rearrange("p a d -> p (a d)"),
                                    vv[0][:, c * TPC * D:(c + 1) * TPC * D], ALU.subtract).then_inc(s_lo, 1)

                def low_xnT(c):
                    v.wait_ge(s_xh, c + 1)
                    v.tensor_tensor(xnT[:, c % 2, 1], p_t[:], xnT[:, c % 2, 0], ALU.subtract).then_inc(s_xl, 1)

                def rows(c):
                    v.wait_ge(s_pow, c + 1)
                    layernorm_rows(v, m, s_xn, xn[:, c], c)

                for c in range(NC):
                    v.wait_ge(m.s_x[c], 16)
                    layernorm_stats(v, m, s_ln, c)
                    if c:
                        rows(c - 1)
                    if c == 1:
                        v.wait_ge(s_wh, 1)
                        v.tensor_tensor(whl[:, 1], m.w_qkv[:], whl[:, 0], ALU.subtract).then_inc(s_wl, 1)
                        low_xnT(0)
                rows(NC - 1)
                v.wait_ge(m.s_w, 16 * m.EARLY)
                for c in range(NC):
                    low(c)

            @block.gpsimd
            def _(g):
                for c in range(NC):
                    layernorm_power(g, m, s_ln, s_pow, c)
                g.wait_ge(m.s_w, 16 * m.EARLY)
                for c in range(NC):
                    xs = m.x_res[:, c * TPC * D:(c + 1) * TPC * D].rearrange("p (t d) -> p t d", d=D)
                    g.wait_ge(s_xn, (c + 1) * TPC)
                    g.tensor_tensor(xs, xs, m.b_rows[:, None, D:2 * D].to_broadcast([P, TPC, D]), ALU.add
                                    ).then_inc(s_bias, 1)

            @block.scalar
            def _(a):
                def copy_xnT(c):
                    a.wait_ge(s_tr, c + 1)
                    if c >= 2:
                        a.wait_ge(s_mm, (c - 1) * NOUT)
                    a.copy(xnT[:, c % 2, 0], p_t[:]).then_inc(s_xh, 1)

                a.wait_ge(m.s_w, 16 * m.EARLY)
                a.copy(whl[:, 0], m.w_qkv[:]).then_inc(s_wh, 1)
                copy_xnT(0)
                for c in range(NC):
                    for k in range(2 * KC):
                        a.wait_ge(s_mm, c * NOUT + k + 1)
                        a.activation(qk[0][:, k, c * CH:(c + 1) * CH], p_qk[:, k, :], ACT.Identity,
                                     bias=m.b_qk[:, k:k + 1]).then_inc(s_hi, 1)
                    if c + 1 < NC:
                        copy_xnT(c + 1)
                    a.wait_ge(s_mm, (c + 1) * NOUT)
                    a.copy(vv[0][:, c * TPC * D:(c + 1) * TPC * D],
                           p_v[:].rearrange("p a d -> p (a d)")).then_inc(s_hi, 1)

            @block.tensor
            def _(pe):
                def transposes(c):
                    pe.wait_ge(s_xn, (c + 1) * TPC)
                    if c:
                        pe.wait_ge(s_xl, c)
                    for k in range(KC):
                        for j in range(TPC):
                            last = pe.transpose(p_t[:, k, j * P:(j + 1) * P],
                                                xn[:, c, j * D + k * P:j * D + (k + 1) * P], m.ident[:])
                    last.then_inc(s_tr, 1)

                products = [(wp, xp, k) for wp, xp in PASSES for k in range(KC)]
                transposes(0)
                pe.wait_ge(s_wl, 1)
                for c in range(NC):
                    pe.wait_ge(s_xl, c + 1)
                    for n in range(2 * KC):
                        if c:
                            pe.wait_ge(s_lo, (c - 1) * NOUT + n + 1)
                        for i, (wp, xp, k) in enumerate(products):
                            last = pe.matmul(p_qk[:, n, :], whl[:, wp, k, n * P:(n + 1) * P], xnT[:, c % 2, xp, k, :],
                                             start=(i == 0), stop=(i == len(products) - 1))
                        last.then_inc(s_mm, 1)
                    if c + 1 < NC:
                        transposes(c + 1)
                    if c:
                        pe.wait_ge(s_lo, c * NOUT)
                    for j in range(TPC):
                        for i, (wp, xp, k) in enumerate(products):
                            last = pe.matmul(p_v[:, j, :], xnT[:, c % 2, xp, k, j * P:(j + 1) * P], whl[:, wp, k, 2 * D:],
                                             start=(i == 0), stop=(i == len(products) - 1))
                    last.then_inc(s_mm, 1)

def self_attention_phase(nc, m, qk, vv):
    with ExitStack() as st:
        p32 = m.sb("p32", [P, T], F32, st)
        pp = [m.sb(f"pp{r}", [P, T], BF16, st) for r in range(2)]
        ppT = m.sb("ppT", [P, NC, 2, TPC * P], BF16, st)
        ctx_n = m.sb("ctx_n", [P, D], F32, st)
        ctxT = m.sb("ctxT", [P, KC, P], F32, st)
        mx4 = m.sb("mx4", [P, NC], F32, st)
        mx1 = m.sb("mx1", [P, 1], F32, st)
        neg_max = m.sb("neg_max", [P, 1], F32, st)
        sums = m.sb("sums", [P, NC], F32, st)
        sum1 = m.sb("sum1", [P, 1], F32, st)
        rsum = m.sb("rsum", [P, 1], F32, st)
        w32 = m.sb("w32", [P, 2, 2 * KC * F // 2], F32, st)
        zeros = m.sb("zeros", [P, KC * F], F32, st)
        whl = m.sb("whl", [P, 2, 2, KC * F], BF16, st)
        p_s = m.pb("p_s", [P, NC, CH], F32, st)
        p_t = m.pb("p_pt", [P, 2, 2 * TPC * P], BF16, st)
        p_o = m.pb("p_o", [P, D], F32, st)
        p_y = m.pb("p_y", [P, 2, D], F32, st)
        s_s, s_max, s_exp = m.sem("scores", st), m.sem("max_ready", st), m.sem("exp_done", st)
        s_split, s_tr, s_pt = m.sem("split", st), m.sem("p_transposed", st), m.sem("pT_ready", st)
        s_pv, s_ctx, s_ct = m.sem("pv_done", st), m.sem("ctx_ready", st), m.sem("ctx_transposed", st)
        s_ctT, s_y, s_add = m.sem("ctxT_ready", st), m.sem("y_ready", st), m.sem("added", st)
        s_v = m.sem("dve_chain", st)
        NV = 10
        s_wl = [m.sem(f"weights_in{r}", st) for r in range(2)]
        s_wh, s_wlo = m.sem("weights_high", st), m.sem("weights_low", st)
        s_ws = [m.sem(f"weights_stored{r}", st) for r in range(2)]
        s_zero, s_zs = m.sem("zeroed", st), m.sem("slots_zeroed", st)
        NW = KC * F
        SCALE = 1.0 / 16.0
        assert SCALE * SCALE * D == 1.0

        with nc.Block() as block:
            @block.tensor
            def _(pe):
                def scores(i, chunks=range(NC)):
                    for c in chunks:
                        pe.wait_ge(s_exp, i * NC + c + 1)
                        n = 0
                        for a, b in PASSES:
                            for k in range(KC):
                                last = pe.matmul(p_s[:, c, :], qk[a][:, k, ds(i * P, P)],
                                                 qk[b][:, KC + k, c * CH:(c + 1) * CH],
                                                 start=(n == 0), stop=(n == 3 * KC - 1))
                                n += 1
                        last.then_inc(s_s, 1)

                def transposes(i, g):
                    pe.wait_ge(s_split, NC + i * NC + g + 1)
                    pe.wait_ge(s_pt, i * NC + g + 1)
                    for r in range(2):
                        for b in range(TPC):
                            last = pe.transpose(p_t[:, g % 2, (r * TPC + b) * P:(r * TPC + b + 1) * P],
                                                pp[r][:, g * CH + b * P:g * CH + (b + 1) * P], m.identb[:])
                    last.then_inc(s_tr, 1)

                def values(i, g):
                    pe.wait_ge(s_pt, 2 + i * NC + g + 1)
                    if g == 0:
                        pe.wait_ge(s_ctx, i + 1)
                    for b in range(TPC):
                        kt = g * TPC + b
                        for n, (a, w) in enumerate(PASSES):
                            last = pe.matmul(p_o[:], ppT[:, g, a, b * P:(b + 1) * P],
                                             vv[w][:, kt * D:(kt + 1) * D],
                                             start=(kt == 0 and n == 0), stop=(kt == NT - 1 and n == 2))
                    last.then_inc(s_pv, 1)

                def weigh(i):
                    for g in range(NC):
                        if g + 1 < NC:
                            transposes(i, g + 1)
                        values(i, g)

                def context_T(i):
                    pe.wait_ge(s_ctx, 1 + i + 1)
                    pe.wait_ge(s_add, i + 1)
                    for k in range(KC):
                        last = pe.transpose(p_y[:, 0, k * P:(k + 1) * P], ctx_n[:, k * P:(k + 1) * P], m.ident[:])
                    last.then_inc(s_ct, 1)

                def project(i):
                    pe.wait_ge(s_ctT, i + 1)
                    for k in range(KC):
                        last = pe.matmul(p_y[:, 1, :], ctxT[:, k, :], m.w_out[:, k, :],
                                         start=(k == 0), stop=(k == KC - 1))
                    last.then_inc(s_y, 1)

                scores(0)
                scores(1, range(NC - 1))
                transposes(0, 0)
                scores(1, (NC - 1,))
                weigh(0)
                with pe.Fori(2, NT) as i:
                    scores(i, range(NC - 1))
                    transposes(i - 1, 0)
                    scores(i, (NC - 1,))
                    context_T(i - 2)
                    weigh(i - 1)
                    project(i - 2)
                transposes(NT - 1, 0)
                context_T(NT - 2)
                weigh(NT - 1)
                project(NT - 2)
                context_T(NT - 1)
                project(NT - 1)

            @block.vector
            def _(v):
                v.sem_inc(s_split, NC)
                v.sem_inc(s_ctx, 1)
                v.sem_inc(s_add, 1)

                def maxima(i):
                    for c in range(NC):
                        v.wait_ge(s_s, i * NC + c + 1)
                        v.reduce_max(mx4[:, c:c + 1], p_s[:, c, :], AX_X).then_inc(s_v, 1)
                    v.wait_ge(s_v, i * NV + NC)
                    v.reduce_max(mx1[:], mx4[:], AX_X).then_inc(s_v, 1)
                    v.wait_ge(s_v, i * NV + NC + 1)
                    v.tensor_scalar(neg_max[:], mx1[:], -SCALE, None, ALU.mult).then_inc(s_max, 1)

                def split(i):
                    for g in range(NC):
                        cols = slice(g * CH, (g + 1) * CH)
                        v.wait_ge(s_exp, NC + i * NC + g + 1)
                        v.wait_ge(s_tr, i * NC + g + 1)
                        v.tensor_copy(pp[0][:, cols], p32[:, cols]).then_inc(s_v, 1)
                        v.wait_ge(s_v, i * NV + NC + 2 + g)
                        v.tensor_tensor(pp[1][:, cols], p32[:, cols], pp[0][:, cols], ALU.subtract).then_inc(s_split, 1)

                def normalise(i):
                    v.wait_ge(s_pv, NC + i * NC + NC)
                    v.wait_ge(s_ct, i + 1)
                    v.scalar_tensor_tensor(out=ctx_n[:], in0=p_o[:], scalar=rsum[:], in1=m.b_rows[:, 0:D],
                                           op0=ALU.mult, op1=ALU.add).then_inc(s_ctx, 1)

                def row_sums(i):
                    v.reduce_sum(sum1[:], sums[:], AX_X).then_inc(s_v, 1)
                    v.wait_ge(s_v, i * NV + NV)
                    v.reciprocal(rsum[:], sum1[:]).then_inc(s_rs, 1)

                def add(i):
                    v.wait_ge(s_y, 1 + i + 1)
                    xs = m.x_res[:, ds(i * D, D)]
                    v.tensor_tensor(xs, p_y[:, 1, :], xs, ALU.add).then_inc(s_add, 1)

                s_rs = m.sem("row_sums", st)
                maxima(0)
                split(0)
                row_sums(0)
                maxima(1)
                split(1)
                v.wait_ge(s_rs, 1)
                normalise(0)
                v.wait_ge(s_ctx, 2)
                row_sums(1)
                with v.Fori(2, NT) as i:
                    maxima(i)
                    split(i)
                    v.wait_ge(s_rs, i)
                    normalise(i - 1)
                    v.wait_ge(s_ctx, i + 1)
                    row_sums(i)
                    add(i - 2)
                v.wait_ge(s_rs, NT)
                normalise(NT - 1)
                add(NT - 2)
                add(NT - 1)

            @block.scalar
            def _(a):
                a.sem_inc(s_exp, NC)
                a.sem_inc(s_pt, 2)

                def exps(i, c):
                    if c == 0:
                        a.wait_ge(s_max, i + 1)
                    a.wait_ge(s_split, i * NC + c + 1)
                    a.activation(p32[:, c * CH:(c + 1) * CH], p_s[:, c, :], ACT.Exp, bias=neg_max[:],
                                 scale=SCALE, accum_out=sums[:, c:c + 1]).then_inc(s_exp, 1)

                def copy_pT(i, g):
                    a.wait_ge(s_tr, NC + i * NC + g + 1)
                    a.wait_ge(s_pv, i * NC + g + 1)
                    a.copy(ppT[:, g].rearrange("p r n -> p (r n)"), p_t[:, g % 2, :]).then_inc(s_pt, 1)

                def copy_ctxT(i):
                    a.wait_ge(s_ct, 1 + i + 1)
                    a.wait_ge(s_y, i + 1)
                    a.copy(ctxT[:].rearrange("p k n -> p (k n)"), p_y[:, 0, :]).then_inc(s_ctT, 1)

                def mixed(i):
                    copy_pT(i - 1, 1)
                    exps(i, 0)
                    copy_pT(i - 1, 2)
                    exps(i, 1)
                    copy_pT(i - 1, 3)
                    exps(i, 2)
                    exps(i, 3)

                for c in range(NC):
                    exps(0, c)
                copy_pT(0, 0)
                mixed(1)
                with a.Fori(2, NT) as i:
                    copy_pT(i - 1, 0)
                    copy_ctxT(i - 2)
                    mixed(i)
                copy_pT(NT - 1, 0)
                copy_ctxT(NT - 2)
                for g in range(1, NC):
                    copy_pT(NT - 1, g)
                copy_ctxT(NT - 1)

            @block.gpsimd
            def _(g):
                for s, n in ((s_tr, NC), (s_pv, NC), (s_ct, 1), (s_y, 1)):
                    g.sem_inc(s, n)

                g.memset(zeros[:], 0.0).then_inc(s_zero, 1)
                g.wait_ge(s_zero, 1)

                def split_weights(e, r):
                    g.wait_ge(s_wl[r], (e + 1) * 16)
                    g.wait_ge(s_ws[r], (e + 1) * 16)
                    g.tensor_tensor(whl[:, r, 0, :], w32[:, r, :], zeros[:], ALU.add).then_inc(s_wh, 1)
                    g.wait_ge(s_wh, 2 * e + r + 1)
                    g.tensor_tensor(whl[:, r, 1, :], w32[:, r, :], whl[:, r, 0, :], ALU.subtract).then_inc(s_wlo, 1)

                with g.Fori(0, E + 1) as e:
                    split_weights(e, 0)
                    split_weights(e, 1)

            @block.sync
            def _(sp):
                def load(r, src):
                    sp.dma_start(w32[:, r, :].rearrange("p (k n) -> p k n", k=src.shape[0] // P),
                                 src.rearrange("(k p) n -> p k n", p=P)).then_inc(s_wl[r], 16)

                def store(e, r):
                    sp.wait_ge(s_wlo, 2 * e + r + 1)
                    sp.dma_start(m.w_img[ds(e, 1), :, r * 2 * NW:(r + 1) * 2 * NW].rearrange("e p n -> (e p) n"),
                                 whl[:, r].rearrange("p h n -> p (h n)")).then_inc(s_ws[r], 16)

                sp.wait_ge(s_zero, 1)
                zv = zeros[:, 0:RB // P * D].bitcast(BF16).rearrange("p (a n) -> p a n", n=2 * D)
                for b in range(ROUTED):
                    sp.dma_start(m.x_slots[b * RB:(b + 1) * RB, :].rearrange("(a p) n -> p a n", p=P), zv).then_inc(s_zs, 16)
                sp.sem_inc(s_ws[0], 16)
                sp.sem_inc(s_ws[1], 16)
                load(0, m.routed_up[0])
                load(1, m.routed_down[0])
                with sp.Fori(0, E - 1) as e:
                    store(e, 0)
                    load(0, m.routed_up[ds(e + 1, 1)].rearrange("e k n -> (e k) n"))
                    store(e, 1)
                    load(1, m.routed_down[ds(e + 1, 1)].rearrange("e k n -> (e k) n"))
                store(E - 1, 0)
                load(0, m.shared_up[0])
                store(E - 1, 1)
                load(1, m.shared_down[0])
                store(E, 0)
                store(E, 1)
                sp.wait_ge(s_zs, 16 * ROUTED)
                sp.wait_ge(s_ws[0], 16 * (E + 2))
                sp.wait_ge(s_ws[1], 16 * (E + 2))


def cross_projection_phase(nc, m, v2):
    with ExitStack() as st:
        xn = m.sb("xn2", [P, NC, TPC * D], F32, st)
        ctx_sb, s_cx = m.ctx_sb, m.s_cx
        rT = m.sb("rT2", [P, 2, KC, CH], F32, st)
        parts = m.parts
        rest = m.sb("rest", [P, KC, CH], F32, st)
        p_t = m.pb("p_t2", [P, KC, CH], F32, st)
        p_m = m.pb("p_m2", [P, 2, KC, CH], F32, st)
        p_v = m.pb("p_v2", [P, TPC, D], F32, st)
        s_ln, s_pow, s_xn = m.sem("ln2_stats", st), m.sem("ln2_pow", st), m.sem("xn2_ready", st)
        s_one, s_zero = m.sem("ones_set", st), m.sem("constants_set", st)
        s_tr, s_rT = m.sem("transposed2", st), m.sem("rT2_ready", st)
        s_mm, s_p0, s_r1 = m.sem("projected2", st), m.sem("part0", st), m.sem("rest1", st)
        s_p1, s_p2 = m.sem("part1", st), m.sem("part2", st)
        s_st = m.s_parts
        s_vm, s_vd = m.sem("values_done", st), m.sem("values_copied", st)
        q_dst = m.q2_parts.rearrange("r (m h) k t -> (h k) (r m) t", m=KC)
        k_dst = m.k2_parts.rearrange("r (m h) k t -> (h k) (r m) t", m=KC)
        with nc.Block() as block:
            @block.sync
            def _(sp):

                def store(n):
                    dst, c = (k_dst, n) if n < NC else (q_dst, n - NC)
                    sp.wait_ge(s_p2, (n + 1) * KC)
                    sp.dma_start(dst[:, :, c * CH:(c + 1) * CH],
                                 parts[:, n % 2].rearrange("p r m t -> p (r m) t")).then_inc(s_st[n % 2], 16)

                def stored(n):
                    sp.wait_ge(s_st[n % 2], 16 * (n // 2 + 1))

                for n in range(NC + 1):
                    store(n)
                stored(NC - 2)
                stored(NC - 1)
                key_stack(sp, m, 0)
                store(NC + 1)
                stored(NC)
                stored(NC + 1)
                query_stack(sp, m, 0, 0, T // 2, m.s_stack[0])
                for n in range(NC + 2, 2 * NC):
                    store(n)

            @block.gpsimd
            def _(g):
                for c in range(NC):
                    layernorm_power(g, m, s_ln, s_pow, c)
                g.wait_ge(s_pow, NC)
                g.memset(m.ks[STACK:STACK + 2], 1.0).then_inc(s_zero, 1)
                g.wait_ge(s_zero, 1)
                g.memset(m.mask[:], 0.0).then_inc(s_zero, 1)
                g.wait_ge(s_zero, 2)
                g.affine_select(out=m.mask[:], in_=m.mask[:], compare_op=ALU.is_ge, fill=NEG, base=0,
                                pattern=[[-1, P]], channel_multiplier=1).then_inc(s_one, 1)

            @block.scalar
            def _(a):
                def copy_rT(n):
                    a.wait_ge(s_tr, n + 1)
                    if n >= 2:
                        a.wait_ge(s_mm, (n - 1) * KC)
                        a.wait_ge(s_vm, min(n - 1, NC))
                    a.copy(rT[:, n % 2], p_t[:]).then_inc(s_rT, 1)

                copy_rT(0)
                for n in range(2 * NC):
                    for k in range(KC):
                        if n >= 2:
                            a.wait_ge(s_st[n % 2], 16 * (n // 2))
                        a.wait_ge(s_mm, n * KC + k + 1)
                        a.copy(parts[:, n % 2, 0, k, :], p_m[:, n % 2, k, :]).then_inc(s_p0, 1)
                        if k == 0 and n + 1 < 2 * NC:
                            copy_rT(n + 1)
                    if n < NC:
                        a.wait_ge(s_vm, n + 1)
                        tiles = min(TPC, NTC - n * TPC)
                        a.copy(v2[:, n * TPC:n * TPC + tiles, :, 0:DK],
                               p_v[:, 0:tiles].rearrange("p a (h k) -> p a h k", k=DK)).then_inc(s_vd, 1)

            @block.vector
            def _(v):
                def lower_parts(n):
                    r = n % 2
                    for k in range(KC):
                        v.wait_ge(s_p0, n * KC + k + 1)
                        if n:
                            v.wait_ge(s_p2, (n - 1) * KC + k + 1)
                        v.tensor_tensor(rest[:, k, :], p_m[:, r, k, :], parts[:, r, 0, k, :],
                                        ALU.subtract).then_inc(s_r1, 1)
                    for k in range(KC):
                        v.wait_ge(s_r1, n * KC + k + 1)
                        v.tensor_copy(parts[:, r, 1, k, :], rest[:, k, :]).then_inc(s_p1, 1)
                    for k in range(KC):
                        v.wait_ge(s_p1, n * KC + k + 1)
                        v.tensor_tensor(parts[:, r, 2, k, :], rest[:, k, :], parts[:, r, 1, k, :],
                                        ALU.subtract).then_inc(s_p2, 1)

                v.memset(v2[:, :, :, DK:DK + 1], 1.0).then_inc(s_one, 1)
                layernorm_stats(v, m, s_ln, 0)
                for c in range(NC):
                    if c + 1 < NC:
                        layernorm_stats(v, m, s_ln, c + 1)
                    v.wait_ge(s_pow, c + 1)
                    layernorm_rows(v, m, s_xn, xn[:, c], c)
                    lower_parts(c)
                for c in range(NC):
                    lower_parts(NC + c)

            @block.tensor
            def _(pe):
                def transposes(n):
                    if n < NC:
                        pe.wait_ge(s_cx[n], 16)
                    else:
                        pe.wait_ge(s_xn, (n - NC + 1) * TPC)
                    if n:
                        pe.wait_ge(s_rT, n)
                    src = ctx_sb if n < NC else xn
                    for k in range(KC):
                        for j in range(TPC):
                            last = pe.transpose(p_t[:, k, j * P:(j + 1) * P],
                                                src[:, n % NC, j * D + k * P:j * D + (k + 1) * P], m.ident[:])
                    last.then_inc(s_tr, 1)

                transposes(0)
                for n in range(2 * NC):
                    pe.wait_ge(s_rT, n + 1)
                    for o in range(KC):
                        if n >= 2:
                            pe.wait_ge(s_r1, (n - 2) * KC + o + 1)
                        for k in range(KC):
                            last = pe.matmul(p_m[:, n % 2, o, :], m.w_x[:, 1 if n < NC else 0, k, o * P:(o + 1) * P],
                                             rT[:, n % 2, k, :], start=(k == 0), stop=(k == KC - 1))
                        last.then_inc(s_mm, 1)
                        if o == 0 and n + 1 < 2 * NC:
                            transposes(n + 1)
                    if n < NC:
                        if n:
                            pe.wait_ge(s_vd, n)
                        for j in range(min(TPC, NTC - n * TPC)):
                            for k in range(KC):
                                last = pe.matmul(p_v[:, j, :], rT[:, n % 2, k, j * P:(j + 1) * P], m.w_x[:, 2, k, :],
                                                 start=(k == 0), stop=(k == KC - 1))
                        last.then_inc(s_vm, 1)

KT = NTC * P


def key_stack(sp, m, g):
    for r, part in enumerate(K_PARTS):
        sp.dma_start(m.ks[r * DK:(r + 1) * DK, g % 2, :].rearrange("k (h t) -> k h t", h=GH),
                     m.k2_parts[part, g * GH:(g + 1) * GH, :, 0:KT].rearrange("h k t -> k h t")
                     ).then_inc(m.s_stack[g % 2], 16)


def query_stack(sp, m, g, first, end, sem):
    for r, part in enumerate(Q_PARTS):
        sp.dma_start(m.qs[r * DK:(r + 1) * DK, g % 2, :].rearrange("k (h t) -> k h t", h=GH)[:, :, first:end],
                     m.q2_parts[part, g * GH:(g + 1) * GH, :, first:end].rearrange("h k t -> k h t")
                     ).then_inc(sem, 16)


def cross_attention_phase(nc, m, v2, ctx2):
    PRING, RING = 4, 3
    entries, ranges = cross_schedule()
    index = {x: n for n, x in enumerate(entries)}
    steps = [(n, rho, *CHUNKS[rho], j, off) for n, (rho, j, off) in enumerate(STEPS)]
    keys = [min(P, S_CTX - j * P) for j in range(NTC)]
    diagonal = [n for n, _, _, c, j, _ in steps if j >= TPC * c]
    group_end = [LAST_OF[(g + 1) * NC - 1] + 1 for g in range(NG)]

    with ExitStack() as st:
        qs, ks = m.qs, m.ks
        pw = m.sb("pw", [P, PRING, GH, CH], F32, st)
        vg = m.sb("vg", [P, 2, NTC, GH, 32], F32, st)
        oT = m.sb("oT", [P, CH], F32, st)
        mx_part = m.sb("mx_part", [P, GH * TPC, NC], F32, st)
        mx = m.sb("mx", [P, GH * TPC], F32, st)
        neg = m.sb("neg", [GH * TPC, 2, 2, P], BF16, st)
        rden = m.sb("rden", [P, 2, TPC, GH, 1], F32, st)
        p_st = m.pb("p_st", [P, 2, 2, CH], F32, st)
        p_ring = m.pb("p_ring", [P, RING, CH], F32, st)
        p_acc = m.pb("p_acc", [P, CH], F32, st)
        s_set = m.sem("values_zeroed", st)
        s_ns = [m.sem(f"neg_stored{r}", st) for r in range(2)]
        s_rows = [m.sem(f"neg_rows_in{r}", st) for r in range(2)]
        s_st, s_exp, s_mask = m.sem("st_scores", st), m.sem("weights_ready", st), m.sem("masked", st)
        s_pv, s_acc, s_vg = m.sem("xpv_done", st), m.sem("acc_copied", st), m.sem("values_staged", st)
        s_entry, s_taken = m.sem("entry_ready", st), m.sem("entry_taken", st)
        s_mx, s_nh, s_rd = m.sem("chunk_max", st), m.sem("neg_high", st), m.sem("rden_ready", st)

        with nc.Block() as block:
            @block.tensor
            def _(pe):
                def transposed_scores(n, pair):
                    _, rho, g, c, j, off = steps[n]
                    if pair == 0 and n in FIRST_OF:
                        pe.wait_ge(s_rows[rho % 2], 16 * (rho // 2 + 1))
                    if n >= 1:
                        pe.wait_ge(s_exp, 2 * n + pair - 1)
                    for h in (0, 1):
                        hh = 2 * pair + h
                        last = pe.matmul(p_st[0:keys[j], pair, h, off:CH],
                                         ks[:, g % 2, hh * KT + j * P:hh * KT + j * P + keys[j]],
                                         qs[:, g % 2, hh * T + c * CH + off:hh * T + (c + 1) * CH],
                                         start=True, stop=True)
                    last.then_inc(s_st, 1)

                def values(n):
                    _, rho, g, c, j, off = steps[n]
                    if n in FIRST_OF:
                        pe.wait_ge(s_vg, g + 1)
                        if n:
                            pe.wait_ge(s_acc, rho)
                    if n in diagonal:
                        pe.wait_ge(s_mask, diagonal.index(n) + 1)
                    else:
                        pe.wait_ge(s_exp, 2 * n + 2)
                    for hh in range(GH):
                        last = pe.matmul(p_acc[32 * hh:32 * hh + 32, off:CH], vg[0:keys[j], g % 2, j, hh, :],
                                         pw[0:keys[j], n % PRING, hh, off:CH], start=(j == 0), stop=(n in LAST_OF))
                    last.then_inc(s_pv, 1)

                def unit(bank, rho, u):
                    g, c = CHUNKS[rho]
                    i, h, k0, w = UNITS[c][u]
                    if u == 0:
                        pe.wait_ge(m.s_stack[g % 2], 16 * 2 * len(Q_PARTS) * (g // 2 + 1))
                        if g == 0 and c == NC // 2:
                            pe.wait_ge(m.s_tail, 16 * len(Q_PARTS))
                    diag = k0 <= i * P < k0 + w
                    last = pe.matmul(bank[:, 0:w], qs[0:STACK, g % 2, h * T + i * P:h * T + (i + 1) * P],
                                     ks[0:STACK, g % 2, h * KT + k0:h * KT + k0 + w], start=True, stop=not diag)
                    if diag:
                        last = pe.matmul(bank[:, i * P - k0:w], m.identb[:], m.mask[:, 0:w - (i * P - k0)],
                                         start=False, stop=True)
                    return last

                def ring(n, place):
                    for e in range(*ranges[n, place]):
                        kind, *what = entries[e]
                        bank = p_ring[:, e % RING, :]
                        if e >= RING:
                            pe.wait_ge(s_taken, e - RING + 1)
                        if kind == "unit":
                            last = unit(bank, *what)
                        elif kind == "row":
                            pe.wait_ge(s_mx, what[0] + 1)
                            last = pe.transpose(bank[0:GH * TPC, 0:P], mx[:], m.ident[:])
                        else:
                            pe.wait_ge(s_acc, what[0] + 1)
                            for a in range(TPC):
                                last = pe.transpose(bank[:, a * P:(a + 1) * P], oT[:, a * P:(a + 1) * P], m.ident[:])
                        last.then_inc(s_entry, 1)

                for place in range(3):
                    ring(-1, place)
                for n in range(NSTEP + 2):
                    for pair in range(2):
                        if n < NSTEP:
                            transposed_scores(n, pair)
                        ring(n, pair)
                    if 1 <= n <= NSTEP:
                        values(n - 1)
                    ring(n, 2)

            @block.scalar
            def _(a):
                def stage_values(g):
                    if g >= 2:
                        a.wait_ge(s_pv, group_end[g - 2])
                    a.copy(vg[:, g % 2, :, :, 0:DK + 1], v2[:, :, g * GH:(g + 1) * GH, :]).then_inc(s_vg, 1)

                def copy_sums(rho):
                    a.wait_ge(s_pv, LAST_OF[rho] + 1)
                    if rho:
                        a.wait_ge(s_entry, index["out", rho - 1] + 1)
                    a.copy(oT[:], p_acc[:]).then_inc(s_acc, 1)

                a.wait_ge(s_set, 1)
                stage_values(0)
                for n, rho, g, c, j, off in steps:
                    if n >= PRING:
                        a.wait_ge(s_pv, n - PRING + 1)
                    for pair in range(2):
                        a.wait_ge(s_st, 2 * n + pair + 1)
                        a.activation(pw[0:keys[j], n % PRING, 2 * pair:2 * pair + 2, off:CH],
                                     p_st[0:keys[j], pair, :, off:CH], ACT.Exp, scale=1.0 / 4.0).then_inc(s_exp, 1)
                    if n == group_end[g] - 8 and g + 1 < NG:
                        stage_values(g + 1)
                    if n - 1 in LAST_OF:
                        copy_sums(rho - 1)
                copy_sums(NG * NC - 1)

            @block.gpsimd
            def _(g):
                g.memset(vg[:], 0.0).then_inc(s_set, 1)
                for n in diagonal:
                    *_, j, off = steps[n]
                    blk = pw[0:keys[j], n % PRING, :, off:off + P]
                    g.wait_ge(s_exp, 2 * n + 2)
                    g.affine_select(out=blk, in_=blk, compare_op=ALU.is_ge, fill=0.0, base=0,
                                    pattern=[[0, GH], [1, P]], channel_multiplier=-1).then_inc(s_mask, 1)

            @block.vector
            def _(v):
                for e, (kind, *what) in enumerate(entries):
                    bank = p_ring[:, e % RING, :]
                    v.wait_ge(s_entry, e + 1)
                    if kind == "unit":
                        rho, u = what
                        c = CHUNKS[rho][1]
                        i, h, k0, w = UNITS[c][u]
                        if u == 0 and rho:
                            v.wait_ge(s_mx, rho)
                        v.reduce_max(mx_part[:, h * TPC + i % TPC, k0 // CH:k0 // CH + 1], bank[:, 0:w],
                                     AX_X).then_inc(s_taken, 1)
                        if u == len(UNITS[c]) - 1:
                            v.wait_ge(s_taken, e + 1)
                            v.reduce_max(mx[:], mx_part[:, :, 0:c + 1], AX_X).then_inc(s_mx, 1)
                    elif kind == "row":
                        rho = what[0]
                        if rho >= 2:
                            v.wait_ge(s_ns[rho % 2], 16 * (rho // 2))
                        v.tensor_scalar(neg[:, rho % 2, 0, :], bank[0:GH * TPC, 0:P], -1.0, None,
                                        ALU.mult).then_inc(s_nh, 1)
                        v.wait_ge(s_nh, rho + 1)
                        v.scalar_tensor_tensor(out=neg[:, rho % 2, 1, :], in0=bank[0:GH * TPC, 0:P], scalar=-1.0,
                                               in1=neg[:, rho % 2, 0, :], op0=ALU.mult,
                                               op1=ALU.subtract).then_inc(s_taken, 1)
                    else:
                        g, c = CHUNKS[what[0]]
                        po = bank.rearrange("p (a h w) -> p a h w", a=TPC, w=32)
                        par = what[0] % 2
                        v.reciprocal(rden[:, par], po[:, :, :, DK:DK + 1]).then_inc(s_rd, 1)
                        v.wait_ge(s_rd, what[0] + 1)
                        v.tensor_tensor(ctx2[:, c * TPC:(c + 1) * TPC, g * GH * DK:(g + 1) * GH * DK]
                                        .rearrange("p a (h k) -> p a h k", k=DK),
                                        po[:, :, :, 0:DK], rden[:, par].to_broadcast([P, TPC, GH, DK]),
                                        ALU.mult).then_inc(s_taken, 1)

            @block.sync
            def _(sp):
                def rows(rho):
                    g, c = CHUNKS[rho]
                    par = rho % 2
                    sp.wait_ge(s_taken, index["row", rho] + 1)
                    sp.dma_start(m.neg_rows[rho].rearrange("r a q -> a r q"), neg[:, par]).then_inc(s_ns[par], 16)
                    sp.wait_ge(s_ns[par], 16 * (rho // 2 + 1))
                    if rho >= 2:
                        sp.wait_ge(s_rows[par], 16 * (rho // 2))
                    sp.dma_start(qs[STACK:STACK + 2, g % 2, :].rearrange("r (h t) -> r h t", h=GH)
                                 [:, :, c * CH:(c + 1) * CH],
                                 m.neg_rows[rho].rearrange("r (h a) q -> r h (a q)", h=GH)).then_inc(s_rows[par], 16)

                for r in range(2):
                    sp.wait_ge(m.s_parts[r], 16 * NC)
                query_stack(sp, m, 0, T // 2, T, m.s_tail)
                row_at = {x[1]: n for (n, place), (a, b) in ranges.items() for x in entries[a:b] if x[0] == "row"}
                events = [(row_at[rho], "rows", rho) for rho in range(NG * NC)]
                events += [(row_at[1], "stacks", 1)] + [(group_end[g - 2], "stacks", g) for g in range(2, NG)]
                for at, what, n in sorted(events):
                    if what == "rows":
                        rows(n)
                        continue
                    if n >= 2:
                        sp.wait_ge(s_st, 2 * group_end[n - 2])
                    key_stack(sp, m, n)
                    query_stack(sp, m, n, 0, T, m.s_stack[n % 2])


def output_and_router_phase(nc, m, ctx2):
    with ExitStack() as st:
        rT = m.sb("rT5", [P, 2, KC, CH], F32, st)
        rows = m.sb("rows5", [P, NC, TPC * D], F32, st)
        p_t = m.pb("p_t5", [P, 2, KC, CH], F32, st)
        p_y = m.pb("p_y5", [P, TPC, D], F32, st)
        s_tr, s_rT, s_add = m.sem("transposed5", st), m.sem("rT5_ready", st), m.sem("added5", st)
        s_y, s_lg = m.sem("y5_ready", st), m.sem("logits", st)
        s_ln, s_pow, s_xn = m.sem("ln3_stats", st), m.sem("ln3_pow", st), m.sem("xn3_ready", st)
        s_xh, s_xl, s_res = m.sem("x_high", st), m.sem("x_low", st), m.sem("residual_added", st)
        xhl, p_lg = m.xhl, m.p_lg
        with nc.Block() as block:
            @block.sync
            def _(sp):
                sp.dma_start(m.w_shared[:], m.w_img[E]).then_inc(m.s_ws, 16)

            @block.tensor
            def _(pe):
                def transposes(n):
                    c = n % NC
                    if n >= NC:
                        pe.wait_ge(s_xn, (c + 1) * TPC)
                    if n >= 2:
                        pe.wait_ge(s_rT, n - 1)
                    for k in range(KC):
                        for j in range(TPC):
                            src = (ctx2[:, c * TPC + j, k * P:(k + 1) * P] if n < NC
                                   else rows[:, c, j * D + k * P:j * D + (k + 1) * P])
                            last = pe.transpose(p_t[:, n % 2, k, j * P:(j + 1) * P], src, m.ident[:])
                    last.then_inc(s_tr, 1)

                def project(n):
                    if n:
                        pe.wait_ge(s_add, n)
                    for j in range(TPC):
                        for k in range(KC):
                            last = pe.matmul(p_y[:, j, :], rT[:, n % 2, k, j * P:(j + 1) * P], m.w_x[:, 3, k, :],
                                             start=(k == 0), stop=(k == KC - 1))
                    last.then_inc(s_y, 1)

                def logits(n):
                    for j in range(TPC):
                        for k in range(KC):
                            last = pe.matmul(p_lg[:, (n - NC) * TPC + j, :], rT[:, n % 2, k, j * P:(j + 1) * P],
                                             m.w_rt[:, k, :], start=(k == 0), stop=(k == KC - 1))
                    last.then_inc(s_lg, 1)

                transposes(0)
                for n in range(2 * NC):
                    if n + 1 < 2 * NC:
                        transposes(n + 1)
                    pe.wait_ge(s_rT, n + 1)
                    if n < NC:
                        project(n)
                    else:
                        logits(n)

            @block.scalar
            def _(a):
                def high(c):
                    a.wait_ge(s_xn, (c + 1) * TPC)
                    a.copy(xhl[:, c * TPC:(c + 1) * TPC, 0, :],
                           rows[:, c].rearrange("p (t d) -> p t d", d=D)).then_inc(s_xh, 1)

                for n in range(2 * NC):
                    a.wait_ge(s_tr, n + 1)
                    if n >= 2:
                        a.wait_ge(s_y, min(n - 1, NC))
                        if n - 2 >= NC:
                            a.wait_ge(s_lg, n - 1 - NC)
                    a.copy(rT[:, n % 2], p_t[:, n % 2]).then_inc(s_rT, 1)
                    if n >= NC:
                        high(n - NC)

            @block.gpsimd
            def _(g):
                def add_rows(c):
                    xs = m.x_res[:, c * TPC * D:(c + 1) * TPC * D]
                    g.wait_ge(s_xn, (c + 1) * TPC)
                    g.tensor_tensor(xs, xs, rows[:, c], ALU.add).then_inc(s_res, 1)

                for c in range(NC):
                    layernorm_power(g, m, s_ln, s_pow, c)
                    if c:
                        add_rows(c - 1)
                add_rows(NC - 1)

            @block.vector
            def _(v):
                def low(c):
                    v.wait_ge(s_xh, c + 1)
                    v.tensor_tensor(xhl[:, c * TPC:(c + 1) * TPC, 1, :], rows[:, c].rearrange("p (t d) -> p t d", d=D),
                                    xhl[:, c * TPC:(c + 1) * TPC, 0, :], ALU.subtract).then_inc(s_xl, 1)

                def normalise(c):
                    v.wait_ge(s_pow, c + 1)
                    layernorm_rows(v, m, s_xn, rows[:, c], c)

                for c in range(NC):
                    xs = m.x_res[:, c * TPC * D:(c + 1) * TPC * D]
                    v.wait_ge(s_y, c + 1)
                    v.tensor_tensor(xs, p_y[:].rearrange("p a d -> p (a d)"), xs, ALU.add).then_inc(s_add, 1)
                    v.wait_ge(s_add, c + 1)
                    layernorm_stats(v, m, s_ln, c)
                    if c:
                        normalise(c - 1)
                normalise(NC - 1)
                for c in range(NC):
                    low(c)
def up_products(pe, p_h, w, w0, xT, half):
    rows = xT.shape[-1] // (2 * KC)
    for f in range(half * NF // 2, (half + 1) * NF // 2):
        n = 0
        for wp, xp in PASSES:
            for k in range(KC):
                last = pe.matmul(p_h[:, f * rows:(f + 1) * rows], w[:, ds(w0 + UP + (wp * KC + k) * F + f * P, P)],
                                 xT[:, (xp * KC + k) * rows:(xp * KC + k + 1) * rows],
                                 start=(n == 0), stop=(n == 3 * KC - 1))
                n += 1
    return last


def down_products(pe, p_y, w, w0, hT, half):
    rows = hT.shape[-1] // NF
    for f in range(half * NF // 2, (half + 1) * NF // 2):
        for n, (wp, hp) in enumerate(PASSES):
            for a in range(rows // P):
                last = pe.matmul(p_y[:, a, 0:D], hT[:, hp, f * rows + a * P:f * rows + (a + 1) * P],
                                 w[:, ds(w0 + DOWN + (wp * NF + f) * D, D)],
                                 start=(f == 0 and n == 0), stop=(f == NF - 1 and n == 2))
    return last


def shared_expert_phase(nc, m, w_sb, s_w, slot_idx, gates, block_expert):
    with ExitStack() as st:
        logit = m.sb("logit", [P, NT, E], F32, st)
        prob = m.sb("prob", [P, NT, E], F32, st)
        top1 = m.sb("top1", [P, NT, 1], F32, st)
        psum_ = m.sb("prob_sum", [P, NT, 1], F32, st)
        best_i = m.sb("best_i", [P, NT, E], U32, st)
        idx_f = m.sb("idx_f", [P, NT, TOPK], F32, st)
        pick = m.sb("pick", [P, TOPK, NT, E], F32, st)
        picked = m.sb("picked", [P, NT + 1, E], BF16, st)
        before = m.sb("before", [P, P], BF16, st)
        onesb = m.sb("onesb", [P, P], BF16, st)
        iota_i = m.sb("iota_i", [P, ROUTED], mybir.dt.int32, st)
        iota = m.sb("iota", [P, ROUTED], F32, st)
        ones8 = m.sb("ones8", [P, E], F32, st)
        cnt = m.sb("cnt", [P, E, 1], F32, st)
        over = m.sb("over", [P, E, T // RB], F32, st)
        nblk = m.sb("nblk", [P, E], F32, st)
        end = m.sb("end", [P, E], F32, st)
        base = m.sb("base", [P, 1, E], F32, st)
        pos = m.sb("pos", [P, NT, E], F32, st)
        posk = m.sb("posk", [P, NT, E], F32, st)
        slot_f = m.sb("slot_f", [P, TOPK, NT], F32, st)
        past = m.sb("past", [P, ROUTED, E], F32, st)
        blk_f = m.sb("blk_f", [P, ROUTED], F32, st)
        xT = m.sb("xT6", [P, 2, 2 * KC * P], BF16, st)
        h32 = m.sb("h32_6", [P, 2, NF * P], F32, st)
        hT = m.sb("hT6", [P, 2, 2, NF * P], BF16, st)
        p_x = m.pb("p_x6", [P, 2 * KC * P], BF16, st)
        p_h = m.pb("p_h6", [P, 2, NF * P], F32, st)
        p_y = m.pb("p_y6", [P, 2, CH], F32, st)
        xhl, p_lg = m.xhl, m.p_lg
        p_rank = p_lg[:, NT:]
        s_c, s_v, s_sub, s_ex = m.sem("constants", st), m.sem("routing_chain", st), m.sem("logits_shifted", st), m.sem("prob_exp", st)
        s_pick, s_rank, s_slot = m.sem("picked_ready", st), m.sem("ranked", st), m.sem("slots_ready", st)
        s_xs, s_sc = m.sem("shared_rows_out", st), m.sem("rows_scattered", st)
        s_xt, s_xT, s_up = m.sem("x6_transposed", st), m.sem("xT6_ready", st), m.sem("up6_done", st)
        s_ge, s_hh, s_hl = m.sem("gelu6_done", st), m.sem("h6_high", st), m.sem("h6_low", st)
        s_dn, s_add = m.sem("down6_done", st), m.sem("shared_added", st)
        w, w0 = m.w_shared, 0
        with nc.Block() as block:
            @block.sync
            def _(sp):
                for e in range(E):
                    sp.dma_start(w_sb[:, e, :], m.w_img[e]).then_inc(s_w[e], 16)
                sp.dma_start(m.x_slots[ROUTED * RB:SLOTS, :].rearrange("(t p) n -> p t n", p=P),
                             xhl[:, SHARED:].rearrange("p t r d -> p t (r d)")).then_inc(s_xs, 16)
                sp.wait_ge(s_xs, 16)
                sp.wait_ge(s_sc, 16 * NT * TOPK)
                for b in range(2):
                    sp.dma_start(m.xb[:, b], m.x_slots[b * RB:(b + 1) * RB, :].rearrange("(a p) n -> p a n", p=P)
                                 ).then_inc(m.s_xb[b], 16)

            @block.gpsimd
            def _(g):
                g.memset(onesb[:], 1.0).then_inc(s_c, 1)
                g.memset(before[:], 1.0).then_inc(s_c, 1)
                g.memset(ones8[:], 1.0).then_inc(s_c, 1)
                g.iota(iota_i[:], pattern=[[1, ROUTED]], base=0, channel_multiplier=0).then_inc(s_c, 1)
                g.wait_ge(s_c, 2)
                g.affine_select(out=before[:], in_=before[:], compare_op=ALU.is_gt, fill=0.0, base=0,
                                pattern=[[1, P]], channel_multiplier=-1).then_inc(s_c, 1)
                g.wait_ge(s_slot, 1)
                for t in range(NT):
                    for k in range(TOPK):
                        g.indirect_dma_start(m.x_slots,
                                             bass.IndirectOffsetOnAxis(ap=slot_idx[:, k * NT + t:k * NT + t + 1], axis=0),
                                             xhl[:, t].rearrange("p r d -> p (r d)"), None).then_inc(s_sc, 16)
                g.wait_ge(s_sc, 16 * NT * TOPK)

            @block.tensor
            def _(pe):
                def transposes(b):
                    if b >= 1:
                        pe.wait_ge(s_xT, b)
                    for n in range(2 * KC):
                        last = pe.transpose(p_x[:, n * P:(n + 1) * P],
                                            xhl[:, b, n // KC, n % KC * P:(n % KC + 1) * P], m.identb[:])
                    last.then_inc(s_xt, 1)

                def ranks():
                    pe.wait_ge(s_c, 5)
                    pe.wait_ge(s_pick, 1)
                    pe.matmul(p_rank, before[:], picked[:], start=True, stop=False)
                    for t in range(NT):
                        last = pe.matmul(p_rank[:, t + 1:, :], onesb[:],
                                         picked[:, t:t + 1, :].to_broadcast([P, NT - t, E]),
                                         start=False, stop=(t == NT - 1))
                    last.then_inc(s_rank, 1)

                pe.wait_ge(m.s_ws, 16)
                transposes(0)
                transposes(1)
                for b in range(SHARED + 1):
                    if b < SHARED:
                        pe.wait_ge(s_xT, b + 1)
                        if b >= 2:
                            pe.wait_ge(s_ge, 2 * b - 2)
                        for half in range(2):
                            up_products(pe, p_h[:, b % 2], w, w0, xT[:, b % 2], half).then_inc(s_up, 1)
                    if b + 2 < SHARED:
                        transposes(b + 2)
                    if b == 1:
                        ranks()
                    if b >= 1:
                        if b >= 3:
                            pe.wait_ge(s_add, b - 2)
                        for half in range(2):
                            pe.wait_ge(s_hl, 2 * (b - 1) + half + 1)
                            last = down_products(pe, p_y[:, (b - 1) % 2:(b - 1) % 2 + 1], w, w0, hT[:, (b - 1) % 2], half)
                        last.then_inc(s_dn, 1)

            @block.scalar
            def _(a):
                a.wait_ge(s_sub, 1)
                a.activation(prob[:], logit[:], ACT.Exp).then_inc(s_ex, 1)
                for b in range(SHARED):
                    for z in range(2):
                        half = slice(z * NF * P // 2, (z + 1) * NF * P // 2)
                        a.wait_ge(s_up, 2 * b + z + 1)
                        if b >= 2:
                            a.wait_ge(s_hl, 2 * b + z - 3)
                        a.activation(h32[:, b % 2, half], p_h[:, b % 2, half], ACT.Gelu).then_inc(s_ge, 1)

            @block.vector
            def _(v):
                n = [0]

                def link(ins):
                    n[0] += 1
                    ins.then_inc(s_v, 1)
                    v.wait_ge(s_v, n[0])

                def choose_experts():
                    v.wait_ge(s_c, 5)
                    link(v.tensor_copy(iota[:], iota_i[:]))
                    link(v.memset(picked[:, NT, :], 0.0))
                    link(v.reduce_max(top1[:], p_lg[:, 0:NT], AX_X))
                    v.tensor_tensor(logit[:], p_lg[:, 0:NT], top1[:].to_broadcast([P, NT, E]), ALU.subtract).then_inc(s_sub, 1)
                    v.wait_ge(s_ex, 1)
                    link(v.reduce_sum(psum_[:], prob[:], AX_X))
                    link(v.reciprocal(top1[:], psum_[:]))
                    link(v.tensor_tensor(prob[:], prob[:], top1[:].to_broadcast([P, NT, E]), ALU.mult))
                    for t in range(NT):
                        v.max(gates[:, t, :], prob[:, t, :]).then_inc(s_v, 1)
                    n[0] += NT
                    for t in range(NT):
                        v.wait_ge(s_v, n[0] - NT + t + 1)
                        v.max_index(best_i[:, t, :], gates[:, t, :], prob[:, t, :]).then_inc(s_v, 1)
                    n[0] += NT
                    v.wait_ge(s_v, n[0])
                    link(v.tensor_copy(idx_f[:], best_i[:, :, 0:TOPK]))
                    for k in range(TOPK):
                        link(v.tensor_tensor(pick[:, k], iota[:, None, 0:E].to_broadcast([P, NT, E]),
                                             idx_f[:, :, k:k + 1].to_broadcast([P, NT, E]), ALU.is_equal))
                    v.tensor_tensor(picked[:, 0:NT, :], pick[:, 0], pick[:, 1], ALU.add).then_inc(s_pick, 1)

                def assign_slots():
                    v.wait_ge(s_rank, 1)
                    link(v.tensor_copy(cnt[:, :, 0], p_rank[:, NT, :]))
                    link(v.tensor_scalar(blk_f[:, 0:T // RB], iota[:, 0:T // RB], float(RB), None, ALU.mult))
                    link(v.tensor_tensor(over[:], cnt[:].to_broadcast([P, E, T // RB]),
                                         blk_f[:, None, 0:T // RB].to_broadcast([P, E, T // RB]), ALU.is_gt))
                    link(v.reduce_sum(nblk[:], over[:], AX_X))
                    link(v.tensor_tensor_scan(end[:], ones8[:], nblk[:], 0.0, ALU.mult, ALU.add))
                    link(v.tensor_tensor(base[:, 0, :], end[:], nblk[:], ALU.subtract))
                    link(v.tensor_scalar(base[:], base[:], float(RB), None, ALU.mult))
                    link(v.tensor_tensor(pos[:], p_rank[:, 0:NT, :], base[:].to_broadcast([P, NT, E]), ALU.add))
                    for k in range(TOPK):
                        link(v.tensor_tensor(posk[:], pos[:], pick[:, k], ALU.mult))
                        link(v.reduce_sum(slot_f[:, k, :], posk[:], AX_X))
                    v.tensor_copy(slot_idx[:], slot_f[:].rearrange("p k t -> p (k t)")).then_inc(s_slot, 1)

                def list_blocks():
                    link(v.tensor_tensor(past[:], iota[:, :, None].to_broadcast([P, ROUTED, E]),
                                         end[:, None, :].to_broadcast([P, ROUTED, E]), ALU.is_ge))
                    link(v.reduce_sum(blk_f[:], past[:], AX_X))
                    link(v.tensor_scalar(blk_f[:], blk_f[:], float(E - 1), None, ALU.min))
                    link(v.tensor_copy(block_expert[:], blk_f[:]))

                def copy_xT(b):
                    v.wait_ge(s_xt, b + 1)
                    if b >= 2:
                        v.wait_ge(s_up, 2 * b - 2)
                    v.tensor_copy(xT[:, b % 2, :], p_x[:]).then_inc(s_xT, 1)

                copy_xT(0)
                copy_xT(1)
                choose_experts()
                for b in range(SHARED + 1):
                    if b < SHARED:
                        for z in range(2):
                            half = slice(z * NF * P // 2, (z + 1) * NF * P // 2)
                            v.wait_ge(s_ge, 2 * b + z + 1)
                            if b >= 2:
                                v.wait_ge(s_dn, b - 1)
                            v.tensor_copy(hT[:, b % 2, 0, half], h32[:, b % 2, half]).then_inc(s_hh, 1)
                            v.wait_ge(s_hh, 2 * b + z + 1)
                            v.tensor_tensor(hT[:, b % 2, 1, half], h32[:, b % 2, half], hT[:, b % 2, 0, half],
                                            ALU.subtract).then_inc(s_hl, 1)
                    if b + 2 < SHARED:
                        copy_xT(b + 2)
                    if b == 1:
                        assign_slots()
                    if b == 3:
                        list_blocks()
                    if b >= 1:
                        v.wait_ge(s_dn, b)
                        xs = m.x_res[:, (b - 1) * D:b * D]
                        v.tensor_tensor(xs, p_y[:, (b - 1) % 2, 0:D], xs, ALU.add).then_inc(s_add, 1)


def routed_experts_phase(nc, m, w_sb, s_w, slot_idx, gates, block_expert):
    A = RB // P
    HALF = NF * RB // 2
    NB = ROUTED + TAIL
    PAIRS = (ROUTED - 3) // 2
    REST = 2 + 2 * PAIRS
    BESIDE = 4
    assert ROUTED % 2 == 1 and TAIL >= 2
    with ExitStack() as st:
        xb, s_xb = m.xb, m.s_xb
        xT = m.sb("xT", [P, 2, 2 * KC * RB], BF16, st)
        h32 = m.sb("h32", [P, NF * RB], F32, st)
        assert NT * 2 * D == 2 * 2 * NF * RB
        hT = m.xhl[:].rearrange("p t r d -> p (t r d)").rearrange("p (b r n) -> p b r n", b=2, r=2)
        ysb = m.sb("ysb", [P, 2, A, D], F32, st)
        ya = (w_sb[:].rearrange("p e n -> p (e n)")[:, 0:2 * NT * TOPK * D].bitcast(F32)
              .rearrange("p (t k d) -> p t k d", k=TOPK, d=D))
        p_x = m.pb("p_x", [P, 2, 2 * KC * RB], BF16, st)
        p_h = m.pb("p_h", [P, NF * RB], F32, st)
        p_y = m.pb("p_y7", [P, A, CH], F32, st)
        s_xt, s_xT, s_up = m.sem("x_transposed", st), m.sem("xT_ready", st), m.sem("up_done", st)
        s_ge, s_hh, s_hl = m.sem("gelu_done", st), m.sem("h_high", st), m.sem("h_low", st)
        s_dn, s_ys = m.sem("down_done", st), m.sem("y_copied", st)
        s_yo = [m.sem(f"y_out{r}", st) for r in range(2)]
        s_g = [m.sem(f"gathered{t}", st) for t in range(NT)]
        s_v, s_t, s_out = m.sem("combine_chain", st), m.sem("tile_done", st), m.sem("out_stored", st)
        w = w_sb[:].rearrange("p e n -> p (e n)")
        with nc.Block() as block:
            @block.sync
            def _(sp):
                def load(b, r):
                    sp.dma_start(xb[:, r], m.x_slots[ds(b * RB, RB), :].rearrange("(a p) n -> p a n", p=P)
                                 ).then_inc(s_xb[r], 16)

                def store(b, r):
                    sp.wait_ge(s_ys, b + 1)
                    sp.dma_start(m.y_slots[ds(b * RB, RB), :].rearrange("(a p) n -> p a n", p=P), ysb[:, r]
                                 ).then_inc(s_yo[r], 16)

                for b in range(3):
                    sp.wait_ge(s_xt, b + 1)
                    load(b + 2, b % 2)
                with sp.Fori(0, (ROUTED - 3) // 2) as q:
                    for r in range(2):
                        b = 2 * q + 1 + r
                        sp.wait_ge(s_xt, b + 3)
                        load(b + 4, 1 - r)
                        store(b - 1, r)
                for b in range(ROUTED - 2, ROUTED + 1):
                    if b + 4 < NB:
                        sp.wait_ge(s_xt, b + 3)
                        load(b + 4, b % 2)
                    store(b - 1, (b - 1) % 2)
                for t in range(NT):
                    sp.wait_ge(s_t, t + 1)
                    sp.dma_start(m.out[0, t * P:(t + 1) * P, :], m.x_res[:, t * D:(t + 1) * D]).then_inc(s_out, 16)
                sp.wait_ge(s_out, 16 * NT)

            @block.gpsimd
            def _(g):
                for r in range(2):
                    g.wait_ge(s_yo[r], 16 * ((ROUTED + 1 - r) // 2))
                for t in range(NT):
                    for k in range(TOPK):
                        g.indirect_dma_start(ya[:, t, k, :], None, m.y_slots,
                                             bass.IndirectOffsetOnAxis(ap=slot_idx[:, k * NT + t:k * NT + t + 1], axis=0)
                                             ).then_inc(s_g[t], 16)

            @block.tensor
            def _(pe):
                def transposes(b, r, nth, first=False):
                    pe.wait_ge(s_xb[r], 16 * (nth + 1))
                    if not first:
                        pe.wait_ge(s_xT, b - 1)
                    for n in range(2 * KC):
                        for a in range(A):
                            last = pe.transpose(p_x[:, r, n * RB + a * P:n * RB + (a + 1) * P],
                                                xb[:, r, a, n * P:(n + 1) * P], m.identb[:])
                    last.then_inc(s_xt, 1)

                def weights_of(b):
                    return pe.snap(pe.value_load(block_expert[0:1, ds(b, 1)], min_val=0, max_val=E - 1) * WCOLS)

                def source(w0):
                    return (m.w_shared, 0) if w0 is shared else (w, w0)

                def up(b, r, w0, first=False):
                    pe.wait_ge(s_xT, b + 1)
                    for half in range(2):
                        if not first:
                            pe.wait_ge(s_ge, 2 * b + half - 1)
                        up_products(pe, p_h, *source(w0), xT[:, r], half).then_inc(s_up, 1)

                def down(b, r, w0, first=False):
                    if not first:
                        pe.wait_ge(s_ys, b)
                    for half in range(2):
                        pe.wait_ge(s_hl, 2 * b + half + 1)
                        last = down_products(pe, p_y, *source(w0), hT[:, r], half)
                    last.then_inc(s_dn, 1)

                shared = None
                for e in range(E):
                    pe.wait_ge(s_w[e], 16)
                transposes(0, 0, 0, first=True)
                transposes(1, 1, 0, first=True)
                up(0, 0, weights_of(0), first=True)
                transposes(2, 0, 1)
                up(1, 1, weights_of(1))
                transposes(3, 1, 1)
                down(0, 0, weights_of(0), first=True)
                with pe.Fori(0, PAIRS) as q:
                    before = weights_of(2 * q + 1)
                    for r in range(2):
                        b = 2 * q + 2 + r
                        w0 = weights_of(b)
                        up(b, r, w0)
                        transposes(b + 2, r, q + 2)
                        down(b - 1, 1 - r, before)
                        before = w0
                before = weights_of(REST - 1)
                for b in range(REST, NB):
                    w0 = weights_of(b) if b < ROUTED else shared
                    up(b, b % 2, w0)
                    if b + 2 < NB:
                        transposes(b + 2, b % 2, (b + 2) // 2)
                    down(b - 1, 1 - b % 2, before)
                    before = w0
                down(NB - 1, (NB - 1) % 2, before)

            @block.scalar
            def _(a):
                def gelus(b, first=False):
                    for z in range(2):
                        half = slice(z * HALF, (z + 1) * HALF)
                        a.wait_ge(s_up, 2 * b + z + 1)
                        if not first:
                            a.wait_ge(s_hl, 2 * b + z - 1)
                        a.activation(h32[:, half], p_h[:, half], ACT.Gelu).then_inc(s_ge, 1)

                gelus(0, first=True)
                with a.Fori(0, NB - 1) as q:
                    gelus(q + 1)

            @block.vector
            def _(v):
                def copy_xT(b, r, first=False):
                    v.wait_ge(s_xt, b + 1)
                    if not first:
                        v.wait_ge(s_up, 2 * b - 2)
                    v.tensor_copy(xT[:, r, :], p_x[:, r, :]).then_inc(s_xT, 1)

                def split(b, r, first=False):
                    for z in range(2):
                        half = slice(z * HALF, (z + 1) * HALF)
                        v.wait_ge(s_ge, 2 * b + z + 1)
                        if not first:
                            v.wait_ge(s_dn, b - 1)
                        v.tensor_copy(hT[:, r, 0, half], h32[:, half]).then_inc(s_hh, 1)
                        v.wait_ge(s_hh, 2 * b + z + 1)
                        v.tensor_tensor(hT[:, r, 1, half], h32[:, half], hT[:, r, 0, half],
                                        ALU.subtract).then_inc(s_hl, 1)

                def copy_y(b, r, nth, first=False):
                    v.wait_ge(s_dn, b + 1)
                    if not first:
                        v.wait_ge(s_yo[r], 16 * nth)
                    v.tensor_copy(ysb[:, r], p_y[:, :, 0:D]).then_inc(s_ys, 1)

                def add_y(b):
                    first = SHARED + (b - ROUTED) * A
                    xs = m.x_res[:, first * D:(first + A) * D].rearrange("p (a d) -> p a d", d=D)
                    v.wait_ge(s_dn, b + 1)
                    v.tensor_tensor(xs, p_y[:, :, 0:D], xs, ALU.add).then_inc(s_ys, 1)

                def combine(t):
                    xs = m.x_res[:, t * D:(t + 1) * D]
                    v.wait_ge(s_g[t], 16 * TOPK)
                    v.scalar_tensor_tensor(out=xs, in0=ya[:, t, 0, :], scalar=gates[:, t, 0:1], in1=xs,
                                           op0=ALU.mult, op1=ALU.add).then_inc(s_v, 1)
                    v.wait_ge(s_v, t + 1)
                    v.scalar_tensor_tensor(out=xs, in0=ya[:, t, 1, :], scalar=gates[:, t, 1:2], in1=xs,
                                           op0=ALU.mult, op1=ALU.add).then_inc(s_t, 1)

                copy_xT(0, 0, first=True)
                copy_xT(1, 1, first=True)
                split(0, 0, first=True)
                copy_xT(2, 0)
                split(1, 1, first=True)
                copy_xT(3, 1)
                copy_y(0, 0, 0, first=True)
                split(2, 0)
                copy_xT(4, 0)
                copy_y(1, 1, 0, first=True)
                with v.Fori(0, (ROUTED - 5) // 2) as q:
                    for r in range(2):
                        b = 2 * q + 3 + r
                        split(b, 1 - r)
                        copy_xT(b + 2, 1 - r)
                        copy_y(b - 1, r, q + 1)
                tiles = 0
                for b in range(ROUTED - 2, NB):
                    split(b, b % 2)
                    if b + 2 < NB:
                        copy_xT(b + 2, b % 2)
                    if b <= ROUTED:
                        copy_y(b - 1, 1 - b % 2, (b - 1) // 2)
                    else:
                        add_y(b - 1)
                        for tiles in range(tiles, tiles + BESIDE):
                            combine(tiles)
                        tiles += 1
                add_y(NB - 1)
                v.wait_ge(s_ys, NB)
                for t in range(tiles, NT):
                    combine(t)


def experts_phase(nc, m):
    with ExitStack() as st:
        w_sb = m.sb("w_sb", [P, E, WCOLS], BF16, st)
        slot_idx = m.sb("slot_idx", [P, TOPK * NT], U32, st)
        gates = m.sb("gates", [P, NT, E], F32, st)
        block_expert = m.sb("block_expert", [P, ROUTED], U32, st)
        s_w = [m.sem(f"weights{e}", st) for e in range(E)]
        m.xb = m.sb("xb", [P, 2, RB // P, 2 * D], BF16, st)
        m.s_xb = [m.sem(f"xb_in{r}", st) for r in range(2)]
        shared_expert_phase(nc, m, w_sb, s_w, slot_idx, gates, block_expert)
        m.logits_bank.close()
        routed_experts_phase(nc, m, w_sb, s_w, slot_idx, gates, block_expert)
def build(nc, x, ctx_in, W_qkv, b_qkv, W_out, b_out, WqT, WkT, WvT, WoT,
          shared_up, shared_down, routed_up, routed_down, router_w, out):
    with ExitStack() as top:
        def sb(name, shape, dt=F32, st=top):
            return st.enter_context(nc.sbuf_tensor(name, shape, dt))

        def pb(name, shape, dt=F32, st=top):
            return st.enter_context(nc.psum_tensor(name, shape, dt))

        def sem(name, st=top):
            return st.enter_context(nc.semaphore(name))

        def dram(name, shape, dt):
            return nc.dram_tensor(name, shape, dt, kind="Internal").ap()

        w_img = dram("w_img", [E + 1, P, WCOLS], BF16)
        q2_parts = dram("q2_parts", [3, HEADS, DK, T], BF16)
        k2_parts = dram("k2_parts", [3, HEADS, DK, T], BF16)
        neg_rows = dram("neg_rows", [NG * NC, 2, GH * TPC, P], BF16)
        x_slots = dram("x_slots", [SLOTS, 2 * D], BF16)
        y_slots = dram("y_slots", [ROUTED * RB, D], F32)

        x_res = sb("x_res", [P, NT * D])
        ident = sb("ident", [P, P])
        identb = sb("identb", [P, P], BF16)
        w_rt = sb("w_rt", [P, KC, E])
        stats = sb("stats", [P, NT, 6])
        mv = sb("mv", [P, NT, 2])
        var_eps = sb("var_eps", [P, NT])
        neg_half = sb("neg_half", [P, NT])
        rstd = sb("rstd", [P, NT])

        xhl = sb("xhl", [P, NT, 2, D], BF16)
        w_shared = sb("w_shared", [P, WCOLS], BF16)
        s_ws = sem("shared_weights_in")
        ctx_sb = xhl[:].rearrange("p t r d -> p (t r d)").bitcast(F32).rearrange("p (c n) -> p c n", c=NC)
        s_cx = [sem(f"ctx_in{c}") for c in range(NC)]
        logits_bank = top.enter_context(ExitStack())

        att = top.enter_context(ExitStack())
        w_x = sb("w_x", [P, 4, KC, D], F32, att)

        sa = top.enter_context(ExitStack())
        w_qkv = sb("w_qkv", [P, KC, 3 * D], F32, sa)
        w_out = sb("w_out", [P, KC, D], F32, sa)
        b_rows = sb("b_rows", [P, 2 * D], F32, sa)
        b_qk = sb("b_qk", [P, 2 * KC], F32, sa)

        m = Shared()
        m.sb, m.pb, m.sem, m.x_res, m.ident = sb, pb, sem, x_res, ident
        m.identb, m.b_rows, m.b_qk, m.w_qkv = identb, b_rows, b_qk, w_qkv
        m.w_out, m.w_x, m.w_rt, m.stats, m.mv = w_out, w_x, w_rt, stats, mv
        m.var_eps, m.neg_half, m.rstd, m.w_img, m.q2_parts = var_eps, neg_half, rstd, w_img, q2_parts
        m.k2_parts, m.neg_rows, m.x_slots, m.y_slots, m.ctx_in = k2_parts, neg_rows, x_slots, y_slots, ctx_in
        m.ctx_sb, m.s_cx = ctx_sb, s_cx
        m.xhl, m.w_shared, m.s_ws, m.logits_bank = xhl, w_shared, s_ws, logits_bank
        m.shared_up, m.shared_down, m.routed_up, m.routed_down, m.out = shared_up, shared_down, routed_up, routed_down, out

        m.s_x = [sem(f"x_in{c}") for c in range(NC)]
        m.s_w, m.s_later = sem("qkv_weights_in"), sem("later_inputs_in")
        m.EARLY, m.LATER = 4, 6
        with ExitStack() as st:
            s_fill = sem("filled", st)
            s_sel = sem("selected", st)
            with nc.Block() as block:
                @block.sync
                def _(sp):
                    xv = x.rearrange("a (t p) d -> p (a t) d", p=P)
                    xr = x_res[:].rearrange("p (t d) -> p t d", d=D)
                    for c in range(NC):
                        sp.dma_start(xr[:, TPC * c:TPC * (c + 1), :], xv[:, TPC * c:TPC * (c + 1), :]).then_inc(m.s_x[c], 16)
                    sp.dma_start(w_qkv[:], W_qkv.rearrange("(k p) n -> p k n", p=P)).then_inc(m.s_w, 16)
                    sp.dma_start(b_qk[:], b_qkv[0:2 * D].rearrange("(m p) -> p m", p=P),
                                 allow_slow_non_contiguous=True).then_inc(m.s_w, 16)
                    sp.dma_start(b_rows[:, 0:D], b_qkv[2 * D:3 * D].rearrange("(a n) -> a n", a=1).to_broadcast([P, D])
                                 ).then_inc(m.s_w, 16)
                    sp.dma_start(b_rows[:, D:2 * D], b_out.rearrange("(a n) -> a n", a=1).to_broadcast([P, D])
                                 ).then_inc(m.s_w, 16)
                    sp.dma_start(w_out[:], W_out.rearrange("(k p) n -> p k n", p=P)).then_inc(m.s_later, 16)
                    for n, w in enumerate((WqT, WkT, WvT, WoT)):
                        sp.dma_start(w_x[:, n], w.rearrange("(k p) n -> p k n", p=P)).then_inc(m.s_later, 16)
                    sp.dma_start(w_rt[:], router_w.rearrange("(k p) n -> p k n", p=P)).then_inc(m.s_later, 16)

                @block.gpsimd
                def _(g):
                    g.memset(ident[:], 0.0).then_inc(s_fill, 1)
                    g.memset(identb[:], 0.0).then_inc(s_fill, 1)
                    g.memset(neg_half[:], -0.5)
                    g.memset(ctx_sb[:, NC - 1], 0.0)
                    g.wait_ge(s_fill, 2)
                    for eye in (ident, identb):
                        g.affine_select(out=eye[:], in_=eye[:], compare_op=ALU.not_equal, fill=1.0, base=0,
                                        pattern=[[-1, P]], channel_multiplier=1).then_inc(s_sel, 1)

        qk = [sb(f"qk{r}", [P, 2 * KC, T], BF16, sa) for r in range(2)]
        vv = [sb(f"vv{r}", [P, NT * D], BF16, sa) for r in range(2)]
        qkv_phase(nc, m, qk, vv)
        self_attention_phase(nc, m, qk, vv)
        sa.close()
        with ExitStack() as xa:
            ctx2 = sb("ctx2", [P, NT, HEADS * DK], F32, xa)
            v2 = sb("v2", [P, NTC, HEADS, DK + 1], F32, xa)
            m.qs = sb("qs", [STACK + 2, 2, GH * T], BF16, xa)
            m.ks = sb("ks", [STACK + 2, 2, GH * KT], BF16, xa)
            m.mask = sb("mask", [P, P], BF16, xa)
            m.parts = sb("parts", [P, 2, 3, KC, CH], BF16, xa)
            m.s_parts = [sem(f"parts_stored{r}", xa) for r in range(2)]
            m.s_stack = [sem(f"stacks_in{r}", xa) for r in range(2)]
            m.s_tail = sem("first_group_tail_in", xa)
            cross_projection_phase(nc, m, v2)
            cross_attention_phase(nc, m, v2, ctx2)
            m.p_lg = pb("p_lg", [P, 2 * NT + 1, E], F32, logits_bank)
            output_and_router_phase(nc, m, ctx2)
        att.close()
        experts_phase(nc, m)


_INS = ['x', 'ctx_1024', 'L0_attn_W_qkv', 'L0_attn_b_qkv', 'L0_attn_W_out', 'L0_attn_b_out', 'L0_xattn_Wq',
        'L0_xattn_Wk', 'L0_xattn_Wv', 'L0_xattn_Wo', 'L0_ffn_shared_up', 'L0_ffn_shared_down',
        'L0_ffn_routed_up', 'L0_ffn_routed_down', 'L0_ffn_router_w']
_TRANSPOSED = ['L0_xattn_Wq', 'L0_xattn_Wk', 'L0_xattn_Wv', 'L0_xattn_Wo']


def kernel(**inputs):
    import concourse.bacc as bacc
    from concourse.bass_utils import run_bass_kernel_spmd

    nc = bacc.Bacc("TRN2", target_bir_lowering=False, num_devices=1)
    arrays, args = {}, []
    for name in _INS:
        a = np.asarray(inputs[name])
        a = np.ascontiguousarray(a.T if name in _TRANSPOSED else a)
        arrays[f"in_{name}"] = a
        args.append(nc.dram_tensor(f"in_{name}", a.shape, mybir.dt.from_np(a.dtype), kind="ExternalInput").ap())
    args.append(nc.dram_tensor("out_x", (1, T, D), F32, kind="ExternalOutput").ap())
    build(nc, *args)
    result = run_bass_kernel_spmd(nc, [arrays], core_ids=[0])
    return result.results[0]["out_x"]
```
